# Optimizing a Trainium2 kernel written in Bass

```python
import numpy as np
import jax
import jax.numpy as jnp

def _softmax(x, axis=-1):
    return jax.nn.softmax(x, axis=axis)

def _gelu(x):
    return jax.nn.gelu(x, approximate=True)

def _silu(x):
    return jax.nn.silu(x)

def _sigmoid(x):
    return jax.nn.sigmoid(x)

def _layernorm(x, axis=-1, eps=1e-05):
    m = jnp.mean(x, axis=axis, keepdims=True)
    v = jnp.var(x, axis=axis, keepdims=True)
    return (x - m) / jnp.sqrt(v + eps)

def _scatter_add(tgt, idx, src, axis=0):
    return tgt.at[idx].add(src)

def _segment_sum(src, seg, n):
    return jax.ops.segment_sum(src, seg, n)
kernel_name = 'mk_gps_d1_gnn_r32_e59c22'

def setup_inputs(seed: int=0):
    np.random.seed(seed)
    _w = jnp.asarray

    def _rec_inputs():
        import jax
        import jax.numpy as jnp
        _gk = jax.random.key(seed)
        x = -0.0002117 + 1 * jax.random.normal(jax.random.fold_in(_gk, 1), (50000, 256), jnp.float32)
        src = jax.random.randint(jax.random.fold_in(_gk, 2), (50000,), 0, 50000, jnp.int32)
        dst = jnp.minimum((50000 * jax.random.uniform(jax.random.fold_in(_gk, 3), (50000,)) ** 2.0).astype(jnp.int32), 49999)
        _o = jnp.argsort(dst, stable=True)
        src = src[_o]
        dst = dst[_o]
        edge_attr_64 = jax.random.uniform(jax.random.fold_in(_gk, 11), (50000, 64), jnp.float32, 0.0, 1)
        return (x, src, dst, edge_attr_64)
    x, src, dst, edge_attr_64 = _rec_inputs()

    def _L0_gnn_setup():
        import jax, jax.numpy as jnp
        import numpy as np
        N = 3125
        E = 50000
        D_NODE = 256
        D_MSG = 128
        D_RAD = 64
        HEADS = 4
        OUTC = D_MSG // HEADS

        def _w(key, shape):
            fan_in = shape[-1]
            return jax.random.normal(key, shape, dtype=jnp.float32) / jnp.sqrt(jnp.float32(fan_in))
        key = jax.random.key(seed)
        ks = jax.random.split(key, 16)
        x = jax.random.normal(ks[0], (N, D_NODE), dtype=jnp.float32)
        edge_attr = jax.random.uniform(ks[1], (E, D_RAD), dtype=jnp.float32)
        edge_index = jax.random.randint(ks[2], (2, E), 0, N, dtype=jnp.int64)
        return {'x': x, 'edge_attr': edge_attr, 'edge_index': edge_index, 'W_edge': _w(ks[3], (D_RAD, D_RAD)), 'W_n2m': _w(ks[4], (D_MSG, D_NODE)), 'Wq': _w(ks[5], (D_MSG, D_MSG)), 'bq': jnp.zeros((D_MSG,), jnp.float32), 'Wk': _w(ks[6], (D_MSG, D_MSG)), 'bk': jnp.zeros((D_MSG,), jnp.float32), 'Wv': _w(ks[7], (D_MSG, D_MSG)), 'bv': jnp.zeros((D_MSG,), jnp.float32), 'We': _w(ks[8], (D_MSG, D_RAD)), 'Wskip': _w(ks[9], (D_MSG, D_MSG)), 'bskip': jnp.zeros((D_MSG,), jnp.float32), 'Wbeta': _w(ks[10], (1, 3 * D_MSG)), 'W_m2n': _w(ks[11], (D_NODE, D_MSG))}
    _L0_gnn_all = _L0_gnn_setup()
    _L0_gnn_in = {k: v for k, v in _L0_gnn_all.items() if k in ('W_edge', 'W_n2m', 'Wq', 'bq', 'Wk', 'bk', 'Wv', 'bv', 'We', 'Wskip', 'bskip', 'Wbeta', 'W_m2n')}
    del _L0_gnn_all

    def _L0_mix_setup():
        import jax, jax.numpy as jnp
        import numpy as np
        D_MODEL = 256
        NUM_HEADS = 8
        DEPTH = D_MODEL // NUM_HEADS
        B, L = (32, 128)

        def _feature_map(x):
            return jax.nn.elu(x) + 1.0
        key = jax.random.key(seed)
        ks = jax.random.split(key, 9)
        sc = 1.0 / np.sqrt(D_MODEL)
        return {'x': jax.random.normal(ks[0], (B, L, D_MODEL), dtype=jnp.float32), 'wq': jax.random.normal(ks[1], (D_MODEL, D_MODEL), dtype=jnp.float32) * sc, 'bq': jnp.zeros((D_MODEL,), dtype=jnp.float32), 'wk': jax.random.normal(ks[2], (D_MODEL, D_MODEL), dtype=jnp.float32) * sc, 'bk': jnp.zeros((D_MODEL,), dtype=jnp.float32), 'wv': jax.random.normal(ks[3], (D_MODEL, D_MODEL), dtype=jnp.float32) * sc, 'bv': jnp.zeros((D_MODEL,), dtype=jnp.float32), 'wo': jax.random.normal(ks[4], (D_MODEL, D_MODEL), dtype=jnp.float32) * sc, 'bo': jnp.zeros((D_MODEL,), dtype=jnp.float32)}
    _L0_mix_all = _L0_mix_setup()
    _L0_mix_in = {k: v for k, v in _L0_mix_all.items() if k in ('wq', 'bq', 'wk', 'bk', 'wv', 'bv', 'wo', 'bo')}
    del _L0_mix_all

    def _L0_ffn_setup():
        import jax, jax.numpy as jnp
        import numpy as np
        IN_CH = 256
        OUT_CH = 256
        key = jax.random.key(seed)
        kx, kw, kb = jax.random.split(key, 3)
        x = jax.random.normal(kx, (8, 128, IN_CH), dtype=jnp.float32)
        bound = 1.0 / np.sqrt(IN_CH)
        weight = jax.random.uniform(kw, (OUT_CH, IN_CH), dtype=jnp.float32, minval=-bound, maxval=bound)
        bias = jax.random.uniform(kb, (OUT_CH,), dtype=jnp.float32, minval=-bound, maxval=bound)
        return {'x': x, 'weight': weight, 'bias': bias}
    _L0_ffn_all = _L0_ffn_setup()
    _L0_ffn_in = {k: v for k, v in _L0_ffn_all.items() if k in ('weight', 'bias')}
    del _L0_ffn_all
    return {'x': x, 'src': src, 'dst': dst, 'edge_attr_64': edge_attr_64, 'L0_gnn_W_edge': _L0_gnn_in['W_edge'], 'L0_gnn_W_n2m': _L0_gnn_in['W_n2m'], 'L0_gnn_Wq': _L0_gnn_in['Wq'], 'L0_gnn_bq': _L0_gnn_in['bq'], 'L0_gnn_Wk': _L0_gnn_in['Wk'], 'L0_gnn_bk': _L0_gnn_in['bk'], 'L0_gnn_Wv': _L0_gnn_in['Wv'], 'L0_gnn_bv': _L0_gnn_in['bv'], 'L0_gnn_We': _L0_gnn_in['We'], 'L0_gnn_Wskip': _L0_gnn_in['Wskip'], 'L0_gnn_bskip': _L0_gnn_in['bskip'], 'L0_gnn_Wbeta': _L0_gnn_in['Wbeta'], 'L0_gnn_W_m2n': _L0_gnn_in['W_m2n'], 'L0_mix_wq': _L0_mix_in['wq'], 'L0_mix_bq': _L0_mix_in['bq'], 'L0_mix_wk': _L0_mix_in['wk'], 'L0_mix_bk': _L0_mix_in['bk'], 'L0_mix_wv': _L0_mix_in['wv'], 'L0_mix_bv': _L0_mix_in['bv'], 'L0_mix_wo': _L0_mix_in['wo'], 'L0_mix_bo': _L0_mix_in['bo'], 'L0_ffn_weight': _L0_ffn_in['weight'], 'L0_ffn_bias': _L0_ffn_in['bias']}

def reference(x, src, dst, edge_attr_64, L0_gnn_W_edge, L0_gnn_W_n2m, L0_gnn_Wq, L0_gnn_bq, L0_gnn_Wk, L0_gnn_bk, L0_gnn_Wv, L0_gnn_bv, L0_gnn_We, L0_gnn_Wskip, L0_gnn_bskip, L0_gnn_Wbeta, L0_gnn_W_m2n, L0_mix_wq, L0_mix_bq, L0_mix_wk, L0_mix_bk, L0_mix_wv, L0_mix_bv, L0_mix_wo, L0_mix_bo, L0_ffn_weight, L0_ffn_bias):
    import jax
    import jax.numpy as jnp

    def _L0_gnn_ref(x, edge_attr, edge_index, W_edge, W_n2m, Wq, bq, Wk, bk, Wv, bv, We, Wskip, bskip, Wbeta, W_m2n):
        import jax, jax.numpy as jnp
        import numpy as np
        N = 3125
        E = 50000
        D_NODE = 256
        D_MSG = 128
        D_RAD = 64
        HEADS = 4
        OUTC = D_MSG // HEADS

        def _w(key, shape):
            fan_in = shape[-1]
            return jax.random.normal(key, shape, dtype=jnp.float32) / jnp.sqrt(jnp.float32(fan_in))
        src = edge_index[0]
        dst = edge_index[1]
        n = x.shape[0]
        scale = 1.0 / jnp.sqrt(jnp.float32(OUTC))
        ee = edge_attr @ W_edge.T
        m = x @ W_n2m.T
        q = (m @ Wq.T + bq).reshape(n, HEADS, OUTC)
        k = (m @ Wk.T + bk).reshape(n, HEADS, OUTC)
        v = (m @ Wv.T + bv).reshape(n, HEADS, OUTC)
        e = (ee @ We.T).reshape(-1, HEADS, OUTC)
        kj = k[src] + e
        alpha = jnp.einsum('ehc,ehc->eh', q[dst], kj) * scale
        amax = jax.ops.segment_max(alpha, dst, num_segments=n)
        expa = jnp.exp(alpha - amax[dst])
        asum = jax.ops.segment_sum(expa, dst, num_segments=n)
        alpha = expa / (asum[dst] + 1e-16)
        msg = (v[src] + e) * alpha[..., None]
        out = jax.ops.segment_sum(msg, dst, num_segments=n)
        out = out.reshape(n, D_MSG)
        x_r = m @ Wskip.T + bskip
        beta = jax.nn.sigmoid(jnp.concatenate([out, x_r, out - x_r], axis=-1) @ Wbeta.T)
        out = beta * x_r + (1.0 - beta) * out
        return out @ W_m2n.T

    def _L0_mix_ref(x, wq, bq, wk, bk, wv, bv, wo, bo):
        import jax, jax.numpy as jnp
        import numpy as np
        D_MODEL = 256
        NUM_HEADS = 8
        DEPTH = D_MODEL // NUM_HEADS
        B, L = (32, 128)

        def _feature_map(x):
            return jax.nn.elu(x) + 1.0
        b, l, _ = x.shape
        q = (x @ wq + bq).reshape(b, l, NUM_HEADS, DEPTH)
        k = (x @ wk + bk).reshape(b, l, NUM_HEADS, DEPTH)
        v = (x @ wv + bv).reshape(b, l, NUM_HEADS, DEPTH)
        q = _feature_map(q)
        k = _feature_map(k)
        kv = jnp.einsum('blhd,blhe->bhde', k, v)
        k_sum = jnp.sum(k, axis=1)
        qkv = jnp.einsum('blhd,bhde->blhe', q, kv)
        normalizer = jnp.einsum('blhd,bhd->blh', q, k_sum) + 1e-06
        out = qkv / normalizer[..., None]
        out = out.reshape(b, l, D_MODEL)
        return out @ wo + bo

    def _L0_ffn_ref(x, weight, bias):
        import jax, jax.numpy as jnp
        import numpy as np
        IN_CH = 256
        OUT_CH = 256
        return jnp.einsum('bsi,oi->bso', x, weight) + bias
    edge_index = jnp.stack([src, dst])
    xn = _layernorm(x, axis=-1)
    x = x + _L0_gnn_ref(xn, edge_attr_64, edge_index, L0_gnn_W_edge, L0_gnn_W_n2m, L0_gnn_Wq, L0_gnn_bq, L0_gnn_Wk, L0_gnn_bk, L0_gnn_Wv, L0_gnn_bv, L0_gnn_We, L0_gnn_Wskip, L0_gnn_bskip, L0_gnn_Wbeta, L0_gnn_W_m2n) + _L0_mix_ref(xn[None], L0_mix_wq, L0_mix_bq, L0_mix_wk, L0_mix_bk, L0_mix_wv, L0_mix_bv, L0_mix_wo, L0_mix_bo)[0]
    x = x + _L0_ffn_ref(_layernorm(x, axis=-1)[None], L0_ffn_weight, L0_ffn_bias)[0]
    return x

_drawn_inputs = setup_inputs


def setup_inputs(seed=0):
    import zlib

    import numpy as np

    out = dict(_drawn_inputs(seed))
    spreads = {'L0_gnn_bq': (0.0, 0.8),
     'L0_gnn_bk': (0.0, 0.8),
     'L0_gnn_bv': (0.0, 0.1),
     'L0_gnn_bskip': (0.0, 0.1),
     'L0_mix_bq': (0.0, 0.8),
     'L0_mix_bk': (0.0, 0.8),
     'L0_mix_bv': (0.0, 0.1),
     'L0_mix_bo': (0.0, 0.1)}
    factors = {'L0_mix_wq': 8.0, 'L0_mix_wk': 7.335, 'L0_mix_wv': 7.04}
    for name, (base, spread) in spreads.items():
        noise = np.random.default_rng([zlib.crc32(name.encode()), seed]).standard_normal(out[name].shape)
        drawn = base * np.exp(spread * noise) if base else spread * noise
        out[name] = jnp.asarray(drawn.astype(out[name].dtype))
    for name, factor in factors.items():
        out[name] = (out[name] * factor).astype(out[name].dtype)
    return out
```

```python
from contextlib import ExitStack

import concourse.bass as bass
from concourse import mybir

F32 = mybir.dt.float32
I32 = mybir.dt.int32
ALU = mybir.AluOpType
ACT = mybir.ActivationFunctionType
AX_X = mybir.AxisListType.X

P = 128
N, D = 50000, 256
E, R = 50000, 64
C, H = 128, 4
HC = C // H
MH = 8
MC = D // MH
DC = D // P
T = 4
U = T * P
NU = -(-N // U)
LAST = N - U
DUP = (NU - 1) * U - LAST
EPS = 1e-5
BIG = 1e30
SCALE = float(HC) ** -0.5
NOWHERE = 1 << 20
assert N == E and C == P and NU <= P and DUP % T == 0


class Step:

    def __init__(self, i, k, total, cycle=2, apart=None):
        self.i, self.k, self.total, self.cycle, self.apart = i, k, total, cycle, apart
        self.j = cycle * i + k
        self.s = k % 2
        self.static = isinstance(i, int)

    def slot(self, n):
        return self.k % n

    def back(self, n):
        k = (self.k - n) % self.cycle
        return Step(self.i + (self.k - n - k) // self.cycle, k, self.total, self.cycle, self.apart)

    def wait_count(self, eng, semaphore, value):
        wait = eng.wait_ge(semaphore, value)
        if self.apart is not None:
            wait.then_inc(self.apart, 1)

    def valid(self):
        return not self.static or 0 <= self.j < self.total

    def last(self):
        return self.static and self.j == self.total - 1

    def wait(self, eng, semaphore, per_step=1):
        self.wait_count(eng, semaphore, (self.j + 1) * per_step)

    def wait_free(self, eng, semaphore, per_step=1, slots=2):
        if not self.static or self.j >= slots:
            self.wait_count(eng, semaphore, (self.j - slots + 1) * per_step)

    def wait_dma(self, eng, slot_semaphores, dmas=1):
        n = len(slot_semaphores)
        uses = self.i * (self.cycle // n) + self.k // n + 1
        self.wait_count(eng, slot_semaphores[self.slot(n)], uses * (16 * dmas))

    def wait_dma_free(self, eng, slot_semaphores, dmas=1):
        n = len(slot_semaphores)
        if not self.static or self.j >= n:
            uses = self.i * (self.cycle // n) + self.k // n
            self.wait_count(eng, slot_semaphores[self.slot(n)], uses * (16 * dmas))


def sweep(eng, total, lead, lag, body, cycle=2, apart=None):
    head = -(-lead // cycle) * cycle
    end = (total - 1) // cycle * cycle
    for j in range(head):
        body(Step(j // cycle, j % cycle, total, cycle, apart))
    with eng.Fori(head // cycle, end // cycle) as i:
        for k in range(cycle):
            body(Step(i, k, total, cycle, apart))
    for j in range(end, total + lag):
        body(Step(j // cycle, j % cycle, total, cycle, apart))


def unit_rows(dram, st):
    if st.last():
        return dram[LAST:LAST + U, :]
    if st.static:
        return dram[st.j * U:(st.j + 1) * U, :]
    return dram[bass.ds(st.j * U, U), :]


def half_unit(st):
    return st.i * (st.cycle // 2) + st.k // 2


def half_rows(dram, st):
    u = half_unit(st)
    if st.static:
        first = LAST if u == NU - 1 else u * U
        rows = dram[first:first + U, :]
    else:
        rows = dram[bass.ds(u * U, U), :]
    return rows.rearrange("(p h t) d -> h p t d", h=2, t=2)[st.s]


class Tools:

    def __init__(self, nc, ctx):
        self.nc, self.ctx = nc, ctx

    def sb(self, name, shape, dt=F32):
        return self.ctx.enter_context(self.nc.sbuf_tensor(name, shape, dt))

    def psum(self, name, shape, dt=F32):
        return self.ctx.enter_context(self.nc.psum_tensor(name, shape, dt))

    def sem(self, name):
        return self.ctx.enter_context(self.nc.semaphore(name))

    def sems(self, *names):
        return [self.sem(n) for n in names]

    def slots(self, name, n=2):
        return [self.sem(f"{name}{s}") for s in range(n)]


def setup(nc, A, K):
    with ExitStack() as ctx:
        t = Tools(nc, ctx)
        n2m_nat = t.sb("n2m_nat", [P, D])
        kvqs_nat = t.sb("kvqs_nat", [P, 4, P])
        we_nat = t.sb("we_nat", [P, R])
        wedge_nat = t.sb("wedge_nat", [R, R])
        m2n_nat = t.sb("m2n_nat", [P, DC, P])
        ffn_nat = t.sb("ffn_nat", [P, DC, D])
        weT = t.sb("weT", [R, C])
        b_q = t.sb("b_q", [P, D])
        b_k = t.sb("b_k", [P, D])
        wbeta = t.sb("wbeta", [P, 3, C])
        src_i = t.sb("src_i", [NU, U], I32)
        dst_i = t.sb("dst_i", [NU, U], I32)
        prev_i = t.sb("prev_i", [NU, 1], I32)
        next_i = t.sb("next_i", [NU, 1], I32)
        src_f = t.sb("src_f", [NU, U])
        dst_f = t.sb("dst_f", [NU, U + 2])
        row_f = t.sb("row_f", [NU, U])
        keep = t.sb("keep", [NU, U])
        psA = t.psum("setup_psA", [P, 512])
        psB = t.psum("setup_psB", [P, 512])
        psC = t.psum("setup_psC", [P, 512])
        psD = t.psum("setup_psD", [P, 512])
        psE = t.psum("setup_psE", [P, 512])
        psF = t.psum("setup_psF", [P, 512])
        psG = t.psum("setup_psG", [P, 512])
        psH = t.psum("setup_psH", [P, 512])
        weights_in, index_in, edges_filled, const_set, const_done = t.sems(
            "weights_in", "index_in", "edges_filled", "const_set", "const_done")
        weights_turned, weT_ready, edgeT_ready, cols_turned, rows_turned = t.sems(
            "weights_turned", "weT_ready", "edgeT_ready", "cols_turned", "rows_turned")
        vec, dst_ready, rows_ready = t.sems("setup_vec", "dst_ready", "rows_ready")

        loads = [
            (n2m_nat[:], A["L0_gnn_W_n2m"]),
            (we_nat[:], A["L0_gnn_We"]),
            (wedge_nat[:], A["L0_gnn_W_edge"]),
            (m2n_nat[:], A["L0_gnn_W_m2n"].rearrange("(c p) m -> p c m", c=DC)),
            (ffn_nat[:], A["L0_ffn_weight"].rearrange("(c p) i -> p c i", c=DC)),
            (K.mixq[:], A["L0_mix_wq"].rearrange("(c p) o -> p c o", c=DC)),
            (K.mixk[:], A["L0_mix_wk"].rearrange("(c p) o -> p c o", c=DC)),
            (K.mixv[:], A["L0_mix_wv"].rearrange("(c p) o -> p c o", c=DC)),
            (K.mixo[:], A["L0_mix_wo"].rearrange("(c p) o -> p c o", c=DC)),
            (wbeta[:].rearrange("p a c -> p (a c)"), A["L0_gnn_Wbeta"].to_broadcast([P, 3 * C])),
        ]
        for n, w in enumerate(("Wk", "Wv", "Wq", "Wskip")):
            loads.append((kvqs_nat[:, n, :], A["L0_gnn_" + w]))
        for n, b in enumerate(("bk", "bv", "bq", "bskip")):
            loads.append((K.b_kvqs[:, n * C:(n + 1) * C], row_of(A["L0_gnn_" + b]).to_broadcast([P, C])))
        for tile, b in ((b_q, "L0_mix_bq"), (b_k, "L0_mix_bk"), (K.b_v, "L0_mix_bv"),
                        (K.b_o, "L0_mix_bo"), (K.b_f, "L0_ffn_bias")):
            loads.append((tile[:], row_of(A[b]).to_broadcast([P, D])))

        def units(v):
            return v[0:(NU - 1) * U].rearrange("(u e) -> u e", e=U)

        src, dst = A["src"], A["dst"]
        index_loads = [
            (src_i[0:NU - 1, :], units(src)), (src_i[NU - 1:NU, :], row_of(src[LAST:N])),
            (dst_i[0:NU - 1, :], units(dst)), (dst_i[NU - 1:NU, :], row_of(dst[LAST:N])),
            (prev_i[1:NU - 1, :], dst[U - 1:(NU - 2) * U].rearrange("(u e) -> u e", e=1)[::U]),
            (prev_i[NU - 1:NU, :], row_of(dst[LAST - 1:LAST])),
            (next_i[0:NU - 1, :], dst[U:(NU - 1) * U + 1].rearrange("(u e) -> u e", e=1)[::U]),
        ]

        with nc.Block() as block:
            @block.sync
            def _(sp):
                sp.wait_ge(edges_filled, 2)
                for to, frm in index_loads:
                    sp.dma_start(to, frm, allow_slow_non_contiguous=True).then_inc(index_in, 16)
                for to, frm in loads:
                    sp.dma_start(to, frm).then_inc(weights_in, 16)

            @block.gpsimd
            def _(pool):
                nc.gpsimd.memset(prev_i[:], -1).then_inc(edges_filled, 1)
                nc.gpsimd.memset(next_i[:], -1).then_inc(edges_filled, 1)
                nc.gpsimd.memset(K.ident[:], 1.0).then_inc(const_set, 1)
                nc.gpsimd.memset(K.head_mask[:], 1.0).then_inc(const_set, 1)
                nc.gpsimd.memset(K.sel_w[:], 1.0).then_inc(const_set, 1)
                nc.gpsimd.memset(K.sel_m[:], 1.0).then_inc(const_set, 1)
                nc.gpsimd.memset(K.not_done[:], 1.0).then_inc(const_set, 1)
                nc.gpsimd.memset(K.last_unit[:], 1.0).then_inc(const_set, 1)
                nc.gpsimd.memset(K.neg_half[:], -0.5).then_inc(const_set, 1)
                nc.gpsimd.memset(K.minus_one[:], -1.0).then_inc(const_set, 1)
                pool.wait_ge(const_set, 8)
                nc.gpsimd.affine_select(out=K.ident[:], in_=K.ident[:], compare_op=ALU.is_equal, fill=0.0,
                                        base=0, pattern=[[-1, P]], channel_multiplier=1).then_inc(const_done, 1)
                mask = K.head_mask[:].rearrange("p (g e) -> p g e", e=MC)
                nc.gpsimd.affine_select(out=mask, in_=mask, compare_op=ALU.is_ge, fill=0.0, base=0,
                                        pattern=[[-MC, P // MC], [0, MC]],
                                        channel_multiplier=1).then_inc(const_set, 1)
                pool.wait_ge(const_set, 9)
                nc.gpsimd.affine_select(out=mask, in_=mask, compare_op=ALU.is_ge, fill=0.0, base=MC - 1,
                                        pattern=[[MC, P // MC], [0, MC]],
                                        channel_multiplier=-1).then_inc(const_done, 1)
                sel = K.sel_w[:].rearrange("h (g c) -> h g c", c=HC)
                nc.gpsimd.affine_select(out=sel, in_=sel, compare_op=ALU.is_equal, fill=0.0, base=0,
                                        pattern=[[-1, H], [0, HC]], channel_multiplier=1).then_inc(const_done, 1)
                nc.gpsimd.affine_select(out=K.sel_m[:], in_=K.sel_m[:], compare_op=ALU.is_equal, fill=0.0,
                                        base=-H, pattern=[[0, C]], channel_multiplier=1).then_inc(const_done, 1)
                nc.gpsimd.affine_select(out=K.not_done[:], in_=K.not_done[:], compare_op=ALU.is_ge, fill=0.0,
                                        base=-(DUP // T), pattern=[[0, 1]],
                                        channel_multiplier=1).then_inc(const_done, 1)
                for col, op in ((0, ALU.is_equal), (1, ALU.not_equal)):
                    nc.gpsimd.affine_select(out=K.last_unit[:, col:col + 1], in_=K.last_unit[:, col:col + 1],
                                            compare_op=op, fill=0.0, base=-(NU - 1), pattern=[[0, 1]],
                                            channel_multiplier=1).then_inc(const_done, 1)

            @block.vector
            def _(dve):
                dve.wait_ge(index_in, 16 * len(index_loads))
                nc.vector.tensor_copy(src_f[:], src_i[:])
                nc.vector.tensor_copy(dst_f[:, 1:U + 1], dst_i[:])
                nc.vector.tensor_copy(dst_f[:, 0:1], prev_i[:])
                nc.vector.tensor_copy(dst_f[:, U + 1:U + 2], next_i[:]).then_inc(dst_ready, 1)
                dve.wait_ge(dst_ready, 1)
                nc.vector.tensor_tensor(K.same[:], dst_f[:, 1:U + 2], dst_f[:, 0:U + 1],
                                        ALU.is_equal).then_inc(vec, 1)
                dve.wait_ge(vec, 1)
                nc.vector.tensor_scalar(K.pen[:], K.same[:], -1.0, BIG, ALU.add, ALU.mult).then_inc(vec, 1)
                nc.vector.tensor_scalar(keep[:], K.same[:, 1:U + 1], float(NOWHERE), None,
                                        ALU.mult).then_inc(vec, 1)
                dve.wait_ge(vec, 3)
                nc.vector.tensor_tensor(row_f[:], keep[:], dst_f[:, 1:U + 1], ALU.add).then_inc(rows_ready, 1)
                dve.wait_ge(cols_turned, 3)
                for cols, ps in ((K.src_cols, psE), (K.dst_cols, psF), (K.row_cols, psG)):
                    nc.vector.tensor_copy(cols[:].rearrange("p u t -> p t u"),
                                          ps[:, 0:T * NU].rearrange("p (t u) -> p t u", t=T))
                dve.wait_ge(weights_in, 16 * len(loads))
                nc.vector.tensor_scalar(K.b_q1[:], b_q[:], 1.0, None, ALU.add)
                nc.vector.tensor_scalar(K.b_k1[:], b_k[:], 1.0, None, ALU.add)
                nc.vector.tensor_tensor(K.gate_w[:, 0, :], wbeta[:, 0, :], wbeta[:, 2, :], ALU.add)
                nc.vector.tensor_tensor(K.gate_w[:, 1, :], wbeta[:, 1, :], wbeta[:, 2, :], ALU.subtract)

            @block.tensor
            def _(pe):
                pe.wait_ge(const_done, 1)
                pe.wait_ge(rows_ready, 1)
                for f, ps in ((src_f[:], psE), (dst_f[:, 1:U + 1], psF), (row_f[:], psG)):
                    for n in range(T):
                        mm = nc.tensor.transpose(ps[:, n * NU:(n + 1) * NU], f[:, n * P:(n + 1) * P],
                                                 K.ident[0:NU, 0:NU])
                    mm.then_inc(cols_turned, 1)
                pe.wait_ge(weights_in, 16 * len(loads))
                nc.tensor.transpose(psD[0:R, 0:C], we_nat[:], K.ident[:]).then_inc(weights_turned, 1)
                for n in range(4):
                    mm = nc.tensor.transpose(psA[:, n * P:(n + 1) * P], kvqs_nat[:, n, :], K.ident[:])
                mm.then_inc(weights_turned, 1)
                for c in range(DC):
                    nc.tensor.transpose(psB[:, c * P:(c + 1) * P], n2m_nat[:, c * P:(c + 1) * P], K.ident[:])
                for c in range(DC):
                    mm = nc.tensor.transpose(psB[:, (DC + c) * P:(DC + c + 1) * P], m2n_nat[:, c, :], K.ident[:])
                mm.then_inc(weights_turned, 1)
                for i in range(DC):
                    for o in range(DC):
                        mm = nc.tensor.transpose(psC[:, i * D + o * P:i * D + (o + 1) * P],
                                                 ffn_nat[:, o, i * P:(i + 1) * P], K.ident[:])
                mm.then_inc(weights_turned, 1)
                pe.wait_ge(weT_ready, 1)
                nc.tensor.matmul(psH[0:R, 0:C], wedge_nat[:], weT[:], start=True, stop=True).then_inc(edgeT_ready, 1)

            @block.scalar
            def _(act):
                act.wait_ge(weights_turned, 1)
                nc.scalar.copy(weT[:], psD[0:R, 0:C]).then_inc(weT_ready, 1)
                act.wait_ge(weights_turned, 4)
                nc.scalar.copy(K.kvqsT[:], psA[:])
                nc.scalar.copy(K.n2mT[:].rearrange("p c m -> p (c m)"), psB[:, 0:D])
                nc.scalar.copy(K.m2nT[:], psB[:, D:2 * D])
                nc.scalar.copy(K.ffnT[:].rearrange("p c o -> p (c o)"), psC[:])
                act.wait_ge(edgeT_ready, 1)
                nc.scalar.copy(K.edgeT[:], psH[0:R, 0:C])


def row_of(v):
    return v.rearrange("(a n) -> a n", a=1)


def project(nc, A, K):
    with ExitStack() as ctx:
        t = Tools(nc, ctx)
        xt = [t.sb(f"pj_x{s}", [P, T, D]) for s in range(2)]
        xn = [t.sb(f"pj_xn{s}", [P, T, D]) for s in range(2)]
        bn = [t.sb(f"pj_bn{s}", [P, T, 6]) for s in range(2)]
        mv = [t.sb(f"pj_mv{s}", [P, T, 2]) for s in range(2)]
        ve = [t.sb(f"pj_ve{s}", [P, T]) for s in range(2)]
        mr = [t.sb(f"pj_mr{s}", [P, T, 2]) for s in range(2)]
        xnT = [t.sb(f"pj_xnT{s}", [P, DC, U]) for s in range(2)]
        mT = [t.sb(f"pj_mT{s}", [P, U]) for s in range(2)]
        pr = [t.sb(f"pj_pr{s}", [P, T, 4 * C]) for s in range(2)]
        zeros = t.sb("pj_zeros", [P, 20 * P])
        psT = [t.psum(f"pj_psT{c}", [P, U]) for c in range(DC)]
        psM = [t.psum(f"pj_psM{s}", [P, U]) for s in range(2)]
        psP = [t.psum(f"pj_psP{n}", [P, 4 * C]) for n in range(T)]
        x_in, tabs_out = t.slots("pj_x_in"), t.slots("pj_tabs_out")
        zero_set, zero_out = t.sems("pj_zero_set", "pj_zero_out")
        bn_done, mv_done, ve_done, pow_done, mr_done, xn_done, stat_done = t.sems(
            "pj_bn_done", "pj_mv_done", "pj_ve_done", "pj_pow_done", "pj_mr_done", "pj_xn_done", "pj_stat_done")
        T_done, T_copied, m_done, m_copied, p_done, p_added = t.sems(
            "pj_T_done", "pj_T_copied", "pj_m_done", "pj_m_copied", "pj_p_done", "pj_p_added")

        def tiles(dram, st):
            return unit_rows(dram, st).rearrange("(p t) d -> p t d", t=T)

        with nc.Block() as block:
            @block.sync
            def _(sp):
                def body(st):
                    if st.valid():
                        st.wait_free(sp, xn_done, T)
                        sp.dma_start(xt[st.s][:], tiles(A["x"], st)).then_inc(x_in[st.s], 16)
                    if st.static and st.j == 0:
                        sp.wait_ge(zero_set, 1)
                        sp.dma_start(K.agg_tab[0:49920, :].rearrange("(p a r) c -> p a (r c)", p=P, r=15),
                                     zeros[:, 0:15 * P].rearrange("p (a r) -> p a r", a=1)
                                     .to_broadcast([P, 26, 15 * P])).then_inc(zero_out, 16)
                        sp.dma_start(K.agg_tab[49920:N, :], zeros[0:80, 0:C]).then_inc(zero_out, 16)
                    done = st.back(4)
                    if done.valid():
                        done.wait(sp, p_added, T)
                        if done.last():
                            done.back(1).wait_dma(sp, tabs_out, 3)
                        for tab, lo, hi in ((K.kv_tab, 0, 2 * C), (K.q_tab, 2 * C, 3 * C), (K.skip_tab, 3 * C, 4 * C)):
                            sp.dma_start(tiles(tab, done), pr[done.s][:, :, lo:hi]).then_inc(tabs_out[done.s], 16)
                sweep(sp, NU, 6, 4, body)
                sp.wait_ge(zero_out, 32)
                for s in range(2):
                    sp.wait_ge(tabs_out[s], 16 * 3 * (NU // 2))

            @block.vector
            def _(dve):
                nc.vector.memset(zeros[:], 0.0).then_inc(zero_set, 1)

                def body(st):
                    if st.valid():
                        st.wait_dma(dve, x_in)
                        st.wait_free(dve, mv_done, T)
                        for n in range(T):
                            nc.vector.bn_stats(bn[st.s][:, n, :], xt[st.s][:, n, :]).then_inc(bn_done, 1)
                        st.wait_free(dve, mr_done)
                        for n in range(T):
                            dve.wait_ge(bn_done, st.j * T + n + 1).then_inc(K.dve_waits, 1)
                            nc.vector.bn_aggr(mv[st.s][:, n, :], bn[st.s][:, n, :]).then_inc(mv_done, 1)
                    done = st.back(3)
                    if done.valid():
                        done.wait_dma_free(dve, tabs_out, 3)
                        for n in range(T):
                            dve.wait_ge(p_done, done.j * T + n + 1)
                            nc.vector.tensor_tensor(pr[done.s][:, n, :], psP[n][:], K.b_kvqs[:],
                                                    ALU.add).then_inc(p_added, 1)
                sweep(dve, NU, 6, 3, body)

            @block.gpsimd
            def _(pool):
                def body(st):
                    if st.valid():
                        st.wait(pool, mv_done, T)
                        nc.gpsimd.tensor_scalar(ve[st.s][:], mv[st.s][:, :, 1], EPS, None, ALU.add).then_inc(ve_done, 1)
                        st.wait_free(pool, stat_done)
                        st.wait(pool, ve_done)
                        nc.gpsimd.tensor_copy(mr[st.s][:, :, 0], mv[st.s][:, :, 0]).then_inc(pow_done, 1)
                        nc.gpsimd.tensor_tensor(mr[st.s][:, :, 1], ve[st.s][:], K.neg_half[:], ALU.pow
                                                ).then_inc(mr_done, 1)
                        st.wait(pool, pow_done)
                        st.wait(pool, mr_done)
                        st.wait_free(pool, T_done)
                        for n in range(T):
                            nc.gpsimd.tensor_scalar(xn[st.s][:, n, :], xt[st.s][:, n, :], mr[st.s][:, n, 0:1],
                                                    mr[st.s][:, n, 1:2], ALU.subtract, ALU.mult
                                                    ).then_inc(xn_done, 1)
                        nc.gpsimd.tensor_copy(K.stat_at(st.j), mr[st.s][:].rearrange("p t a -> p (t a)")
                                              ).then_inc(stat_done, 1)
                sweep(pool, NU, 2, 0, body, apart=K.pool_waits)

            @block.tensor
            def _(pe):
                def body(st):
                    if st.valid():
                        st.wait(pe, xn_done, T)
                        if not (st.static and st.j == 0):
                            pe.wait_ge(T_copied, st.j * DC)
                        for c in range(DC):
                            for n in range(T):
                                mm = nc.tensor.transpose(psT[c][:, n * P:(n + 1) * P],
                                                         xn[st.s][:, n, c * P:(c + 1) * P], K.ident[:])
                        mm.then_inc(T_done, 1)
                    mid = st.back(1)
                    if mid.valid():
                        mid.wait(pe, T_copied, DC)
                        mid.wait_free(pe, m_copied)
                        for c in range(DC):
                            mm = nc.tensor.matmul(psM[mid.s][:], K.n2mT[:, c, :], xnT[mid.s][:, c, :],
                                                  start=(c == 0), stop=(c == DC - 1))
                        mm.then_inc(m_done, 1)
                    late = st.back(2)
                    if late.valid():
                        late.wait(pe, m_copied)
                        for n in range(T):
                            if not (late.static and late.j == 0):
                                pe.wait_ge(p_added, (late.j - 1) * T + n + 1)
                            nc.tensor.matmul(psP[n][:], mT[late.s][:, n * P:(n + 1) * P], K.kvqsT[:],
                                             start=True, stop=True).then_inc(p_done, 1)
                sweep(pe, NU, 4, 2, body)

            @block.scalar
            def _(act):
                def body(st):
                    if st.valid():
                        st.wait(act, T_done)
                        st.wait_free(act, m_done)
                        for c in range(DC):
                            nc.scalar.copy(xnT[st.s][:, c, :], psT[c][:]).then_inc(T_copied, 1)
                    mid = st.back(1)
                    if mid.valid():
                        mid.wait(act, m_done)
                        mid.wait_free(act, p_done, T)
                        nc.scalar.copy(mT[mid.s][:], psM[mid.s][:]).then_inc(m_copied, 1)
                sweep(act, NU, 4, 1, body)


def attend(nc, A, K):
    with ExitStack() as ctx:
        t = Tools(nc, ctx)
        xt = [t.sb(f"at_x{s}", [P, T, D]) for s in range(2)]
        xn = [t.sb(f"at_xn{s}", [P, T, D + 1]) for s in range(4)]
        mr = [t.sb(f"at_mr{s}", [P, T, 2]) for s in range(2)]
        xnT = [t.sb(f"at_xnT{s}", [P, DC, U]) for s in range(2)]
        z1 = [t.sb(f"at_z1{s}", [P, T, D]) for s in range(2)]
        ex = [t.sb(f"at_ex{s}", [P, T, D]) for s in range(2)]
        phi = [t.sb(f"at_phi{s}", [P, T, D]) for s in range(2)]
        ea = [t.sb(f"at_ea{s}", [P, T, R]) for s in range(2)]
        eaT = [t.sb(f"at_eaT{s}", [R, U]) for s in range(2)]
        kv = [t.sb(f"at_kv{s}", [P, T, 2 * C]) for s in range(2)]
        qd = [t.sb(f"at_qd{s}", [P, T, C]) for s in range(2)]
        vj = [t.sb(f"at_vj{s}", [P, T, C]) for s in range(2)]
        prod = t.sb("at_prod", [P, T, C])
        sc = [t.sb(f"at_sc{s}", [P, H, T]) for s in range(2)]
        scT = [t.sb(f"at_scT{s}", [H * T, P]) for s in range(2)]
        idx = [t.sb(f"at_idx{s}", [P, 2, T], I32) for s in range(2)]
        psT = [t.psum(f"at_psT{c}", [P, U]) for c in range(DC)]
        psK = t.psum("at_psK", [P, 2, D])
        psE = t.psum("at_psE", [P, T, C])
        psX = t.psum("at_psX", [P, U])
        psS = t.psum("at_psS", [P, P])
        acc = [t.psum(f"at_acc{c}", [P, D + 1]) for c in range(DC)]
        x_in, ea_in, kv_in, qd_in = t.slots("at_x_in"), t.slots("at_ea_in"), t.slots("at_kv_in"), t.slots("at_qd_in")
        vj_out, sc_out = t.slots("at_vj_out"), t.slots("at_sc_out")
        ones_set, mr_done, xn_done, T_done, T_copied, k_done, z_done, ex_done, phi_done, masked, acc_step = t.sems(
            "at_ones_set", "at_mr_done", "at_xn_done", "at_T_done", "at_T_copied", "at_k_done", "at_z_done",
            "at_ex_done", "at_phi_done", "at_masked", "at_acc_step")
        idx_done, eaT_done, eaT_copied, e_done, vj_done, kj_done, prod_done, sc_done, scT_done, scT_copied = t.sems(
            "at_idx_done", "at_eaT_done", "at_eaT_copied", "at_e_done", "at_vj_done", "at_kj_done",
            "at_prod_done", "at_sc_done", "at_scT_done", "at_scT_copied")

        def edge_tiles(dram, st):
            return unit_rows(dram, st).rearrange("(t p) d -> p t d", p=P)

        with nc.Block() as block:
            @block.sync
            def _(sp):
                def body(st):
                    if st.valid():
                        st.wait_free(sp, eaT_done)
                        sp.dma_start(ea[st.s][:], edge_tiles(A["edge_attr_64"], st)).then_inc(ea_in[st.s], 16)
                        st.wait_free(sp, xn_done, T)
                        sp.dma_start(xt[st.s][:], unit_rows(A["x"], st).rearrange("(p t) d -> p t d", t=T)
                                     ).then_inc(x_in[st.s], 16)
                    mid = st.back(2)
                    if mid.valid():
                        mid.wait(sp, vj_done)
                        if mid.last():
                            mid.back(1).wait_dma(sp, vj_out)
                        sp.dma_start(edge_tiles(K.vj_tab, mid), vj[mid.s][:]).then_inc(vj_out[mid.s], 16)
                    late = st.back(3)
                    if late.valid():
                        late.wait(sp, scT_copied)
                        rows = H * T
                        to = (K.score_tab[late.j * rows:(late.j + 1) * rows, :] if late.static else
                              K.score_tab[bass.ds(late.j * rows, rows), :])
                        sp.dma_start(to, scT[late.s][:]).then_inc(sc_out[late.s], 16)
                sweep(sp, NU, 6, 3, body, cycle=4)
                for s in range(2):
                    sp.wait_ge(vj_out[s], 16 * (NU // 2))
                    sp.wait_ge(sc_out[s], 16 * (NU // 2))

            @block.gpsimd
            def _(pool):
                for s in range(4):
                    nc.gpsimd.memset(xn[s][:, :, D:D + 1], 1.0).then_inc(ones_set, 1)

                def gather(st):
                    st.wait(pool, idx_done)
                    st.wait_free(pool, vj_done)
                    st.wait_free(pool, kj_done)
                    for n in range(T):
                        nc.gpsimd.indirect_dma_start(
                            out=kv[st.s][:, n, :], out_offset=None, in_=K.kv_tab[:, :],
                            in_offset=bass.IndirectOffsetOnAxis(ap=idx[st.s][:, 0, n:n + 1], axis=0),
                            ).then_inc(kv_in[st.s], 16)
                    st.wait_free(pool, prod_done)
                    for n in range(T):
                        nc.gpsimd.indirect_dma_start(
                            out=qd[st.s][:, n, :], out_offset=None, in_=K.q_tab[:, :],
                            in_offset=bass.IndirectOffsetOnAxis(ap=idx[st.s][:, 1, n:n + 1], axis=0),
                            ).then_inc(qd_in[st.s], 16)

                def body(st):
                    if st.valid():
                        gather(st)
                sweep(pool, NU, 2, 0, body, cycle=4, apart=K.pool_waits)

            @block.vector
            def _(dve):
                def body(st):
                    if st.valid():
                        st.wait_dma_free(dve, kv_in, T)
                        st.wait_dma_free(dve, qd_in, T)
                        nc.vector.tensor_copy(idx[st.s][:, 0, :], K.cols_at(K.src_cols, st.j))
                        nc.vector.tensor_copy(idx[st.s][:, 1, :], K.cols_at(K.dst_cols, st.j)).then_inc(idx_done, 1)
                        st.wait_free(dve, xn_done, T)
                        nc.vector.tensor_copy(mr[st.s][:].rearrange("p t a -> p (t a)"), K.stat_at(st.j)
                                              ).then_inc(mr_done, 1)
                        st.wait(dve, mr_done)
                        st.wait_dma(dve, x_in)
                        st.wait_free(dve, T_done, slots=4)
                        st.wait_free(dve, acc_step, slots=4)
                        for n in range(T):
                            nc.vector.tensor_scalar(xn[st.slot(4)][:, n, 0:D], xt[st.s][:, n, :], mr[st.s][:, n, 0:1],
                                                    mr[st.s][:, n, 1:2], ALU.subtract, ALU.mult
                                                    ).then_inc(xn_done, 1)
                    mid = st.back(1)
                    if mid.valid():
                        mid.wait_free(dve, ex_done, 2)
                        mid.wait_free(dve, phi_done, 2)
                        for g in range(2):
                            dve.wait_ge(k_done, mid.j * 2 + g + 1)
                            nc.vector.tensor_tensor(
                                z1[mid.s][:, 2 * g:2 * g + 2, :], psK[:],
                                K.b_k1[:].rearrange("p (a d) -> p a d", a=1).to_broadcast([P, 2, D]),
                                ALU.add).then_inc(z_done, 1)
                        mid.wait(dve, e_done)
                        mid.wait_dma(dve, kv_in, T)
                        mid.wait_dma_free(dve, vj_out)
                        nc.vector.tensor_tensor(vj[mid.s][:], kv[mid.s][:, :, C:2 * C], psE[:], ALU.add
                                                ).then_inc(vj_done, 1)
                        mid.wait(dve, vj_done)
                        nc.vector.tensor_tensor(psE[:], kv[mid.s][:, :, 0:C], psE[:], ALU.add).then_inc(kj_done, 1)
                    late = st.back(2)
                    if late.valid():
                        late.wait_free(dve, acc_step)
                        for g in range(2):
                            dve.wait_ge(ex_done, late.j * 2 + g + 1)
                            nc.vector.scalar_tensor_tensor(
                                out=phi[late.s][:, 2 * g:2 * g + 2, :], in0=ex[late.s][:, 2 * g:2 * g + 2, :],
                                scalar=1.0, in1=z1[late.s][:, 2 * g:2 * g + 2, :], op0=ALU.min, op1=ALU.max
                                ).then_inc(phi_done, 1)
                        if late.last():
                            late.wait(dve, phi_done, 2)
                            nc.vector.tensor_scalar(phi[late.s][:], phi[late.s][:], K.not_done[:, 0:1], None,
                                                    ALU.mult).then_inc(masked, 1)
                    if mid.valid():
                        mid.wait(dve, kj_done)
                        mid.wait_dma(dve, qd_in, T)
                        if not (mid.static and mid.j == 0):
                            dve.wait_ge(sc_done, mid.j)
                        nc.vector.tensor_tensor(prod[:], qd[mid.s][:], psE[:], ALU.mult).then_inc(prod_done, 1)
                        mid.wait(dve, prod_done)
                        mid.wait_free(dve, scT_done)
                        nc.vector.tensor_reduce(sc[mid.s][:].rearrange("p h t -> p t h"),
                                                prod[:].rearrange("p t (h c) -> p t h c", h=H), AX_X, ALU.add
                                                ).then_inc(sc_done, 1)
                sweep(dve, NU, 4, 2, body, cycle=4)

            @block.tensor
            def _(pe):
                pe.wait_ge(ones_set, 4)

                def body(st):
                    if st.valid():
                        st.wait_dma(pe, ea_in)
                        if not (st.static and st.j == 0):
                            pe.wait_ge(eaT_copied, st.j).then_inc(K.pe_waits, 1)
                        for n in range(T):
                            mm = nc.tensor.transpose(psX[0:R, n * P:(n + 1) * P], ea[st.s][:, n, :], K.ident[:])
                        mm.then_inc(eaT_done, 1)
                        st.wait(pe, xn_done, T)
                        if not (st.static and st.j == 0):
                            pe.wait_ge(T_copied, st.j * DC)
                        for c in range(DC):
                            for n in range(T):
                                mm = nc.tensor.transpose(psT[c][:, n * P:(n + 1) * P],
                                                         xn[st.slot(4)][:, n, c * P:(c + 1) * P], K.ident[:])
                        mm.then_inc(T_done, 1)
                    late = st.back(3)
                    if late.valid():
                        late.wait(pe, phi_done, 2)
                        if late.last():
                            pe.wait_ge(masked, 1)
                        for n in range(T):
                            for c in range(DC):
                                first = late.static and late.j == 0 and n == 0
                                mm = nc.tensor.matmul(acc[c][:], phi[late.s][:, n, c * P:(c + 1) * P],
                                                      xn[late.slot(4)][:, n, :], start=first,
                                                      stop=late.last() and n == T - 1, skip_group_check=True)
                        mm.then_inc(acc_step, 1)
                    mid = st.back(1)
                    if mid.valid():
                        mid.wait(pe, eaT_copied)
                        if not (mid.static and mid.j == 0):
                            pe.wait_ge(prod_done, mid.j)
                        for n in range(T):
                            mm = nc.tensor.matmul(psE[:, n, :], eaT[mid.s][:, n * P:(n + 1) * P], K.edgeT[:],
                                                  start=True, stop=True)
                        mm.then_inc(e_done, 1)
                        mid.wait(pe, T_copied, DC)
                        for g in range(2):
                            if not (mid.static and mid.j == 0 and g == 0):
                                pe.wait_ge(z_done, mid.j * 2 + g)
                            for n in range(2):
                                for c in range(DC):
                                    mm = nc.tensor.matmul(psK[:, n, :],
                                                          xnT[mid.s][:, c, (2 * g + n) * P:(2 * g + n + 1) * P],
                                                          K.mixk[:, c, :], start=(c == 0), stop=(c == DC - 1))
                            mm.then_inc(k_done, 1)
                    score = st.back(2)
                    if score.valid():
                        score.wait(pe, sc_done)
                        if not (score.static and score.j == 0):
                            pe.wait_ge(scT_copied, score.j)
                        nc.tensor.transpose(psS[0:H * T, :], sc[score.s][:].rearrange("p h t -> p (h t)"),
                                            K.ident[:]).then_inc(scT_done, 1)
                sweep(pe, NU, 4, 3, body, cycle=4)

            @block.scalar
            def _(act):
                def body(st):
                    if st.valid():
                        st.wait(act, eaT_done)
                        st.wait_free(act, e_done)
                        nc.scalar.copy(eaT[st.s][:], psX[0:R, :]).then_inc(eaT_copied, 1)
                        st.wait(act, T_done)
                        st.wait_free(act, k_done, 2)
                        for c in range(DC):
                            nc.scalar.copy(xnT[st.s][:, c, :], psT[c][:]).then_inc(T_copied, 1)
                    mid = st.back(1)
                    if mid.valid():
                        mid.wait_free(act, phi_done, 2)
                        for g in range(2):
                            act.wait_ge(z_done, mid.j * 2 + g + 1)
                            nc.scalar.activation(ex[mid.s][:, 2 * g:2 * g + 2, :], z1[mid.s][:, 2 * g:2 * g + 2, :],
                                                 ACT.Exp, bias=K.minus_one[:]).then_inc(ex_done, 1)
                    score = st.back(2)
                    if score.valid():
                        score.wait(act, scT_done)
                        score.wait_dma_free(act, sc_out)
                        nc.scalar.copy(scT[score.s][:], psS[0:H * T, :]).then_inc(scT_copied, 1)
                sweep(act, NU, 4, 2, body, cycle=4)
                act.wait_ge(acc_step, NU)
                for c in range(DC):
                    nc.scalar.copy(K.M[:, c, :], acc[c][:])


def softmax(nc, A, K):
    with ExitStack() as ctx:
        t = Tools(nc, ctx)
        score = t.sb("sm_score", [NU, H, U])
        fwd = t.sb("sm_fwd", [NU, H, U])
        whole = t.sb("sm_whole", [NU, H, U])
        prob = t.sb("sm_prob", [NU, H, U])
        wgt = t.sb("sm_wgt", [NU, H + 1, U])
        hand = t.sb("sm_hand", [NU, 2, H])
        behind = t.sb("sm_behind", [NU, H])
        chain = t.sb("sm_chain", [H, 2, NU])
        carry = t.sb("sm_carry", [H, NU + 2])
        start = t.sb("sm_start", [NU, H])
        psX = t.psum("sm_psX", [P, P])
        psY = t.psum("sm_psY", [P, P])
        psZ = t.psum("sm_psZ", [P, P])
        score_in, wgt_out, vec, hand_ready, turned, carry_ready, turned_back, shifted, prob_ready, wgt_ready = t.sems(
            "sm_score_in", "sm_wgt_out", "sm_vec", "sm_hand_ready", "sm_turned", "sm_carry_ready",
            "sm_turned_back", "sm_shifted", "sm_prob_ready", "sm_wgt_ready")
        BEFORE = U - DUP
        scans = [("on", ALU.add, ALU.max, -BIG), ("back", ALU.add, ALU.max, -BIG),
                 ("on", ALU.mult, ALU.add, 0.0), ("back", ALU.add, ALU.max, -BIG)]

        with nc.Block() as block:
            @block.sync
            def _(sp):
                sp.dma_start(score[:].rearrange("u h e -> u (h e)"),
                             K.score_tab.rearrange("(u r) e -> u (r e)", r=H * T)).then_inc(score_in, 16)
                sp.wait_ge(wgt_ready, 1)
                sp.dma_start(K.wgt_tab.rearrange("(u r) e -> u (r e)", r=H + 1),
                             wgt[:].rearrange("u h e -> u (h e)")).then_inc(wgt_out, 16)
                sp.wait_ge(wgt_out, 16)

            @block.vector
            def _(dve):
                count = [0]

                def chained(ins):
                    ins.then_inc(vec, 1)
                    count[0] += 1
                    dve.wait_ge(vec, count[0])

                def scan_units(n, way, op0, op1, empty, frm, to):
                    gates = K.pen if op0 == ALU.add else K.same
                    along = slice(None) if way == "on" else slice(None, None, -1)
                    gate = gates[:, 0:U] if way == "on" else gates[:, 1:U + 1]
                    end = U - 1 if way == "on" else 0
                    for h in range(H):
                        ins = nc.vector.tensor_tensor_scan(to[:, h, along], gate[:, along], frm[:, h, along],
                                                           empty, op0, op1)
                    chained(ins)
                    chained(nc.vector.tensor_copy(hand[:, 0, :], to[:, :, end]))
                    chained(nc.vector.tensor_reduce(hand[:, 1, 0:1], gate, AX_X, ALU.min))
                    if way == "on":
                        u = NU - 2
                        chained(nc.vector.tensor_copy(hand[u:u + 1, 0, :], to[u:u + 1, :, BEFORE - 1]))
                        chained(nc.vector.tensor_reduce(hand[u:u + 1, 1, 0:1], gate[u:u + 1, 0:BEFORE], AX_X, ALU.min))
                    else:
                        chained(nc.vector.tensor_scalar(behind[:], to[:, :, DUP], K.last_unit[0:NU, 0:1], None,
                                                        ALU.mult))
                        chained(nc.vector.scalar_tensor_tensor(
                            out=hand[:, 0, :], in0=hand[:, 0, :], scalar=K.last_unit[0:NU, 1:2],
                            in1=behind[:], op0=ALU.mult, op1=ALU.add))
                    nc.vector.tensor_copy(hand[:, 1, 1:H], hand[:, 1, 0:1].to_broadcast([NU, H - 1])
                                          ).then_inc(hand_ready, 1)
                    dve.wait_ge(turned, n + 1)
                    nc.vector.memset(carry[:], empty)
                    nc.vector.tensor_copy(chain[:, 0, :], psX[0:H, 0:NU])
                    chained(nc.vector.tensor_copy(chain[:, 1, :], psY[0:H, 0:NU]))
                    nc.vector.tensor_tensor_scan(carry[:, 1:NU + 1][:, along], chain[:, 1, along],
                                                 chain[:, 0, along], empty, op0, op1).then_inc(carry_ready, 1)
                    dve.wait_ge(turned_back, n + 1)
                    chained(nc.vector.tensor_copy(start[:], psZ[0:NU, 0:H]))
                    for h in range(H):
                        ins = nc.vector.tensor_tensor_scan(to[:, h, along], gate[:, along], frm[:, h, along],
                                                           start[:, h:h + 1], op0, op1)
                    chained(ins)

                dve.wait_ge(score_in, 16)
                scan_units(0, *scans[0], score, fwd)
                scan_units(1, *scans[1], fwd, whole)
                nc.vector.tensor_tensor(score[:], score[:], whole[:], ALU.subtract).then_inc(shifted, 1)
                dve.wait_ge(prob_ready, 1)
                scan_units(2, *scans[2], prob, fwd)
                scan_units(3, *scans[3], fwd, whole)
                chained(nc.vector.tensor_scalar(whole[:], whole[:], 1e-16, None, ALU.add))
                chained(nc.vector.reciprocal(whole[:], whole[:]))
                nc.vector.tensor_tensor(wgt[:, 0:H, :], prob[:], whole[:], ALU.mult)
                nc.vector.tensor_copy(wgt[:, H, :], K.same[:, 0:U]).then_inc(wgt_ready, 1)

            @block.scalar
            def _(act):
                act.wait_ge(shifted, 1)
                nc.scalar.activation(prob[:].rearrange("u h e -> u (h e)"), score[:].rearrange("u h e -> u (h e)"),
                                     ACT.Exp, scale=SCALE).then_inc(prob_ready, 1)

            @block.tensor
            def _(pe):
                for n, (way, *_) in enumerate(scans):
                    pe.wait_ge(hand_ready, n + 1)
                    nc.tensor.transpose(psX[0:H, 0:NU], hand[:, 0, :], K.ident[0:NU, 0:NU])
                    nc.tensor.transpose(psY[0:H, 0:NU], hand[:, 1, :], K.ident[0:NU, 0:NU]).then_inc(turned, 1)
                    pe.wait_ge(carry_ready, n + 1)
                    frm = carry[:, 0:NU] if way == "on" else carry[:, 2:NU + 2]
                    nc.tensor.transpose(psZ[0:NU, 0:H], frm, K.ident[0:H, 0:H]).then_inc(turned_back, 1)


def readout(nc, A, K):
    with ExitStack() as ctx:
        t = Tools(nc, ctx)
        MT = t.sb("ro_MT", [P, DC, D])
        kvm = t.sb("ro_kvm", [P, DC, P])
        kvT = t.sb("ro_kvT", [P, DC, P])
        ks = t.sb("ro_ks", [P, DC, P])
        psT = [t.psum(f"ro_psT{c}", [P, D]) for c in range(DC)]
        psV = t.psum("ro_psV", [P, DC, P])
        psKT = t.psum("ro_psKT", [P, DC, P])
        psS = t.psum("ro_psS", [P, DC, P])
        psG = t.psum("ro_psG", [P, DC, D])
        m_turned, m_copied, kv_done, ks_ready, vec, kvm_ready, kv_turned, kv_copied, g_done, ks_turned = t.sems(
            "ro_m_turned", "ro_m_copied", "ro_kv_done", "ro_ks_ready", "ro_vec", "ro_kvm_ready", "ro_kv_turned",
            "ro_kv_copied", "ro_g_done", "ro_ks_turned")
        with nc.Block() as block:
            @block.tensor
            def _(pe):
                for x in range(DC):
                    for d in range(DC):
                        mm = nc.tensor.transpose(psT[x][:, d * P:(d + 1) * P], K.M[:, d, x * P:(x + 1) * P], K.ident[:])
                mm.then_inc(m_turned, 1)
                pe.wait_ge(m_copied, DC)
                for d in range(DC):
                    for x in range(DC):
                        mm = nc.tensor.matmul(psV[:, d, :], MT[:, x, d * P:(d + 1) * P],
                                              K.mixv[:, x, d * P:(d + 1) * P], start=(x == 0), stop=(x == DC - 1))
                mm.then_inc(kv_done, 1)
                pe.wait_ge(ks_ready, 1)
                for d in range(DC):
                    mm = nc.tensor.transpose(psS[:, d, :], ks[:, d, :], K.ident[:])
                mm.then_inc(ks_turned, 1)
                pe.wait_ge(kvm_ready, 1)
                for d in range(DC):
                    mm = nc.tensor.transpose(psKT[:, d, :], kvm[:, d, :], K.ident[:])
                mm.then_inc(kv_turned, 1)
                pe.wait_ge(kv_copied, 1)
                for d in range(DC):
                    mm = nc.tensor.matmul(psG[:, d, :], kvT[:, d, :], K.mixo[:, d, :], start=True, stop=True)
                mm.then_inc(g_done, 1)

            @block.scalar
            def _(act):
                act.wait_ge(m_turned, 1)
                for x in range(DC):
                    nc.scalar.copy(MT[:, x, :], psT[x][:]).then_inc(m_copied, 1)
                act.wait_ge(kv_turned, 1)
                nc.scalar.copy(kvT[:], psKT[:]).then_inc(kv_copied, 1)
                act.wait_ge(g_done, 1)
                nc.scalar.copy(K.G[:], psG[:])

            @block.vector
            def _(dve):
                for d in range(DC):
                    ins = nc.vector.tensor_copy(ks[:, d, :], K.M[:, d, D:D + 1].to_broadcast([P, P]))
                ins.then_inc(ks_ready, 1)
                dve.wait_ge(kv_done, 1)
                for d in range(DC):
                    ins = nc.vector.scalar_tensor_tensor(out=kvm[:, d, :], in0=K.b_v[:, d * P:(d + 1) * P],
                                                         scalar=K.M[:, d, D:D + 1], in1=psV[:, d, :],
                                                         op0=ALU.mult, op1=ALU.add)
                ins.then_inc(vec, 1)
                dve.wait_ge(vec, 1)
                for d in range(DC):
                    ins = nc.vector.tensor_tensor(kvm[:, d, :], kvm[:, d, :], K.head_mask[:], ALU.mult)
                ins.then_inc(kvm_ready, 1)
                dve.wait_ge(ks_turned, 1)
                nc.vector.tensor_copy(K.ksum[:], psS[:].rearrange("p c d -> p (c d)"))


def aggregate(nc, A, K):
    with ExitStack() as ctx:
        t = Tools(nc, ctx)
        vj = [t.sb(f"ag_vj{s}", [P, T, C]) for s in range(2)]
        wg = [t.sb(f"ag_wg{s}", [H + 1, U]) for s in range(2)]
        vT = [t.sb(f"ag_vT{s}", [P, U]) for s in range(2)]
        msg = [t.sb(f"ag_msg{s}", [P, U]) for s in range(2)]
        run = [t.sb(f"ag_run{s}", [P, U]) for s in range(2)]
        rows = [t.sb(f"ag_rows{s}", [P, T, C]) for s in range(2)]
        idx = [t.sb(f"ag_idx{s}", [P, T], I32) for s in range(2)]
        psV = [t.psum(f"ag_psV{s}", [P, U]) for s in range(2)]
        psW = [t.psum(f"ag_psW{s}", [P, U]) for s in range(2)]
        psG = [t.psum(f"ag_psG{s}", [P, U]) for s in range(2)]
        psR = [t.psum(f"ag_psR{s}", [P, T, C]) for s in range(2)]
        vj_in, wg_in, rows_out = t.slots("ag_vj_in"), t.slots("ag_wg_in"), t.slots("ag_rows_out")
        v_turned, v_copied, w_spread, msg_done, run_done, run_turned, rows_done, idx_done = t.sems(
            "ag_v_turned", "ag_v_copied", "ag_w_spread", "ag_msg_done", "ag_run_done", "ag_run_turned",
            "ag_rows_done", "ag_idx_done")

        with nc.Block() as block:
            @block.sync
            def _(sp):
                def body(st):
                    st.wait_free(sp, v_turned)
                    sp.dma_start(vj[st.s][:], unit_rows(K.vj_tab, st).rearrange("(t p) d -> p t d", p=P)
                                 ).then_inc(vj_in[st.s], 16)
                    st.wait_free(sp, w_spread)
                    n = H + 1
                    frm = (K.wgt_tab[st.j * n:(st.j + 1) * n, :] if st.static else
                           K.wgt_tab[bass.ds(st.j * n, n), :])
                    sp.dma_start(wg[st.s][:], frm).then_inc(wg_in[st.s], 16)
                sweep(sp, NU, 2, 0, body)

            @block.tensor
            def _(pe):
                def body(st):
                    if st.valid():
                        st.wait_dma(pe, vj_in)
                        st.wait_free(pe, v_copied)
                        for n in range(T):
                            mm = nc.tensor.transpose(psV[st.s][:, n * P:(n + 1) * P], vj[st.s][:, n, :], K.ident[:])
                        mm.then_inc(v_turned, 1)
                        st.wait_dma(pe, wg_in)
                        st.wait_free(pe, run_done)
                        nc.tensor.matmul(psW[st.s][:], K.sel_w[:], wg[st.s][:], start=True, stop=True)
                        nc.tensor.matmul(psG[st.s][:], K.sel_m[:], wg[st.s][:], start=True, stop=True
                                         ).then_inc(w_spread, 1)
                    late = st.back(2)
                    if late.valid():
                        late.wait(pe, run_done)
                        late.wait_free(pe, rows_done)
                        for n in range(T):
                            mm = nc.tensor.transpose(psR[late.s][:, n, :], run[late.s][:, n * P:(n + 1) * P], K.ident[:])
                        mm.then_inc(run_turned, 1)
                sweep(pe, NU, 4, 2, body)

            @block.scalar
            def _(act):
                def body(st):
                    if st.valid():
                        st.wait(act, v_turned)
                        st.wait_free(act, msg_done)
                        nc.scalar.copy(vT[st.s][:], psV[st.s][:]).then_inc(v_copied, 1)
                    late = st.back(2)
                    if late.valid():
                        late.wait(act, run_turned)
                        late.wait_dma_free(act, rows_out, T)
                        nc.scalar.copy(rows[late.s][:], psR[late.s][:]).then_inc(rows_done, 1)
                sweep(act, NU, 4, 2, body)

            @block.vector
            def _(dve):
                def body(st):
                    if st.valid():
                        st.wait_dma_free(dve, rows_out, T)
                        nc.vector.tensor_copy(idx[st.s][:], K.cols_at(K.row_cols, st.j)).then_inc(idx_done, 1)
                        st.wait(dve, v_copied)
                        st.wait(dve, w_spread)
                        st.wait_free(dve, run_done)
                        nc.vector.tensor_tensor(msg[st.s][:], vT[st.s][:], psW[st.s][:], ALU.mult).then_inc(msg_done, 1)
                    mid = st.back(1)
                    if mid.valid():
                        mid.wait(dve, msg_done)
                        mid.wait_free(dve, run_turned)
                        if mid.static and mid.j == 0:
                            first = 0.0
                        else:
                            dve.wait_ge(run_done, mid.j)
                            col = U - DUP if mid.last() else U
                            first = run[1 - mid.s][:, col - 1:col]
                        nc.vector.tensor_tensor_scan(run[mid.s][:], psG[mid.s][:], msg[mid.s][:], first,
                                                     ALU.mult, ALU.add).then_inc(run_done, 1)
                sweep(dve, NU, 4, 1, body)

            @block.gpsimd
            def _(pool):
                def body(st):
                    st.wait(pool, rows_done)
                    st.wait(pool, idx_done)
                    if st.last():
                        st.back(1).wait_dma(pool, rows_out, T)
                    for n in range(T):
                        nc.gpsimd.indirect_dma_start(
                            out=K.agg_tab[:, :], out_offset=bass.IndirectOffsetOnAxis(ap=idx[st.s][:, n:n + 1], axis=0),
                            in_=rows[st.s][:, n, :], in_offset=None, bounds_check=N - 1, oob_is_err=False,
                            ).then_inc(rows_out[st.s], 16)
                sweep(pool, NU, 2, 0, body, apart=K.pool_waits)
                for s in range(2):
                    pool.wait_ge(rows_out[s], 16 * T * (NU // 2))


def combine(nc, A, K):
    HT = 2
    with ExitStack() as ctx:
        t = Tools(nc, ctx)

        def two(name, shape, dt=F32):
            return [t.sb(f"cb_{name}{s}", shape, dt) for s in range(2)]

        xt = [t.sb(f"cb_x{s}", [P, HT, D]) for s in range(4)]
        ax = two("ax", [P, HT, 2, C])
        mr, xn = two("mr", [P, HT * 2]), two("xn", [P, HT, D])
        xb = [t.sb(f"cb_xb{s}", [P, HT, D]) for s in range(4)]
        xnT = two("xnT", [P, DC, HT * P])
        ex, pk, qn, qnT = two("ex", [P, HT, D]), two("pk", [P, HT, D]), two("qn", [P, HT, D]), two("qnT", [P, DC, HT * P])
        nrm, rn = two("nrm", [P, HT, MH]), two("rn", [P, HT, MH])
        gp, gs, ge, beta = two("gp", [P, HT, 2 * C]), two("gs", [P, HT]), two("ge", [P, HT]), two("beta", [P, HT])
        dif, o, oT = two("dif", [P, HT, C]), two("o", [P, HT, C]), two("oT", [P, HT * P])
        x1, x1b, bn, mv, ve = two("x1", [P, HT, D]), two("x1b", [P, HT, D]), two("bn", [P, HT, 6]), \
            two("mv", [P, HT, 2]), two("ve", [P, HT])
        rs, xm, xmT, y = two("rs", [P, HT]), two("xm", [P, HT, D]), two("xmT", [P, DC, HT * P]), two("y", [P, HT, D])
        psT = t.psum("cb_psT", [P, DC, HT * P])
        psQ = [t.psum(f"cb_psQ{s}", [P, HT, D]) for s in range(2)]
        psN = t.psum("cb_psN", [P, DC, HT * P])
        psO = t.psum("cb_psO", [P, HT * P])
        psF = t.psum("cb_psF", [P, HT, D])
        psM = t.psum("cb_psM", [P, DC, HT * P])
        psY = t.psum("cb_psY", [P, HT, D])
        x_in, ax_in, y_out = t.slots("cb_x_in", 4), t.slots("cb_ax_in"), t.slots("cb_y_out")
        names = ("mr xn xb T Tc q z ex phi pk nrm nre rn qn N Nc gp gs ge gb beta dif o O Oc F x1 x1b bn mv ve rs xm "
                 "M Mc Y y").split()
        S = {n: t.sem("cb_" + n) for n in names}

        with nc.Block() as block:
            @block.sync
            def _(sp):
                def body(st):
                    if st.valid():
                        st.wait_free(sp, S["xn"], HT, slots=4)
                        st.wait_free(sp, S["xb"], slots=4)
                        sp.dma_start(xt[st.slot(4)][:], half_rows(A["x"], st)).then_inc(x_in[st.slot(4)], 16)
                        st.wait_free(sp, S["gp"])
                        st.wait_free(sp, S["o"], HT)
                        sp.dma_start(ax[st.s][:, :, 0, :], half_rows(K.agg_tab, st)).then_inc(ax_in[st.s], 16)
                        sp.dma_start(ax[st.s][:, :, 1, :], half_rows(K.skip_tab, st)).then_inc(ax_in[st.s], 16)
                    done = st.back(5)
                    if done.valid():
                        done.wait(sp, S["y"])
                        if done.static and half_unit(done) == NU - 1:
                            done.back(1).wait_dma(sp, y_out)
                            done.back(2).wait_dma(sp, y_out)
                        sp.dma_start(half_rows(K.out, done), y[done.s][:]).then_inc(y_out[done.s], 16)
                sweep(sp, 2 * NU, 8, 5, body, cycle=4, apart=K.sp_waits)
                for s in range(2):
                    sp.wait_ge(y_out[s], 16 * NU)

            @block.gpsimd
            def _(pool):
                def body(st):
                    if st.valid():
                        st.wait_free(pool, S["xn"], HT)
                        nc.gpsimd.tensor_copy(mr[st.s][:], K.stat_half(st)).then_inc(S["mr"], 1)
                        st.wait(pool, S["mr"])
                        st.wait_dma(pool, x_in)
                        st.wait_free(pool, S["T"])
                        for n in range(HT):
                            nc.gpsimd.tensor_scalar(xn[st.s][:, n, :], xt[st.slot(4)][:, n, :], mr[st.s][:, 2 * n:2 * n + 1],
                                                    mr[st.s][:, 2 * n + 1:2 * n + 2], ALU.subtract, ALU.mult
                                                    ).then_inc(S["xn"], 1)
                        st.wait_free(pool, S["x1"], slots=4)
                        nc.gpsimd.tensor_tensor(xb[st.slot(4)][:], xt[st.slot(4)][:], K.b_o[:].rearrange("p (a d) -> p a d", a=1)
                                                .to_broadcast([P, HT, D]), ALU.add).then_inc(S["xb"], 1)
                        st.wait_dma(pool, ax_in, 2)
                        st.wait_free(pool, S["gs"])
                        nc.gpsimd.tensor_tensor(gp[st.s][:], ax[st.s][:].rearrange("p t a c -> p t (a c)"),
                                                K.gate_w[:].rearrange("p (b a) c -> p b (a c)", b=1)
                                                .to_broadcast([P, HT, 2 * C]), ALU.mult).then_inc(S["gp"], 1)
                        st.wait_free(pool, S["o"], HT)
                        nc.gpsimd.tensor_tensor(dif[st.s][:], ax[st.s][:, :, 1, :], ax[st.s][:, :, 0, :],
                                                ALU.subtract).then_inc(S["dif"], 1)
                    late = st.back(3)
                    if late.valid():
                        late.wait(pool, S["mv"], HT)
                        nc.gpsimd.tensor_scalar(ve[late.s][:], mv[late.s][:, :, 1], EPS, None, ALU.add
                                                ).then_inc(S["ve"], 1)
                        late.wait(pool, S["ve"])
                        late.wait_free(pool, S["xm"], HT)
                        nc.gpsimd.tensor_tensor(rs[late.s][:], ve[late.s][:], K.neg_half[:, 0:HT], ALU.pow
                                                ).then_inc(S["rs"], 1)
                        late.wait_free(pool, S["y"])
                        nc.gpsimd.tensor_tensor(x1b[late.s][:], x1[late.s][:], K.b_f[:].rearrange("p (a d) -> p a d", a=1)
                                                .to_broadcast([P, HT, D]), ALU.add).then_inc(S["x1b"], 1)
                sweep(pool, 2 * NU, 6, 3, body, cycle=4, apart=K.pool_waits)

            @block.vector
            def _(dve):
                def body(st):
                    a = st.back(1)
                    if a.valid():
                        a.wait(dve, S["q"])
                        nc.vector.tensor_tensor(psQ[a.s][:], psQ[a.s][:], K.b_q1[:].rearrange("p (a d) -> p a d", a=1)
                                                .to_broadcast([P, HT, D]), ALU.add).then_inc(S["z"], 1)
                        a.wait(dve, S["gp"])
                        a.wait_free(dve, S["ge"])
                        nc.vector.tensor_reduce(gs[a.s][:], gp[a.s][:], AX_X, ALU.add).then_inc(S["gs"], 1)
                    d = st.back(3)
                    if d.valid():
                        d.wait(dve, S["F"])
                        d.wait(dve, S["xb"])
                        d.wait_free(dve, S["x1b"])
                        d.wait_free(dve, S["xm"], HT)
                        nc.vector.tensor_tensor(x1[d.s][:], xb[d.slot(4)][:], psF[:], ALU.add).then_inc(S["x1"], 1)
                    if a.valid():
                        a.wait(dve, S["ex"])
                        nc.vector.scalar_tensor_tensor(out=psQ[a.s][:], in0=ex[a.s][:], scalar=1.0, in1=psQ[a.s][:],
                                                       op0=ALU.min, op1=ALU.max).then_inc(S["phi"], 1)
                    if d.valid():
                        d.wait(dve, S["x1"])
                        for n in range(HT):
                            nc.vector.bn_stats(bn[d.s][:, n, :], x1[d.s][:, n, :]).then_inc(S["bn"], 1)
                    if a.valid():
                        a.wait(dve, S["phi"])
                        nc.vector.tensor_tensor(pk[a.s][:], psQ[a.s][:], K.ksum[:].rearrange("p (a d) -> p a d", a=1)
                                                .to_broadcast([P, HT, D]), ALU.mult).then_inc(S["pk"], 1)
                    if d.valid():
                        d.wait_free(dve, S["ve"])
                        dve.wait_ge(S["bn"], (d.j + 1) * HT).then_inc(K.dve_waits, 1)
                        for n in range(HT):
                            nc.vector.bn_aggr(mv[d.s][:, n, :], bn[d.s][:, n, :]).then_inc(S["mv"], 1)
                    if a.valid():
                        a.wait(dve, S["pk"])
                        nc.vector.tensor_reduce(nrm[a.s][:], pk[a.s][:].rearrange("p t (h d) -> p t h d", h=MH),
                                                AX_X, ALU.add).then_inc(S["nrm"], 1)
                        a.wait(dve, S["ge"])
                        nc.vector.tensor_scalar(ge[a.s][:], ge[a.s][:], 1.0, None, ALU.add).then_inc(S["gb"], 1)
                        a.wait(dve, S["nrm"])
                        nc.vector.tensor_scalar(nrm[a.s][:], nrm[a.s][:], 1e-6, None, ALU.add).then_inc(S["nre"], 1)
                        a.wait(dve, S["gb"])
                        nc.vector.reciprocal(beta[a.s][:], ge[a.s][:]).then_inc(S["beta"], 1)
                        a.wait(dve, S["nre"])
                        nc.vector.reciprocal(rn[a.s][:], nrm[a.s][:]).then_inc(S["rn"], 1)
                        a.wait(dve, S["beta"])
                        a.wait(dve, S["dif"])
                        a.wait_free(dve, S["O"])
                        for n in range(HT):
                            nc.vector.scalar_tensor_tensor(out=o[a.s][:, n, :], in0=dif[a.s][:, n, :],
                                                           scalar=beta[a.s][:, n:n + 1], in1=ax[a.s][:, n, 0, :],
                                                           op0=ALU.mult, op1=ALU.add).then_inc(S["o"], 1)
                        a.wait(dve, S["rn"])
                        a.wait_free(dve, S["N"])
                        nc.vector.tensor_tensor(qn[a.s][:].rearrange("p t (h d) -> p t h d", h=MH),
                                                psQ[a.s][:].rearrange("p t (h d) -> p t h d", h=MH),
                                                rn[a.s][:].rearrange("p t (h a) -> p t h a", a=1)
                                                .to_broadcast([P, HT, MH, MC]), ALU.mult).then_inc(S["qn"], 1)
                    if d.valid():
                        d.wait(dve, S["rs"])
                        d.wait_free(dve, S["M"])
                        for n in range(HT):
                            nc.vector.tensor_scalar(xm[d.s][:, n, :], x1[d.s][:, n, :], mv[d.s][:, n, 0:1],
                                                    rs[d.s][:, n:n + 1], ALU.subtract, ALU.mult).then_inc(S["xm"], 1)
                    e = st.back(5)
                    if e.valid():
                        e.wait(dve, S["Y"])
                        e.wait(dve, S["x1b"])
                        e.wait_dma_free(dve, y_out)
                        nc.vector.tensor_tensor(y[e.s][:], x1b[e.s][:], psY[:], ALU.add).then_inc(S["y"], 1)
                sweep(dve, 2 * NU, 8, 5, body, cycle=4)

            @block.tensor
            def _(pe):
                def turn(ps, tile, st):
                    for c in range(DC):
                        for n in range(HT):
                            mm = nc.tensor.transpose(ps[:, c, n * P:(n + 1) * P], tile[:, n, c * P:(c + 1) * P],
                                                     K.ident[:])
                    return mm

                def not_first(st):
                    return not (st.static and st.j == 0)

                def body(st):
                    if st.valid():
                        st.wait(pe, S["xn"], HT)
                        if not_first(st):
                            pe.wait_ge(S["Tc"], st.j)
                        turn(psT, xn[st.s], st).then_inc(S["T"], 1)
                    e = st.back(4)
                    if e.valid():
                        e.wait(pe, S["xm"], HT)
                        if not_first(e):
                            pe.wait_ge(S["Mc"], e.j)
                        turn(psM, xm[e.s], e).then_inc(S["M"], 1)
                    b = st.back(2)
                    if b.valid():
                        b.wait(pe, S["qn"])
                        if not_first(b):
                            pe.wait_ge(S["Nc"], b.j)
                        turn(psN, qn[b.s], b).then_inc(S["N"], 1)
                        b.wait(pe, S["o"], HT)
                        if not_first(b):
                            pe.wait_ge(S["Oc"], b.j)
                        for n in range(HT):
                            mm = nc.tensor.transpose(psO[:, n * P:(n + 1) * P], o[b.s][:, n, :], K.ident[:])
                        mm.then_inc(S["O"], 1)
                    if st.valid():
                        st.wait(pe, S["Tc"])
                        st.wait_free(pe, S["qn"])
                        for n in range(HT):
                            for c in range(DC):
                                mm = nc.tensor.matmul(psQ[st.s][:, n, :], xnT[st.s][:, c, n * P:(n + 1) * P],
                                                      K.mixq[:, c, :], start=(c == 0), stop=(c == DC - 1))
                        mm.then_inc(S["q"], 1)
                    if b.valid():
                        b.wait(pe, S["Nc"])
                        b.wait(pe, S["Oc"])
                        if not_first(b):
                            pe.wait_ge(S["x1"], b.j)
                        for n in range(HT):
                            for c in range(DC):
                                nc.tensor.matmul(psF[:, n, :], qnT[b.s][:, c, n * P:(n + 1) * P], K.G[:, c, :],
                                                 start=(c == 0), stop=False)
                            mm = nc.tensor.matmul(psF[:, n, :], oT[b.s][:, n * P:(n + 1) * P], K.m2nT[:],
                                                  start=False, stop=True)
                        mm.then_inc(S["F"], 1)
                    if e.valid():
                        e.wait(pe, S["Mc"])
                        if not_first(e):
                            pe.wait_ge(S["y"], e.j)
                        for n in range(HT):
                            for c in range(DC):
                                mm = nc.tensor.matmul(psY[:, n, :], xmT[e.s][:, c, n * P:(n + 1) * P],
                                                      K.ffnT[:, c, :], start=(c == 0), stop=(c == DC - 1))
                        mm.then_inc(S["Y"], 1)
                sweep(pe, 2 * NU, 6, 4, body, cycle=4)

            @block.scalar
            def _(act):
                def body(st):
                    if st.valid():
                        st.wait(act, S["T"])
                        st.wait_free(act, S["q"])
                        nc.scalar.copy(xnT[st.s][:], psT[:]).then_inc(S["Tc"], 1)
                    e = st.back(4)
                    if e.valid():
                        e.wait(act, S["M"])
                        e.wait_free(act, S["Y"])
                        nc.scalar.copy(xmT[e.s][:], psM[:]).then_inc(S["Mc"], 1)
                    b = st.back(2)
                    if b.valid():
                        b.wait(act, S["N"])
                        b.wait_free(act, S["F"])
                        nc.scalar.copy(qnT[b.s][:], psN[:]).then_inc(S["Nc"], 1)
                        b.wait(act, S["O"])
                        nc.scalar.copy(oT[b.s][:], psO[:]).then_inc(S["Oc"], 1)
                    a = st.back(1)
                    if a.valid():
                        a.wait(act, S["z"])
                        a.wait_free(act, S["phi"])
                        nc.scalar.activation(ex[a.s][:], psQ[a.s][:], ACT.Exp, bias=K.minus_one[:]).then_inc(S["ex"], 1)
                        a.wait(act, S["gs"])
                        a.wait_free(act, S["beta"])
                        nc.scalar.activation(ge[a.s][:], gs[a.s][:], ACT.Exp, scale=-1.0).then_inc(S["ge"], 1)
                sweep(act, 2 * NU, 6, 4, body, cycle=4)


class Kept:

    def __init__(self, nc, ctx, out):
        t = Tools(nc, ctx)
        self.out = out
        self.pool_waits, self.dve_waits, self.pe_waits, self.sp_waits = t.sems(
            "pool_waits", "dve_waits", "pe_waits", "sp_waits")

        def dram(name, shape):
            return nc.dram_tensor(name, shape, F32).ap()

        self.kv_tab, self.q_tab, self.skip_tab = dram("kv_tab", (N, 2 * C)), dram("q_tab", (N, C)), dram("skip_tab", (N, C))
        self.vj_tab, self.agg_tab = dram("vj_tab", (E, C)), dram("agg_tab", (N, C))
        self.score_tab, self.wgt_tab = dram("score_tab", (NU * H * T, P)), dram("wgt_tab", (NU * (H + 1), U))
        self.ident = t.sb("ident", [P, P])
        self.neg_half = t.sb("neg_half", [P, T])
        self.minus_one = t.sb("minus_one", [P, 1])
        self.head_mask = t.sb("head_mask", [P, P])
        self.sel_w = t.sb("sel_w", [H + 1, C])
        self.sel_m = t.sb("sel_m", [H + 1, C])
        self.not_done = t.sb("not_done", [P, 1])
        self.last_unit = t.sb("last_unit", [P, 2])
        self.mixq, self.mixk, self.mixv, self.mixo = [t.sb(n, [P, DC, D]) for n in ("mixq", "mixk", "mixv", "mixo")]
        self.b_kvqs = t.sb("b_kvqs", [P, 4 * C])
        self.b_q1, self.b_k1, self.b_v, self.b_o, self.b_f = [t.sb(n, [P, D]) for n in ("b_q1", "b_k1", "b_v", "b_o", "b_f")]
        self.kvqsT = t.sb("kvqsT", [P, 4 * C])
        self.n2mT = t.sb("n2mT", [P, DC, C])
        self.m2nT = t.sb("m2nT", [P, D])
        self.ffnT = t.sb("ffnT", [P, DC, D])
        self.edgeT = t.sb("edgeT", [R, C])
        self.gate_w = t.sb("gate_w", [P, 2, C])
        self.src_cols, self.dst_cols, self.row_cols = [t.sb(n, [P, NU, T], I32) for n in ("src_cols", "dst_cols", "row_cols")]
        self.same = t.sb("same", [NU, U + 1])
        self.pen = t.sb("pen", [NU, U + 1])
        self.stat = t.sb("stat", [P, NU, T * 2])
        self.M = t.sb("M", [P, DC, D + 1])
        self.G = t.sb("G", [P, DC, D])
        self.ksum = t.sb("ksum", [P, D])

    def stat_at(self, j):
        if isinstance(j, int):
            return self.stat[:, j, :]
        return self.stat[:, bass.ds(j, 1), :].rearrange("p a b -> p (a b)")

    def stat_half(self, st):
        half = slice(st.s * T, (st.s + 1) * T)
        if st.static:
            return self.stat[:, half_unit(st), half]
        return self.stat[:, bass.ds(half_unit(st), 1), half].rearrange("p a b -> p (a b)")

    def cols_at(self, cols, j):
        if isinstance(j, int):
            return cols[:, j, :]
        return cols[:, bass.ds(j, 1), :].rearrange("p a b -> p (a b)")


STAGES = [setup, project, attend, softmax, readout, aggregate, combine]


def build(nc, A, out):
    with ExitStack() as ctx:
        K = Kept(nc, ctx, out)
        for stage in STAGES:
            stage(nc, A, K)


def kernel(**inputs):
    import numpy as _np
    import concourse.bacc as _bacc
    from concourse import mybir as _mybir
    from concourse.bass_utils import run_bass_kernel_spmd as _run

    nc = _bacc.Bacc("TRN2", target_bir_lowering=False, num_devices=1)
    arrays, args = {}, {}
    for name, a in inputs.items():
        a = _np.ascontiguousarray(a)
        arrays[f"in_{name}_dram"] = a
        args[name] = nc.dram_tensor(f"in_{name}_dram", a.shape, _mybir.dt.from_np(a.dtype), kind="ExternalInput").ap()
    out = nc.dram_tensor("out_0_dram", (N, D), F32, kind="ExternalOutput").ap()
    build(nc, args, out)
    r = _run(nc, [arrays], core_ids=[0])
    return r.results[0]["out_0_dram"]
```

```python
from contextlib import ExitStack

import concourse.bass as bass
from concourse import mybir

F32 = mybir.dt.float32
BF16 = mybir.dt.bfloat16
I32 = mybir.dt.int32
ALU = mybir.AluOpType
ACT = mybir.ActivationFunctionType
AX_X = mybir.AxisListType.X

P = 128
N, D = 50000, 256
E, R = 50000, 64
C, H = 128, 4
HC = C // H
MH = 8
MC = D // MH
DC = D // P
T = 4
U = T * P
NU = -(-N // U)
LAST = N - U
DUP = (NU - 1) * U - LAST
EPS = 1e-5
BIG = 1e30
SCALE = float(HC) ** -0.5
NOWHERE = 1 << 20
assert N == E and C == P and NU <= P and DUP % T == 0


class Step:

    def __init__(self, i, k, total, cycle=2, apart=None):
        self.i, self.k, self.total, self.cycle, self.apart = i, k, total, cycle, apart
        self.j = cycle * i + k
        self.s = k % 2
        self.static = isinstance(i, int)

    def slot(self, n):
        return self.k % n

    def back(self, n):
        k = (self.k - n) % self.cycle
        return Step(self.i + (self.k - n - k) // self.cycle, k, self.total, self.cycle, self.apart)

    def ahead(self, n):
        return self.back(-n)

    def wait_count(self, eng, semaphore, value):
        wait = eng.wait_ge(semaphore, value)
        if self.apart is not None:
            wait.then_inc(self.apart, 1)

    def valid(self):
        return not self.static or 0 <= self.j < self.total

    def last(self):
        return self.static and self.j == self.total - 1

    def wait(self, eng, semaphore, per_step=1):
        self.wait_count(eng, semaphore, (self.j + 1) * per_step)

    def wait_free(self, eng, semaphore, per_step=1, slots=2):
        if not self.static or self.j >= slots:
            self.wait_count(eng, semaphore, (self.j - slots + 1) * per_step)

    def wait_dma(self, eng, slot_semaphores, dmas=1):
        n = len(slot_semaphores)
        uses = self.i * (self.cycle // n) + self.k // n + 1
        self.wait_count(eng, slot_semaphores[self.slot(n)], uses * (16 * dmas))

    def wait_dma_free(self, eng, slot_semaphores, dmas=1):
        n = len(slot_semaphores)
        if not self.static or self.j >= n:
            uses = self.i * (self.cycle // n) + self.k // n
            self.wait_count(eng, slot_semaphores[self.slot(n)], uses * (16 * dmas))


def sweep(eng, total, lead, lag, body, cycle=2, apart=None, reach=1):
    head = -(-lead // cycle) * cycle
    end = (total - 1 - reach) // cycle * cycle
    for j in range(head):
        body(Step(j // cycle, j % cycle, total, cycle, apart))
    with eng.Fori(head // cycle, end // cycle) as i:
        for k in range(cycle):
            body(Step(i, k, total, cycle, apart))
    for j in range(end, total + lag):
        body(Step(j // cycle, j % cycle, total, cycle, apart))


def unit_rows(dram, st):
    if st.last():
        return dram[LAST:LAST + U, :]
    if st.static:
        return dram[st.j * U:(st.j + 1) * U, :]
    return dram[bass.ds(st.j * U, U), :]


def half_unit(st):
    return st.i * (st.cycle // 2) + st.k // 2


def half_rows(dram, st):
    u = half_unit(st)
    if st.static:
        first = LAST if u == NU - 1 else u * U
        rows = dram[first:first + U, :]
    else:
        rows = dram[bass.ds(u * U, U), :]
    return rows.rearrange("(p h t) d -> h p t d", h=2, t=2)[st.s]


class Tools:

    def __init__(self, nc, ctx):
        self.nc, self.ctx = nc, ctx
        self.numbers = []

    def sb(self, name, shape, dt=F32):
        return self.ctx.enter_context(self.nc.sbuf_tensor(name, shape, dt))

    def psum(self, name, shape, dt=F32):
        return self.ctx.enter_context(self.nc.psum_tensor(name, shape, dt))

    def sem(self, name):
        semaphore = self.ctx.enter_context(self.nc.semaphore(name))
        self.numbers.append(semaphore.num)
        return semaphore

    def clear(self):
        first, last = min(self.numbers), max(self.numbers)
        assert last - first + 1 == len(self.numbers)
        with self.nc.Block() as block:
            @block.gpsimd
            def _(pool):
                pool.sem_clear(range(first, last + 1))

    def sems(self, *names):
        return [self.sem(n) for n in names]

    def slots(self, name, n=2):
        return [self.sem(f"{name}{s}") for s in range(n)]


def setup(nc, A, K):
    with ExitStack() as ctx:
        t = Tools(nc, ctx)
        n2m_nat = t.sb("n2m_nat", [P, D])
        kvqs_nat = t.sb("kvqs_nat", [P, 4, P])
        we_nat = t.sb("we_nat", [P, R])
        wedge_nat = t.sb("wedge_nat", [R, R])
        m2n_nat = t.sb("m2n_nat", [P, DC, P])
        ffn_nat = t.sb("ffn_nat", [P, DC, D])
        weT = t.sb("weT", [R, C])
        b_k = t.sb("b_k", [P, D])
        b_rows = t.sb("b_rows", [3, 3, D])
        b_rest = t.sb("b_rest", [3, 2, 3, D])
        b_part = t.sb("b_part", [3, 3, 3, D], BF16)
        b_sum = t.sb("b_sum", [3, 2, 3, D], BF16)
        wbeta = t.sb("wbeta", [P, 3, C])
        src_i = t.sb("src_i", [NU, U], I32)
        dst_i = t.sb("dst_i", [NU, U], I32)
        prev_i = t.sb("prev_i", [NU, 1], I32)
        next_i = t.sb("next_i", [NU, 1], I32)
        src_f = t.sb("src_f", [NU, U])
        dst_f = t.sb("dst_f", [NU, U + 2])
        row_f = t.sb("row_f", [NU, U])
        keep = t.sb("keep", [NU, U])
        psA = t.psum("setup_psA", [P, 512])
        psB = t.psum("setup_psB", [P, 512])
        psC = t.psum("setup_psC", [P, 512])
        psD = t.psum("setup_psD", [P, 512])
        psE = t.psum("setup_psE", [P, 512])
        psF = t.psum("setup_psF", [P, 512])
        psG = t.psum("setup_psG", [P, 512])
        psH = t.psum("setup_psH", [P, 512])
        weights_in, index_in, edges_filled, const_set, const_done = t.sems(
            "weights_in", "index_in", "edges_filled", "const_set", "const_done")
        weights_turned, weT_ready, edgeT_ready, cols_turned, rows_turned = t.sems(
            "weights_turned", "weT_ready", "edgeT_ready", "cols_turned", "rows_turned")
        vec, dst_ready, rows_ready, parts = t.sems("setup_vec", "dst_ready", "rows_ready", "bias_parts")

        loads = [
            (n2m_nat[:], A["L0_gnn_W_n2m"]),
            (we_nat[:], A["L0_gnn_We"]),
            (wedge_nat[:], A["L0_gnn_W_edge"]),
            (m2n_nat[:], A["L0_gnn_W_m2n"].rearrange("(c p) m -> p c m", c=DC)),
            (ffn_nat[:], A["L0_ffn_weight"].rearrange("(c p) i -> p c i", c=DC)),
            (K.mixq[:], A["L0_mix_wq"].rearrange("(c p) o -> p c o", c=DC)),
            (K.mixk[:], A["L0_mix_wk"].rearrange("(c p) o -> p c o", c=DC)),
            (K.mixv[:], A["L0_mix_wv"].rearrange("(c p) o -> p c o", c=DC)),
            (K.mixo[:], A["L0_mix_wo"].rearrange("(c p) o -> p c o", c=DC)),
            (wbeta[:].rearrange("p a c -> p (a c)"), A["L0_gnn_Wbeta"].to_broadcast([P, 3 * C])),
        ]
        for n, w in enumerate(("Wk", "Wv", "Wq", "Wskip")):
            loads.append((kvqs_nat[:, n, :], A["L0_gnn_" + w]))
        for n, b in enumerate(("bk", "bv", "bq", "bskip")):
            loads.append((K.b_kvqs[:, n * C:(n + 1) * C], row_of(A["L0_gnn_" + b]).to_broadcast([P, C])))
        for tile, b in ((b_k, "L0_mix_bk"), (K.b_v, "L0_mix_bv")):
            loads.append((tile[:], row_of(A[b]).to_broadcast([P, D])))
        for n, b in enumerate(("L0_mix_bq", "L0_mix_bo", "L0_ffn_bias")):
            loads.append((b_rows[:, n, :], row_of(A[b]).to_broadcast([3, D])))

        def units(v):
            return v[0:(NU - 1) * U].rearrange("(u e) -> u e", e=U)

        src, dst = A["src"], A["dst"]
        index_loads = [
            (src_i[0:NU - 1, :], units(src)), (src_i[NU - 1:NU, :], row_of(src[LAST:N])),
            (dst_i[0:NU - 1, :], units(dst)), (dst_i[NU - 1:NU, :], row_of(dst[LAST:N])),
            (prev_i[1:NU - 1, :], dst[U - 1:(NU - 2) * U].rearrange("(u e) -> u e", e=1)[::U]),
            (prev_i[NU - 1:NU, :], row_of(dst[LAST - 1:LAST])),
            (next_i[0:NU - 1, :], dst[U:(NU - 1) * U + 1].rearrange("(u e) -> u e", e=1)[::U]),
        ]

        with nc.Block() as block:
            @block.sync
            def _(sp):
                sp.wait_ge(edges_filled, 2)
                for to, frm in index_loads:
                    sp.dma_start(to, frm, allow_slow_non_contiguous=True).then_inc(index_in, 16)
                for to, frm in loads:
                    sp.dma_start(to, frm).then_inc(weights_in, 16)

            @block.gpsimd
            def _(pool):
                nc.gpsimd.memset(prev_i[:], -1).then_inc(edges_filled, 1)
                nc.gpsimd.memset(next_i[:], -1).then_inc(edges_filled, 1)
                nc.gpsimd.memset(K.ident[:], 1.0).then_inc(const_set, 1)
                nc.gpsimd.memset(K.head_mask[:], 1.0).then_inc(const_set, 1)
                nc.gpsimd.memset(K.sel_w[:], 1.0).then_inc(const_set, 1)
                nc.gpsimd.memset(K.sel_m[:], 1.0).then_inc(const_set, 1)
                nc.gpsimd.memset(K.not_done[:], 1.0).then_inc(const_set, 1)
                nc.gpsimd.memset(K.last_unit[:], 1.0).then_inc(const_set, 1)
                nc.gpsimd.memset(K.neg_half[:], -0.5).then_inc(const_set, 1)
                nc.gpsimd.memset(K.minus_one[:], -1.0).then_inc(const_set, 1)
                nc.gpsimd.memset(K.ones3[:], 1.0)
                pool.wait_ge(const_set, 8)
                nc.gpsimd.affine_select(out=K.ident[:], in_=K.ident[:], compare_op=ALU.is_equal, fill=0.0,
                                        base=0, pattern=[[-1, P]], channel_multiplier=1).then_inc(const_done, 1)
                mask = K.head_mask[:].rearrange("p (g e) -> p g e", e=MC)
                nc.gpsimd.affine_select(out=mask, in_=mask, compare_op=ALU.is_ge, fill=0.0, base=0,
                                        pattern=[[-MC, P // MC], [0, MC]],
                                        channel_multiplier=1).then_inc(const_set, 1)
                pool.wait_ge(const_set, 9)
                nc.gpsimd.affine_select(out=mask, in_=mask, compare_op=ALU.is_ge, fill=0.0, base=MC - 1,
                                        pattern=[[MC, P // MC], [0, MC]],
                                        channel_multiplier=-1).then_inc(const_done, 1)
                sel = K.sel_w[:].rearrange("h (g c) -> h g c", c=HC)
                nc.gpsimd.affine_select(out=sel, in_=sel, compare_op=ALU.is_equal, fill=0.0, base=0,
                                        pattern=[[-1, H], [0, HC]], channel_multiplier=1).then_inc(const_done, 1)
                nc.gpsimd.affine_select(out=K.sel_m[:], in_=K.sel_m[:], compare_op=ALU.is_equal, fill=0.0,
                                        base=-H, pattern=[[0, C]], channel_multiplier=1).then_inc(const_done, 1)
                nc.gpsimd.affine_select(out=K.not_done[:], in_=K.not_done[:], compare_op=ALU.is_ge, fill=0.0,
                                        base=-(DUP // T), pattern=[[0, 1]],
                                        channel_multiplier=1).then_inc(const_done, 1)
                for col, op in ((0, ALU.is_equal), (1, ALU.not_equal)):
                    nc.gpsimd.affine_select(out=K.last_unit[:, col:col + 1], in_=K.last_unit[:, col:col + 1],
                                            compare_op=op, fill=0.0, base=-(NU - 1), pattern=[[0, 1]],
                                            channel_multiplier=1).then_inc(const_done, 1)

            @block.vector
            def _(dve):
                dve.wait_ge(index_in, 16 * len(index_loads))
                nc.vector.tensor_copy(src_f[:], src_i[:])
                nc.vector.tensor_copy(dst_f[:, 1:U + 1], dst_i[:])
                nc.vector.tensor_copy(dst_f[:, 0:1], prev_i[:])
                nc.vector.tensor_copy(dst_f[:, U + 1:U + 2], next_i[:]).then_inc(dst_ready, 1)
                dve.wait_ge(dst_ready, 1)
                nc.vector.tensor_tensor(K.same[:], dst_f[:, 1:U + 2], dst_f[:, 0:U + 1],
                                        ALU.is_equal).then_inc(vec, 1)
                dve.wait_ge(vec, 1)
                nc.vector.tensor_scalar(K.pen[:], K.same[:], -1.0, BIG, ALU.add, ALU.mult).then_inc(vec, 1)
                nc.vector.tensor_scalar(keep[:], K.same[:, 1:U + 1], float(NOWHERE), None,
                                        ALU.mult).then_inc(vec, 1)
                dve.wait_ge(vec, 3)
                nc.vector.tensor_tensor(row_f[:], keep[:], dst_f[:, 1:U + 1], ALU.add).then_inc(rows_ready, 1)
                dve.wait_ge(cols_turned, 3)
                for cols, ps in ((K.src_cols, psE), (K.dst_cols, psF), (K.row_cols, psG)):
                    nc.vector.tensor_copy(cols[:].rearrange("p u t -> p t u"),
                                          ps[:, 0:T * NU].rearrange("p (t u) -> p t u", t=T))
                dve.wait_ge(weights_in, 16 * len(loads))
                dve.wait_ge(const_done, 1)
                nc.vector.tensor_scalar(K.b_k1[:], b_k[:], 1.0, None, ALU.add)
                nc.vector.tensor_scalar(b_rows[:, 0, :], b_rows[:, 0, :], 1.0, None, ALU.add).then_inc(parts, 1)
                dve.wait_ge(parts, 1)
                rest = b_rows[:]
                for r in range(3):
                    nc.vector.tensor_copy(b_part[:, r], rest).then_inc(parts, 1)
                    dve.wait_ge(parts, 2 * r + 2)
                    if r < 2:
                        nc.vector.tensor_tensor(b_rest[:, r], rest, b_part[:, r], ALU.subtract).then_inc(parts, 1)
                        dve.wait_ge(parts, 2 * r + 3)
                        rest = b_rest[:, r]
                nc.vector.tensor_scalar(b_sum[:, 0], b_part[:, 0], K.ident[0:3, 0:1], None, ALU.mult).then_inc(parts, 1)
                for r in range(1, 3):
                    to = b_sum[:, 1] if r == 1 else K.b_parts[:]
                    dve.wait_ge(parts, 6 + r)
                    nc.vector.scalar_tensor_tensor(out=to, in0=b_part[:, r], scalar=K.ident[0:3, r:r + 1],
                                                   in1=b_sum[:, r - 1], op0=ALU.mult, op1=ALU.add).then_inc(parts, 1)
                nc.vector.tensor_tensor(K.gate_w[:, 0, :], wbeta[:, 0, :], wbeta[:, 2, :], ALU.add)
                nc.vector.tensor_tensor(K.gate_w[:, 1, :], wbeta[:, 1, :], wbeta[:, 2, :], ALU.subtract)

            @block.tensor
            def _(pe):
                pe.wait_ge(const_done, 1)
                pe.wait_ge(rows_ready, 1)
                for f, ps in ((src_f[:], psE), (dst_f[:, 1:U + 1], psF), (row_f[:], psG)):
                    for n in range(T):
                        mm = nc.tensor.transpose(ps[:, n * NU:(n + 1) * NU], f[:, n * P:(n + 1) * P],
                                                 K.ident[0:NU, 0:NU])
                    mm.then_inc(cols_turned, 1)
                pe.wait_ge(weights_in, 16 * len(loads))
                nc.tensor.transpose(psD[0:R, 0:C], we_nat[:], K.ident[:]).then_inc(weights_turned, 1)
                for n in range(4):
                    mm = nc.tensor.transpose(psA[:, n * P:(n + 1) * P], kvqs_nat[:, n, :], K.ident[:])
                mm.then_inc(weights_turned, 1)
                for c in range(DC):
                    nc.tensor.transpose(psB[:, c * P:(c + 1) * P], n2m_nat[:, c * P:(c + 1) * P], K.ident[:])
                for c in range(DC):
                    mm = nc.tensor.transpose(psB[:, (DC + c) * P:(DC + c + 1) * P], m2n_nat[:, c, :], K.ident[:])
                mm.then_inc(weights_turned, 1)
                for i in range(DC):
                    for o in range(DC):
                        mm = nc.tensor.transpose(psC[:, i * D + o * P:i * D + (o + 1) * P],
                                                 ffn_nat[:, o, i * P:(i + 1) * P], K.ident[:])
                mm.then_inc(weights_turned, 1)
                pe.wait_ge(weT_ready, 1)
                nc.tensor.matmul(psH[0:R, 0:C], wedge_nat[:], weT[:], start=True, stop=True).then_inc(edgeT_ready, 1)

            @block.scalar
            def _(act):
                act.wait_ge(weights_turned, 1)
                nc.scalar.copy(weT[:], psD[0:R, 0:C]).then_inc(weT_ready, 1)
                act.wait_ge(weights_turned, 4)
                nc.scalar.copy(K.kvqsT[:], psA[:])
                nc.scalar.copy(K.n2mT[:].rearrange("p c m -> p (c m)"), psB[:, 0:D])
                nc.scalar.copy(K.m2nT[:], psB[:, D:2 * D])
                nc.scalar.copy(K.ffnT[:].rearrange("p c o -> p (c o)"), psC[:])
                act.wait_ge(edgeT_ready, 1)
                nc.scalar.copy(K.edgeT[:], psH[0:R, 0:C])
        t.clear()


def row_of(v):
    return v.rearrange("(a n) -> a n", a=1)


def project(nc, A, K):
    with ExitStack() as ctx:
        t = Tools(nc, ctx)
        xt = [t.sb(f"pj_x{s}", [P, T, D]) for s in range(4)]
        xn = [t.sb(f"pj_xn{s}", [P, T, D]) for s in range(2)]
        bn = [t.sb(f"pj_bn{s}", [P, T, 6]) for s in range(2)]
        mv = [t.sb(f"pj_mv{s}", [P, T, 2]) for s in range(2)]
        ve = [t.sb(f"pj_ve{s}", [P, T]) for s in range(2)]
        mr = [t.sb(f"pj_mr{s}", [P, T, 2]) for s in range(2)]
        xnT = [t.sb(f"pj_xnT{s}", [P, DC, U]) for s in range(2)]
        mT = [t.sb(f"pj_mT{s}", [P, U]) for s in range(2)]
        pr = [t.sb(f"pj_pr{s}", [P, T, 4 * C]) for s in range(2)]
        zeros = t.sb("pj_zeros", [P, 20 * P])
        psT = [t.psum(f"pj_psT{c}", [P, U]) for c in range(DC)]
        psM = [t.psum(f"pj_psM{s}", [P, U]) for s in range(2)]
        psP = [t.psum(f"pj_psP{n}", [P, 4 * C]) for n in range(T)]
        x_in, tabs_out = t.slots("pj_x_in", 4), t.slots("pj_tabs_out")
        zero_set, zero_out = t.sems("pj_zero_set", "pj_zero_out")
        bn_done, mv_done, ve_done, pow_done, mr_done, xn_done, stat_done = t.sems(
            "pj_bn_done", "pj_mv_done", "pj_ve_done", "pj_pow_done", "pj_mr_done", "pj_xn_done", "pj_stat_done")
        T_done, T_copied, m_done, m_copied, p_done, p_added = t.sems(
            "pj_T_done", "pj_T_copied", "pj_m_done", "pj_m_copied", "pj_p_done", "pj_p_added")

        def tiles(dram, st):
            return unit_rows(dram, st).rearrange("(p t) d -> p t d", t=T)

        with nc.Block() as block:
            @block.sync
            def _(sp):
                def body(st):
                    if st.valid():
                        st.wait_free(sp, xn_done, T, slots=4)
                        sp.dma_start(xt[st.slot(4)][:], tiles(A["x"], st)).then_inc(x_in[st.slot(4)], 16)
                    if st.static and st.j == 0:
                        sp.wait_ge(zero_set, 1)
                        sp.dma_start(K.agg_tab[0:49920, :].rearrange("(p a r) c -> p a (r c)", p=P, r=15),
                                     zeros[:, 0:15 * P].rearrange("p (a r) -> p a r", a=1)
                                     .to_broadcast([P, 26, 15 * P])).then_inc(zero_out, 16)
                        sp.dma_start(K.agg_tab[49920:N, :], zeros[0:80, 0:C]).then_inc(zero_out, 16)
                    done = st.back(5)
                    if done.valid():
                        done.wait(sp, p_added, T)
                        if done.last():
                            done.back(1).wait_dma(sp, tabs_out, 3)
                        for tab, lo, hi in ((K.kv_tab, 0, 2 * C), (K.q_tab, 2 * C, 3 * C), (K.skip_tab, 3 * C, 4 * C)):
                            sp.dma_start(tiles(tab, done), pr[done.s][:, :, lo:hi]).then_inc(tabs_out[done.s], 16)
                sweep(sp, NU, 6, 5, body, cycle=4)
                sp.wait_ge(zero_out, 32)
                for s in range(2):
                    sp.wait_ge(tabs_out[s], 16 * 3 * (NU // 2))

            @block.vector
            def _(dve):
                nc.vector.memset(zeros[:], 0.0).then_inc(zero_set, 1)

                def body(st):
                    if st.valid():
                        st.wait_dma(dve, x_in)
                        st.wait_free(dve, mv_done, T)
                        for n in range(T):
                            nc.vector.bn_stats(bn[st.s][:, n, :], xt[st.slot(4)][:, n, :]).then_inc(bn_done, 1)
                        st.wait_free(dve, mr_done)
                        for n in range(T):
                            dve.wait_ge(bn_done, st.j * T + n + 1).then_inc(K.dve_waits, 1)
                            nc.vector.bn_aggr(mv[st.s][:, n, :], bn[st.s][:, n, :]).then_inc(mv_done, 1)
                        st.wait(dve, pow_done)
                        st.wait_free(dve, stat_done)
                        st.wait_free(dve, xn_done, T)
                        nc.vector.scalar_tensor_tensor(out=mr[st.s][:, :, 1], in0=mv[st.s][:, :, 0], scalar=-1.0,
                                                       in1=mr[st.s][:, :, 0], op0=ALU.mult, op1=ALU.mult
                                                       ).then_inc(mr_done, 1)
                    done = st.back(4)
                    if done.valid():
                        done.wait_dma_free(dve, tabs_out, 3)
                        for n in range(T):
                            dve.wait_ge(p_done, done.j * T + n + 1)
                            nc.vector.tensor_tensor(pr[done.s][:, n, :], psP[n][:], K.b_kvqs[:],
                                                    ALU.add).then_inc(p_added, 1)
                sweep(dve, NU, 6, 4, body, cycle=4)

            @block.gpsimd
            def _(pool):
                def body(st):
                    if st.valid():
                        st.wait(pool, mv_done, T)
                        nc.gpsimd.tensor_scalar(ve[st.s][:], mv[st.s][:, :, 1], EPS, None, ALU.add).then_inc(ve_done, 1)
                        st.wait_free(pool, mr_done)
                        st.wait_free(pool, stat_done)
                        st.wait_free(pool, xn_done, T)
                        st.wait(pool, ve_done)
                        nc.gpsimd.tensor_tensor(mr[st.s][:, :, 0], ve[st.s][:], K.neg_half[:], ALU.pow
                                                ).then_inc(pow_done, 1)
                    kept = st.back(1)
                    if kept.valid():
                        kept.wait(pool, mr_done)
                        nc.gpsimd.tensor_copy(K.stat_at(kept.j), mr[kept.s][:].rearrange("p t a -> p (t a)")
                                              ).then_inc(stat_done, 1)
                sweep(pool, NU, 2, 1, body, cycle=4, apart=K.pool_waits)

            @block.tensor
            def _(pe):
                def body(st):
                    if st.valid():
                        st.wait(pe, xn_done, T)
                        if not (st.static and st.j == 0):
                            pe.wait_ge(T_copied, st.j * DC)
                        for c in range(DC):
                            for n in range(T):
                                mm = nc.tensor.transpose(psT[c][:, n * P:(n + 1) * P],
                                                         xn[st.s][:, n, c * P:(c + 1) * P], K.ident[:])
                        mm.then_inc(T_done, 1)
                    mid = st.back(1)
                    if mid.valid():
                        mid.wait(pe, T_copied, DC)
                        mid.wait_free(pe, m_copied)
                        for c in range(DC):
                            mm = nc.tensor.matmul(psM[mid.s][:], K.n2mT[:, c, :], xnT[mid.s][:, c, :],
                                                  start=(c == 0), stop=(c == DC - 1))
                        mm.then_inc(m_done, 1)
                    late = st.back(2)
                    if late.valid():
                        late.wait(pe, m_copied)
                        for n in range(T):
                            if not (late.static and late.j == 0):
                                pe.wait_ge(p_added, (late.j - 1) * T + n + 1)
                            nc.tensor.matmul(psP[n][:], mT[late.s][:, n * P:(n + 1) * P], K.kvqsT[:],
                                             start=True, stop=True).then_inc(p_done, 1)
                sweep(pe, NU, 4, 2, body, cycle=4)

            @block.scalar
            def _(act):
                def normalise(st):
                    st.wait(act, mr_done)
                    st.wait_dma(act, x_in)
                    st.wait_free(act, T_done)
                    for n in range(T):
                        nc.scalar.activation(xn[st.s][:, n, :], xt[st.slot(4)][:, n, :], ACT.Identity,
                                             scale=mr[st.s][:, n, 0:1], bias=mr[st.s][:, n, 1:2]
                                             ).then_inc(xn_done, 1)

                def body(st):
                    if st.static and st.j == 0:
                        normalise(st)
                    if st.valid():
                        st.wait(act, T_done)
                        st.wait_free(act, m_done)
                        for c in range(DC):
                            nc.scalar.copy(xnT[st.s][:, c, :], psT[c][:]).then_inc(T_copied, 1)
                    mid = st.back(1)
                    if mid.valid():
                        mid.wait(act, m_done)
                        mid.wait_free(act, p_done, T)
                        nc.scalar.copy(mT[mid.s][:], psM[mid.s][:]).then_inc(m_copied, 1)
                    if st.ahead(1).valid():
                        normalise(st.ahead(1))
                sweep(act, NU, 4, 1, body, cycle=4)
        t.clear()


def attend(nc, A, K):
    with ExitStack() as ctx:
        t = Tools(nc, ctx)
        xt = [t.sb(f"at_x{s}", [P, T, D]) for s in range(4)]
        xn = [t.sb(f"at_xn{s}", [P, T, D + 1]) for s in range(4)]
        mr = [t.sb(f"at_mr{s}", [P, T, 2]) for s in range(2)]
        xnT = [t.sb(f"at_xnT{s}", [P, DC, U]) for s in range(2)]
        z1 = [t.sb(f"at_z1{s}", [P, T, D]) for s in range(2)]
        ex = [t.sb(f"at_ex{s}", [P, T, D]) for s in range(2)]
        phi = [t.sb(f"at_phi{s}", [P, T, D]) for s in range(2)]
        ea = [t.sb(f"at_ea{s}", [P, T, R]) for s in range(4)]
        eaT = [t.sb(f"at_eaT{s}", [R, U]) for s in range(2)]
        kv = [t.sb(f"at_kv{s}", [P, T, 2 * C]) for s in range(4)]
        qd = [t.sb(f"at_qd{s}", [P, T, C]) for s in range(4)]
        vj = [t.sb(f"at_vj{s}", [P, T, C]) for s in range(2)]
        prod = t.sb("at_prod", [P, T, C])
        sc = [t.sb(f"at_sc{s}", [P, H, T]) for s in range(2)]
        scT = [t.sb(f"at_scT{s}", [H * T, P]) for s in range(2)]
        idx = [t.sb(f"at_idx{s}", [P, 2, T], I32) for s in range(4)]
        psT = [t.psum(f"at_psT{c}", [P, U]) for c in range(DC)]
        psK = t.psum("at_psK", [P, 2, D])
        psE = t.psum("at_psE", [P, T, C])
        psX = t.psum("at_psX", [P, U])
        psS = t.psum("at_psS", [P, P])
        acc = [t.psum(f"at_acc{c}", [P, D + 1]) for c in range(DC)]
        x_in, ea_in = t.slots("at_x_in", 4), t.slots("at_ea_in", 4)
        kv_in, qd_in = t.slots("at_kv_in", 4), t.slots("at_qd_in", 4)
        vj_out, sc_out = t.slots("at_vj_out"), t.slots("at_sc_out")
        ones_set, mr_done, xn_done, T_done, T_copied, k_done, z_done, ex_done, phi_done, masked, acc_step = t.sems(
            "at_ones_set", "at_mr_done", "at_xn_done", "at_T_done", "at_T_copied", "at_k_done", "at_z_done",
            "at_ex_done", "at_phi_done", "at_masked", "at_acc_step")
        idx_done, eaT_done, eaT_copied, e_done, vj_done, kj_done, prod_done, sc_done, scT_done, scT_copied = t.sems(
            "at_idx_done", "at_eaT_done", "at_eaT_copied", "at_e_done", "at_vj_done", "at_kj_done",
            "at_prod_done", "at_sc_done", "at_scT_done", "at_scT_copied")

        def edge_tiles(dram, st):
            return unit_rows(dram, st).rearrange("(t p) d -> p t d", p=P)

        with nc.Block() as block:
            @block.sync
            def _(sp):
                def load(st):
                    st.wait_free(sp, eaT_done, slots=4)
                    sp.dma_start(ea[st.slot(4)][:], edge_tiles(A["edge_attr_64"], st)).then_inc(ea_in[st.slot(4)], 16)
                    st.wait_free(sp, xn_done, T, slots=4)
                    sp.dma_start(xt[st.slot(4)][:], unit_rows(A["x"], st).rearrange("(p t) d -> p t d", t=T)
                                 ).then_inc(x_in[st.slot(4)], 16)

                def body(st):
                    if st.static and st.j == 0:
                        load(st)
                        load(st.ahead(1))
                    if st.ahead(2).valid():
                        load(st.ahead(2))
                    mid = st.back(2)
                    if mid.valid():
                        mid.wait(sp, vj_done)
                        if mid.last():
                            mid.back(1).wait_dma(sp, vj_out)
                        sp.dma_start(edge_tiles(K.vj_tab, mid), vj[mid.s][:]).then_inc(vj_out[mid.s], 16)
                    late = st.back(3)
                    if late.valid():
                        late.wait(sp, scT_copied)
                        rows = H * T
                        to = (K.score_tab[late.j * rows:(late.j + 1) * rows, :] if late.static else
                              K.score_tab[bass.ds(late.j * rows, rows), :])
                        sp.dma_start(to, scT[late.s][:]).then_inc(sc_out[late.s], 16)
                sweep(sp, NU, 4, 3, body, cycle=4, reach=2)
                for s in range(2):
                    sp.wait_ge(vj_out[s], 16 * (NU // 2))
                    sp.wait_ge(sc_out[s], 16 * (NU // 2))

            @block.gpsimd
            def _(pool):
                for s in range(4):
                    nc.gpsimd.memset(xn[s][:, :, D:D + 1], 1.0).then_inc(ones_set, 1)

                def gather(st):
                    st.wait(pool, idx_done)
                    st.wait_free(pool, kj_done, slots=4)
                    for n in range(T):
                        nc.gpsimd.indirect_dma_start(
                            out=kv[st.slot(4)][:, n, :], out_offset=None, in_=K.kv_tab[:, :],
                            in_offset=bass.IndirectOffsetOnAxis(ap=idx[st.slot(4)][:, 0, n:n + 1], axis=0),
                            ).then_inc(kv_in[st.slot(4)], 16)
                    st.wait_free(pool, prod_done, slots=4)
                    for n in range(T):
                        nc.gpsimd.indirect_dma_start(
                            out=qd[st.slot(4)][:, n, :], out_offset=None, in_=K.q_tab[:, :],
                            in_offset=bass.IndirectOffsetOnAxis(ap=idx[st.slot(4)][:, 1, n:n + 1], axis=0),
                            ).then_inc(qd_in[st.slot(4)], 16)

                def body(st):
                    if st.valid():
                        gather(st)
                sweep(pool, NU, 2, 0, body, cycle=4, apart=K.pool_waits)

            @block.vector
            def _(dve):
                def index(st):
                    st.wait_dma_free(dve, kv_in, T)
                    st.wait_dma_free(dve, qd_in, T)
                    nc.vector.tensor_copy(idx[st.slot(4)][:, 0, :], K.cols_at(K.src_cols, st.j))
                    nc.vector.tensor_copy(idx[st.slot(4)][:, 1, :], K.cols_at(K.dst_cols, st.j)).then_inc(idx_done, 1)

                def normalise(st):
                    st.wait_free(dve, xn_done, T)
                    nc.vector.tensor_copy(mr[st.s][:].rearrange("p t a -> p (t a)"), K.stat_at(st.j)
                                          ).then_inc(mr_done, 1)
                    st.wait(dve, mr_done)
                    st.wait_dma(dve, x_in)
                    st.wait_free(dve, T_done, slots=4)
                    st.wait_free(dve, acc_step, slots=4)
                    for n in range(T):
                        nc.vector.tensor_scalar(xn[st.slot(4)][:, n, 0:D], xt[st.slot(4)][:, n, :],
                                                mr[st.s][:, n, 0:1], mr[st.s][:, n, 1:2], ALU.mult, ALU.add
                                                ).then_inc(xn_done, 1)

                def add_bias(st, g):
                    dve.wait_ge(k_done, st.j * 2 + g + 1)
                    nc.vector.tensor_tensor(
                        z1[st.s][:, 2 * g:2 * g + 2, :], psK[:],
                        K.b_k1[:].rearrange("p (a d) -> p a d", a=1).to_broadcast([P, 2, D]),
                        ALU.add).then_inc(z_done, 1)

                def body(st):
                    if st.static and st.j == 0:
                        index(st)
                        index(st.ahead(1))
                        normalise(st)
                    if st.ahead(2).valid():
                        index(st.ahead(2))
                    mid = st.back(1)
                    if mid.valid():
                        mid.wait_free(dve, ex_done, 2)
                        mid.wait_free(dve, phi_done, 2)
                        mid.wait(dve, e_done)
                        mid.wait_dma(dve, kv_in, T)
                        mid.wait_dma_free(dve, vj_out)
                        nc.vector.tensor_tensor(vj[mid.s][:], kv[mid.slot(4)][:, :, C:2 * C], psE[:], ALU.add
                                                ).then_inc(vj_done, 1)
                        add_bias(mid, 0)
                        mid.wait(dve, vj_done)
                        nc.vector.tensor_tensor(psE[:], kv[mid.slot(4)][:, :, 0:C], psE[:], ALU.add).then_inc(kj_done, 1)
                    late = st.back(2)
                    if late.valid():
                        late.wait_free(dve, acc_step)
                        for g in range(2):
                            dve.wait_ge(ex_done, late.j * 2 + g + 1)
                            nc.vector.scalar_tensor_tensor(
                                out=phi[late.s][:, 2 * g:2 * g + 2, :], in0=ex[late.s][:, 2 * g:2 * g + 2, :],
                                scalar=1.0, in1=z1[late.s][:, 2 * g:2 * g + 2, :], op0=ALU.min, op1=ALU.max
                                ).then_inc(phi_done, 1)
                        if late.last():
                            late.wait(dve, phi_done, 2)
                            nc.vector.tensor_scalar(phi[late.s][:], phi[late.s][:], K.not_done[:, 0:1], None,
                                                    ALU.mult).then_inc(masked, 1)
                    if mid.valid():
                        add_bias(mid, 1)
                        mid.wait(dve, kj_done)
                        mid.wait_dma(dve, qd_in, T)
                        if not (mid.static and mid.j == 0):
                            dve.wait_ge(sc_done, mid.j)
                        nc.vector.tensor_tensor(prod[:], qd[mid.slot(4)][:], psE[:], ALU.mult).then_inc(prod_done, 1)
                        mid.wait(dve, prod_done)
                        mid.wait_free(dve, scT_done)
                        nc.vector.tensor_reduce(sc[mid.s][:].rearrange("p h t -> p t h"),
                                                prod[:].rearrange("p t (h c) -> p t h c", h=H), AX_X, ALU.add
                                                ).then_inc(sc_done, 1)
                    if st.ahead(1).valid():
                        normalise(st.ahead(1))
                sweep(dve, NU, 4, 2, body, cycle=4)

            @block.tensor
            def _(pe):
                pe.wait_ge(ones_set, 4)

                def body(st):
                    if st.valid():
                        st.wait_dma(pe, ea_in)
                        if not (st.static and st.j == 0):
                            pe.wait_ge(eaT_copied, st.j).then_inc(K.pe_waits, 1)
                        for n in range(T):
                            mm = nc.tensor.transpose(psX[0:R, n * P:(n + 1) * P], ea[st.slot(4)][:, n, :], K.ident[:])
                        mm.then_inc(eaT_done, 1)
                        st.wait(pe, xn_done, T)
                        if not (st.static and st.j == 0):
                            pe.wait_ge(T_copied, st.j * DC)
                        for c in range(DC):
                            for n in range(T):
                                mm = nc.tensor.transpose(psT[c][:, n * P:(n + 1) * P],
                                                         xn[st.slot(4)][:, n, c * P:(c + 1) * P], K.ident[:])
                        mm.then_inc(T_done, 1)
                    mid, late = st.back(1), st.back(3)
                    if mid.valid():
                        mid.wait(pe, eaT_copied)
                        if not (mid.static and mid.j == 0):
                            pe.wait_ge(prod_done, mid.j)
                        for n in range(T):
                            mm = nc.tensor.matmul(psE[:, n, :], eaT[mid.s][:, n * P:(n + 1) * P], K.edgeT[:],
                                                  start=True, stop=True)
                        mm.then_inc(e_done, 1)
                    for g in range(2):
                        if mid.valid():
                            if g == 0:
                                mid.wait(pe, T_copied, DC)
                            if not (mid.static and mid.j == 0 and g == 0):
                                pe.wait_ge(z_done, mid.j * 2 + g)
                            for n in range(2):
                                for c in range(DC):
                                    mm = nc.tensor.matmul(psK[:, n, :],
                                                          xnT[mid.s][:, c, (2 * g + n) * P:(2 * g + n + 1) * P],
                                                          K.mixk[:, c, :], start=(c == 0), stop=(c == DC - 1))
                            mm.then_inc(k_done, 1)
                        if late.valid():
                            if g == 0:
                                late.wait(pe, phi_done, 2)
                                if late.last():
                                    pe.wait_ge(masked, 1)
                            for n in range(2 * g, 2 * g + 2):
                                for c in range(DC):
                                    first = late.static and late.j == 0 and n == 0
                                    mm = nc.tensor.matmul(acc[c][:], phi[late.s][:, n, c * P:(c + 1) * P],
                                                          xn[late.slot(4)][:, n, :], start=first,
                                                          stop=late.last() and n == T - 1, skip_group_check=True)
                            if g == 1:
                                mm.then_inc(acc_step, 1)
                    score = st.back(2)
                    if score.valid():
                        score.wait(pe, sc_done)
                        if not (score.static and score.j == 0):
                            pe.wait_ge(scT_copied, score.j)
                        nc.tensor.transpose(psS[0:H * T, :], sc[score.s][:].rearrange("p h t -> p (h t)"),
                                            K.ident[:]).then_inc(scT_done, 1)
                sweep(pe, NU, 4, 3, body, cycle=4)

            @block.scalar
            def _(act):
                def body(st):
                    if st.valid():
                        st.wait(act, eaT_done)
                        st.wait_free(act, e_done)
                        nc.scalar.copy(eaT[st.s][:], psX[0:R, :]).then_inc(eaT_copied, 1)
                        st.wait(act, T_done)
                        st.wait_free(act, k_done, 2)
                        for c in range(DC):
                            nc.scalar.copy(xnT[st.s][:, c, :], psT[c][:]).then_inc(T_copied, 1)
                    mid = st.back(1)
                    if mid.valid():
                        mid.wait_free(act, phi_done, 2)
                        for g in range(2):
                            act.wait_ge(z_done, mid.j * 2 + g + 1)
                            nc.scalar.activation(ex[mid.s][:, 2 * g:2 * g + 2, :], z1[mid.s][:, 2 * g:2 * g + 2, :],
                                                 ACT.Exp, bias=K.minus_one[:]).then_inc(ex_done, 1)
                    score = st.back(2)
                    if score.valid():
                        score.wait(act, scT_done)
                        score.wait_dma_free(act, sc_out)
                        nc.scalar.copy(scT[score.s][:], psS[0:H * T, :]).then_inc(scT_copied, 1)
                sweep(act, NU, 4, 2, body, cycle=4)
                act.wait_ge(acc_step, NU)
                for c in range(DC):
                    nc.scalar.copy(K.M[:, c, :], acc[c][:])


def softmax(nc, A, K):
    with ExitStack() as ctx:
        t = Tools(nc, ctx)
        score = t.sb("sm_score", [NU, H, U])
        fwd = t.sb("sm_fwd", [NU, H, U])
        whole = t.sb("sm_whole", [NU, H, U])
        prob = t.sb("sm_prob", [NU, H, U])
        wgt = t.sb("sm_wgt", [NU, H + 1, U])
        hand = t.sb("sm_hand", [NU, 2, H])
        behind = t.sb("sm_behind", [NU, H])
        chain = t.sb("sm_chain", [H, 2, NU])
        carry = t.sb("sm_carry", [H, NU + 2])
        start = t.sb("sm_start", [NU, H])
        psX = t.psum("sm_psX", [P, P])
        psY = t.psum("sm_psY", [P, P])
        psZ = t.psum("sm_psZ", [P, P])
        score_in, wgt_out, vec, hand_ready, turned, carry_ready, turned_back, shifted, prob_ready, wgt_ready = t.sems(
            "sm_score_in", "sm_wgt_out", "sm_vec", "sm_hand_ready", "sm_turned", "sm_carry_ready",
            "sm_turned_back", "sm_shifted", "sm_prob_ready", "sm_wgt_ready")
        BEFORE = U - DUP
        scans = [("on", ALU.add, ALU.max, -BIG), ("back", ALU.add, ALU.max, -BIG),
                 ("on", ALU.mult, ALU.add, 0.0), ("back", ALU.add, ALU.max, -BIG)]

        with nc.Block() as block:
            @block.sync
            def _(sp):
                sp.dma_start(score[:].rearrange("u h e -> u (h e)"),
                             K.score_tab.rearrange("(u r) e -> u (r e)", r=H * T)).then_inc(score_in, 16)
                sp.wait_ge(wgt_ready, 1)
                sp.dma_start(K.wgt_tab.rearrange("(u r) e -> u (r e)", r=H + 1),
                             wgt[:].rearrange("u h e -> u (h e)")).then_inc(wgt_out, 16)
                sp.wait_ge(wgt_out, 16)

            @block.vector
            def _(dve):
                count = [0]

                def chained(ins):
                    ins.then_inc(vec, 1)
                    count[0] += 1
                    dve.wait_ge(vec, count[0])

                def scan_units(n, way, op0, op1, empty, frm, to):
                    gates = K.pen if op0 == ALU.add else K.same
                    along = slice(None) if way == "on" else slice(None, None, -1)
                    gate = gates[:, 0:U] if way == "on" else gates[:, 1:U + 1]
                    end = U - 1 if way == "on" else 0
                    for h in range(H):
                        ins = nc.vector.tensor_tensor_scan(to[:, h, along], gate[:, along], frm[:, h, along],
                                                           empty, op0, op1)
                    chained(ins)
                    chained(nc.vector.tensor_copy(hand[:, 0, :], to[:, :, end]))
                    chained(nc.vector.tensor_reduce(hand[:, 1, 0:1], gate, AX_X, ALU.min))
                    if way == "on":
                        u = NU - 2
                        chained(nc.vector.tensor_copy(hand[u:u + 1, 0, :], to[u:u + 1, :, BEFORE - 1]))
                        chained(nc.vector.tensor_reduce(hand[u:u + 1, 1, 0:1], gate[u:u + 1, 0:BEFORE], AX_X, ALU.min))
                    else:
                        chained(nc.vector.tensor_scalar(behind[:], to[:, :, DUP], K.last_unit[0:NU, 0:1], None,
                                                        ALU.mult))
                        chained(nc.vector.scalar_tensor_tensor(
                            out=hand[:, 0, :], in0=hand[:, 0, :], scalar=K.last_unit[0:NU, 1:2],
                            in1=behind[:], op0=ALU.mult, op1=ALU.add))
                    nc.vector.tensor_copy(hand[:, 1, 1:H], hand[:, 1, 0:1].to_broadcast([NU, H - 1])
                                          ).then_inc(hand_ready, 1)
                    dve.wait_ge(turned, n + 1)
                    nc.vector.memset(carry[:], empty)
                    nc.vector.tensor_copy(chain[:, 0, :], psX[0:H, 0:NU])
                    chained(nc.vector.tensor_copy(chain[:, 1, :], psY[0:H, 0:NU]))
                    nc.vector.tensor_tensor_scan(carry[:, 1:NU + 1][:, along], chain[:, 1, along],
                                                 chain[:, 0, along], empty, op0, op1).then_inc(carry_ready, 1)
                    dve.wait_ge(turned_back, n + 1)
                    chained(nc.vector.tensor_copy(start[:], psZ[0:NU, 0:H]))
                    for h in range(H):
                        ins = nc.vector.tensor_tensor_scan(to[:, h, along], gate[:, along], frm[:, h, along],
                                                           start[:, h:h + 1], op0, op1)
                    chained(ins)

                dve.wait_ge(score_in, 16)
                scan_units(0, *scans[0], score, fwd)
                scan_units(1, *scans[1], fwd, whole)
                nc.vector.tensor_tensor(score[:], score[:], whole[:], ALU.subtract).then_inc(shifted, 1)
                dve.wait_ge(prob_ready, 1)
                scan_units(2, *scans[2], prob, fwd)
                scan_units(3, *scans[3], fwd, whole)
                chained(nc.vector.tensor_scalar(whole[:], whole[:], 1e-16, None, ALU.add))
                chained(nc.vector.reciprocal(whole[:], whole[:]))
                nc.vector.tensor_tensor(wgt[:, 0:H, :], prob[:], whole[:], ALU.mult)
                nc.vector.tensor_copy(wgt[:, H, :], K.same[:, 0:U]).then_inc(wgt_ready, 1)

            @block.scalar
            def _(act):
                act.wait_ge(shifted, 1)
                nc.scalar.activation(prob[:].rearrange("u h e -> u (h e)"), score[:].rearrange("u h e -> u (h e)"),
                                     ACT.Exp, scale=SCALE).then_inc(prob_ready, 1)

            @block.tensor
            def _(pe):
                for n, (way, *_) in enumerate(scans):
                    pe.wait_ge(hand_ready, n + 1)
                    nc.tensor.transpose(psX[0:H, 0:NU], hand[:, 0, :], K.ident[0:NU, 0:NU])
                    nc.tensor.transpose(psY[0:H, 0:NU], hand[:, 1, :], K.ident[0:NU, 0:NU]).then_inc(turned, 1)
                    pe.wait_ge(carry_ready, n + 1)
                    frm = carry[:, 0:NU] if way == "on" else carry[:, 2:NU + 2]
                    nc.tensor.transpose(psZ[0:NU, 0:H], frm, K.ident[0:H, 0:H]).then_inc(turned_back, 1)


def readout(nc, A, K):
    with ExitStack() as ctx:
        t = Tools(nc, ctx)
        MT = t.sb("ro_MT", [P, DC, D])
        kvm = t.sb("ro_kvm", [P, DC, P])
        kvT = t.sb("ro_kvT", [P, DC, P])
        ks = t.sb("ro_ks", [P, DC, P])
        psT = [t.psum(f"ro_psT{c}", [P, D]) for c in range(DC)]
        psV = t.psum("ro_psV", [P, DC, P])
        psKT = t.psum("ro_psKT", [P, DC, P])
        psS = t.psum("ro_psS", [P, DC, P])
        psG = t.psum("ro_psG", [P, DC, D])
        m_turned, m_copied, kv_done, ks_ready, vec, kvm_ready, kv_turned, kv_copied, g_done, ks_turned = t.sems(
            "ro_m_turned", "ro_m_copied", "ro_kv_done", "ro_ks_ready", "ro_vec", "ro_kvm_ready", "ro_kv_turned",
            "ro_kv_copied", "ro_g_done", "ro_ks_turned")
        with nc.Block() as block:
            @block.tensor
            def _(pe):
                for x in range(DC):
                    for d in range(DC):
                        mm = nc.tensor.transpose(psT[x][:, d * P:(d + 1) * P], K.M[:, d, x * P:(x + 1) * P], K.ident[:])
                mm.then_inc(m_turned, 1)
                pe.wait_ge(m_copied, DC)
                for d in range(DC):
                    for x in range(DC):
                        mm = nc.tensor.matmul(psV[:, d, :], MT[:, x, d * P:(d + 1) * P],
                                              K.mixv[:, x, d * P:(d + 1) * P], start=(x == 0), stop=(x == DC - 1))
                mm.then_inc(kv_done, 1)
                pe.wait_ge(ks_ready, 1)
                for d in range(DC):
                    mm = nc.tensor.transpose(psS[:, d, :], ks[:, d, :], K.ident[:])
                mm.then_inc(ks_turned, 1)
                pe.wait_ge(kvm_ready, 1)
                for d in range(DC):
                    mm = nc.tensor.transpose(psKT[:, d, :], kvm[:, d, :], K.ident[:])
                mm.then_inc(kv_turned, 1)
                pe.wait_ge(kv_copied, 1)
                for d in range(DC):
                    mm = nc.tensor.matmul(psG[:, d, :], kvT[:, d, :], K.mixo[:, d, :], start=True, stop=True)
                mm.then_inc(g_done, 1)

            @block.scalar
            def _(act):
                act.wait_ge(m_turned, 1)
                for x in range(DC):
                    nc.scalar.copy(MT[:, x, :], psT[x][:]).then_inc(m_copied, 1)
                act.wait_ge(kv_turned, 1)
                nc.scalar.copy(kvT[:], psKT[:]).then_inc(kv_copied, 1)
                act.wait_ge(g_done, 1)
                nc.scalar.copy(K.G[:], psG[:])

            @block.vector
            def _(dve):
                for d in range(DC):
                    ins = nc.vector.tensor_copy(ks[:, d, :], K.M[:, d, D:D + 1].to_broadcast([P, P]))
                ins.then_inc(ks_ready, 1)
                dve.wait_ge(kv_done, 1)
                for d in range(DC):
                    ins = nc.vector.scalar_tensor_tensor(out=kvm[:, d, :], in0=K.b_v[:, d * P:(d + 1) * P],
                                                         scalar=K.M[:, d, D:D + 1], in1=psV[:, d, :],
                                                         op0=ALU.mult, op1=ALU.add)
                ins.then_inc(vec, 1)
                dve.wait_ge(vec, 1)
                for d in range(DC):
                    ins = nc.vector.tensor_tensor(kvm[:, d, :], kvm[:, d, :], K.head_mask[:], ALU.mult)
                ins.then_inc(kvm_ready, 1)
                dve.wait_ge(ks_turned, 1)
                nc.vector.tensor_copy(K.ksum[:], psS[:].rearrange("p c d -> p (c d)"))


def aggregate(nc, A, K):
    with ExitStack() as ctx:
        t = Tools(nc, ctx)
        vj = [t.sb(f"ag_vj{s}", [P, T, C]) for s in range(4)]
        wg = [t.sb(f"ag_wg{s}", [H + 1, U]) for s in range(4)]
        vT = [t.sb(f"ag_vT{s}", [P, U]) for s in range(2)]
        msg = [t.sb(f"ag_msg{s}", [P, U]) for s in range(2)]
        run = [t.sb(f"ag_run{s}", [P, U]) for s in range(2)]
        rows = [t.sb(f"ag_rows{s}", [P, T, C]) for s in range(4)]
        idx = [t.sb(f"ag_idx{s}", [P, T], I32) for s in range(4)]
        psV = [t.psum(f"ag_psV{s}", [P, U]) for s in range(2)]
        psW = [t.psum(f"ag_psW{s}", [P, U]) for s in range(2)]
        psG = [t.psum(f"ag_psG{s}", [P, U]) for s in range(2)]
        psR = [t.psum(f"ag_psR{s}", [P, T, C]) for s in range(2)]
        vj_in, wg_in, rows_out = t.slots("ag_vj_in", 4), t.slots("ag_wg_in", 4), t.slots("ag_rows_out", 4)
        v_turned, v_copied, w_spread, msg_done, run_done, run_turned, rows_done, idx_done = t.sems(
            "ag_v_turned", "ag_v_copied", "ag_w_spread", "ag_msg_done", "ag_run_done", "ag_run_turned",
            "ag_rows_done", "ag_idx_done")

        with nc.Block() as block:
            @block.sync
            def _(sp):
                def body(st):
                    st.wait_free(sp, v_turned, slots=4)
                    sp.dma_start(vj[st.slot(4)][:], unit_rows(K.vj_tab, st).rearrange("(t p) d -> p t d", p=P)
                                 ).then_inc(vj_in[st.slot(4)], 16)
                    st.wait_free(sp, w_spread, slots=4)
                    n = H + 1
                    frm = (K.wgt_tab[st.j * n:(st.j + 1) * n, :] if st.static else
                           K.wgt_tab[bass.ds(st.j * n, n), :])
                    sp.dma_start(wg[st.slot(4)][:], frm).then_inc(wg_in[st.slot(4)], 16)
                sweep(sp, NU, 2, 0, body, cycle=4)

            @block.tensor
            def _(pe):
                def body(st):
                    if st.valid():
                        st.wait_dma(pe, vj_in)
                        st.wait_free(pe, v_copied)
                        for n in range(T):
                            mm = nc.tensor.transpose(psV[st.s][:, n * P:(n + 1) * P], vj[st.slot(4)][:, n, :], K.ident[:])
                        mm.then_inc(v_turned, 1)
                        st.wait_dma(pe, wg_in)
                        st.wait_free(pe, run_done)
                        nc.tensor.matmul(psW[st.s][:], K.sel_w[:], wg[st.slot(4)][:], start=True, stop=True)
                        nc.tensor.matmul(psG[st.s][:], K.sel_m[:], wg[st.slot(4)][:], start=True, stop=True
                                         ).then_inc(w_spread, 1)
                    late = st.back(2)
                    if late.valid():
                        late.wait(pe, run_done)
                        late.wait_free(pe, rows_done)
                        for n in range(T):
                            mm = nc.tensor.transpose(psR[late.s][:, n, :], run[late.s][:, n * P:(n + 1) * P], K.ident[:])
                        mm.then_inc(run_turned, 1)
                sweep(pe, NU, 4, 2, body, cycle=4)

            @block.scalar
            def _(act):
                def body(st):
                    if st.valid():
                        st.wait(act, v_turned)
                        st.wait_free(act, msg_done)
                        nc.scalar.copy(vT[st.s][:], psV[st.s][:]).then_inc(v_copied, 1)
                    late = st.back(2)
                    if late.valid():
                        late.wait(act, run_turned)
                        late.wait_dma_free(act, rows_out, T)
                        nc.scalar.copy(rows[late.slot(4)][:], psR[late.s][:]).then_inc(rows_done, 1)
                sweep(act, NU, 4, 2, body, cycle=4)

            @block.vector
            def _(dve):
                def body(st):
                    if st.valid():
                        st.wait_dma_free(dve, rows_out, T)
                        nc.vector.tensor_copy(idx[st.slot(4)][:], K.cols_at(K.row_cols, st.j)).then_inc(idx_done, 1)
                        st.wait(dve, v_copied)
                        st.wait(dve, w_spread)
                        st.wait_free(dve, run_done)
                        nc.vector.tensor_tensor(msg[st.s][:], vT[st.s][:], psW[st.s][:], ALU.mult).then_inc(msg_done, 1)
                    mid = st.back(1)
                    if mid.valid():
                        mid.wait(dve, msg_done)
                        mid.wait_free(dve, run_turned)
                        if mid.static and mid.j == 0:
                            first = 0.0
                        else:
                            dve.wait_ge(run_done, mid.j)
                            col = U - DUP if mid.last() else U
                            first = run[1 - mid.s][:, col - 1:col]
                        nc.vector.tensor_tensor_scan(run[mid.s][:], psG[mid.s][:], msg[mid.s][:], first,
                                                     ALU.mult, ALU.add).then_inc(run_done, 1)
                sweep(dve, NU, 4, 1, body, cycle=4)

            @block.gpsimd
            def _(pool):
                def body(st):
                    st.wait(pool, rows_done)
                    st.wait(pool, idx_done)
                    if st.last():
                        st.back(1).wait_dma(pool, rows_out, T)
                    for n in range(T):
                        nc.gpsimd.indirect_dma_start(
                            out=K.agg_tab[:, :], out_offset=bass.IndirectOffsetOnAxis(ap=idx[st.slot(4)][:, n:n + 1], axis=0),
                            in_=rows[st.slot(4)][:, n, :], in_offset=None, bounds_check=N - 1, oob_is_err=False,
                            ).then_inc(rows_out[st.slot(4)], 16)
                sweep(pool, NU, 2, 0, body, cycle=4, apart=K.pool_waits)
                for s in range(4):
                    pool.wait_ge(rows_out[s], 16 * T * len(range(s, NU, 4)))


def combine(nc, A, K):
    HT = 2
    with ExitStack() as ctx:
        t = Tools(nc, ctx)

        def two(name, shape, dt=F32):
            return [t.sb(f"cb_{name}{s}", shape, dt) for s in range(2)]

        xt = [t.sb(f"cb_x{s}", [P, HT, D]) for s in range(6)]
        ax = [t.sb(f"cb_ax{s}", [P, HT, 2, C]) for s in range(6)]
        mr, xn = two("mr", [P, HT * 2]), two("xn", [P, HT, D])
        xnT = two("xnT", [P, DC, HT * P])
        ex, pk, qn, qnT = two("ex", [P, HT, D]), two("pk", [P, HT, D]), two("qn", [P, HT, D]), two("qnT", [P, DC, HT * P])
        nrm, rn = two("nrm", [P, HT, MH]), two("rn", [P, HT, MH])
        gp, gs, ge, beta = two("gp", [P, HT, 2 * C]), two("gs", [P, HT]), two("ge", [P, HT]), two("beta", [P, HT])
        dif, o, oT = two("dif", [P, HT, C]), two("o", [P, HT, C]), two("oT", [P, HT * P])
        x1 = [t.sb(f"cb_x1{s}", [P, HT, D]) for s in range(3)]
        bn, mv, ve, sh = two("bn", [P, HT, 6]), two("mv", [P, HT, 2]), two("ve", [P, HT]), two("sh", [P, HT])
        rs, xm, xmT, y = two("rs", [P, HT]), two("xm", [P, HT, D]), two("xmT", [P, DC, HT * P]), two("y", [P, HT, D])
        psT = t.psum("cb_psT", [P, DC, HT * P])
        psQ = [t.psum(f"cb_psQ{s}", [P, HT, D]) for s in range(2)]
        psN = t.psum("cb_psN", [P, DC, HT * P])
        psO = t.psum("cb_psO", [P, HT * P])
        psF = t.psum("cb_psF", [P, HT, D])
        psM = t.psum("cb_psM", [P, DC, HT * P])
        psY = t.psum("cb_psY", [P, HT, D])
        x_in, ax_in, y_out = t.slots("cb_x_in", 6), t.slots("cb_ax_in", 6), t.slots("cb_y_out")
        names = ("mr xn T Tc q ex phi pk nrm nre rn qn N Nc gs ge gb beta dif o O Oc F x1 bn mv ve rs sh xm "
                 "M Mc Y y").split()
        S = {n: t.sem("cb_" + n) for n in names}

        with nc.Block() as block:
            @block.sync
            def _(sp):
                def load(st):
                    slot = st.slot(6)
                    st.wait_free(sp, S["x1"], slots=6)
                    sp.dma_start(xt[slot][:], half_rows(A["x"], st)).then_inc(x_in[slot], 16)
                    st.wait_free(sp, S["gs"], HT, slots=6)
                    st.wait_free(sp, S["o"], HT, slots=6)
                    sp.dma_start(ax[slot][:, :, 0, :], half_rows(K.agg_tab, st)).then_inc(ax_in[slot], 16)
                    sp.dma_start(ax[slot][:, :, 1, :], half_rows(K.skip_tab, st)).then_inc(ax_in[slot], 16)

                def body(st):
                    if st.static and st.j == 0:
                        load(st)
                        load(st.ahead(1))
                    if st.ahead(2).valid():
                        load(st.ahead(2))
                    done = st.back(5)
                    if done.valid():
                        done.wait(sp, S["y"])
                        if done.static and half_unit(done) == NU - 1:
                            done.back(1).wait_dma(sp, y_out)
                            done.back(2).wait_dma(sp, y_out)
                        sp.dma_start(half_rows(K.out, done), y[done.s][:]).then_inc(y_out[done.s], 16)
                sweep(sp, 2 * NU, 8, 5, body, cycle=6, apart=K.sp_waits)
                for s in range(2):
                    sp.wait_ge(y_out[s], 16 * NU)

            @block.gpsimd
            def _(pool):
                def stat(st):
                    st.wait_free(pool, S["xn"], HT)
                    nc.gpsimd.tensor_copy(mr[st.s][:], K.stat_half(st)).then_inc(S["mr"], 1)

                def body(st):
                    if st.static and st.j == 0:
                        stat(st)
                    if st.ahead(1).valid():
                        stat(st.ahead(1))
                    d = st.back(3)
                    if d.valid():
                        d.wait(pool, S["mv"], HT)
                        nc.gpsimd.tensor_scalar(ve[d.s][:], mv[d.s][:, :, 1], EPS, None, ALU.add).then_inc(S["ve"], 1)
                        d.wait(pool, S["ve"])
                        d.wait_free(pool, S["xm"], HT)
                        d.wait_free(pool, S["sh"])
                        nc.gpsimd.tensor_tensor(rs[d.s][:], ve[d.s][:], K.neg_half[:, 0:HT], ALU.pow
                                                ).then_inc(S["rs"], 1)
                    if st.valid():
                        st.wait_dma(pool, ax_in, 2)
                        st.wait_free(pool, S["o"], HT)
                        nc.gpsimd.tensor_tensor(dif[st.s][:], ax[st.slot(6)][:, :, 1, :], ax[st.slot(6)][:, :, 0, :],
                                                ALU.subtract).then_inc(S["dif"], 1)
                sweep(pool, 2 * NU, 6, 3, body, cycle=6, apart=K.pool_waits)

            @block.vector
            def _(dve):
                def rowwise(tile, shape):
                    return tile.rearrange("p (a d) -> p a d", a=1).to_broadcast(shape)

                def body(st):
                    a = st.back(1)
                    d = st.back(3)
                    e = st.back(5)
                    if a.valid():
                        a.wait_dma(dve, ax_in, 2)
                        a.wait_free(dve, S["ge"])
                        for n in range(HT):
                            nc.vector.tensor_tensor_reduce(
                                out=gp[a.s][:, n, :], in0=ax[a.slot(6)][:, n, :, :].rearrange("p a c -> p (a c)"),
                                in1=K.gate_w[:].rearrange("p a c -> p (a c)"), scale=1.0, scalar=0.0,
                                op0=ALU.mult, op1=ALU.add, accum_out=gs[a.s][:, n:n + 1]).then_inc(S["gs"], 1)
                    if d.valid():
                        d.wait(dve, S["F"])
                        d.wait_free(dve, S["y"], slots=3)
                        d.wait_free(dve, S["xm"], HT, slots=3)
                        nc.vector.tensor_tensor(x1[d.slot(3)][:], xt[d.slot(6)][:], psF[:], ALU.add).then_inc(S["x1"], 1)
                    if a.valid():
                        a.wait(dve, S["ex"])
                        nc.vector.scalar_tensor_tensor(out=psQ[a.s][:], in0=ex[a.s][:], scalar=1.0, in1=psQ[a.s][:],
                                                       op0=ALU.min, op1=ALU.max).then_inc(S["phi"], 1)
                    if d.valid():
                        d.wait(dve, S["x1"])
                        for n in range(HT):
                            nc.vector.bn_stats(bn[d.s][:, n, :], x1[d.slot(3)][:, n, :]).then_inc(S["bn"], 1)
                    if a.valid():
                        a.wait(dve, S["phi"])
                        nc.vector.tensor_tensor(pk[a.s][:], psQ[a.s][:], rowwise(K.ksum[:], [P, HT, D]), ALU.mult
                                                ).then_inc(S["pk"], 1)
                    if d.valid():
                        d.wait_free(dve, S["ve"])
                        d.wait_free(dve, S["sh"])
                        dve.wait_ge(S["bn"], (d.j + 1) * HT).then_inc(K.dve_waits, 1)
                        for n in range(HT):
                            nc.vector.bn_aggr(mv[d.s][:, n, :], bn[d.s][:, n, :]).then_inc(S["mv"], 1)
                    if a.valid():
                        a.wait(dve, S["pk"])
                        nc.vector.tensor_reduce(nrm[a.s][:], pk[a.s][:].rearrange("p t (h d) -> p t h d", h=MH),
                                                AX_X, ALU.add).then_inc(S["nrm"], 1)
                        a.wait(dve, S["ge"])
                        nc.vector.tensor_scalar(ge[a.s][:], ge[a.s][:], 1.0, None, ALU.add).then_inc(S["gb"], 1)
                        a.wait(dve, S["nrm"])
                        nc.vector.tensor_scalar(nrm[a.s][:], nrm[a.s][:], 1e-6, None, ALU.add).then_inc(S["nre"], 1)
                        a.wait(dve, S["gb"])
                        nc.vector.reciprocal(beta[a.s][:], ge[a.s][:]).then_inc(S["beta"], 1)
                        a.wait(dve, S["nre"])
                        nc.vector.reciprocal(rn[a.s][:], nrm[a.s][:]).then_inc(S["rn"], 1)
                        a.wait(dve, S["beta"])
                        a.wait(dve, S["dif"])
                        a.wait_free(dve, S["O"])
                        for n in range(HT):
                            nc.vector.scalar_tensor_tensor(out=o[a.s][:, n, :], in0=dif[a.s][:, n, :],
                                                           scalar=beta[a.s][:, n:n + 1], in1=ax[a.slot(6)][:, n, 0, :],
                                                           op0=ALU.mult, op1=ALU.add).then_inc(S["o"], 1)
                        a.wait(dve, S["rn"])
                        a.wait_free(dve, S["N"])
                        nc.vector.tensor_tensor(qn[a.s][:].rearrange("p t (h d) -> p t h d", h=MH),
                                                psQ[a.s][:].rearrange("p t (h d) -> p t h d", h=MH),
                                                rn[a.s][:].rearrange("p t (h a) -> p t h a", a=1)
                                                .to_broadcast([P, HT, MH, MC]), ALU.mult).then_inc(S["qn"], 1)
                    if d.valid():
                        d.wait(dve, S["rs"])
                        d.wait_free(dve, S["xm"], HT)
                        nc.vector.scalar_tensor_tensor(out=sh[d.s][:], in0=mv[d.s][:, :, 0], scalar=-1.0,
                                                       in1=rs[d.s][:], op0=ALU.mult, op1=ALU.mult
                                                       ).then_inc(S["sh"], 1)
                    if e.valid():
                        e.wait(dve, S["Y"])
                        e.wait_dma_free(dve, y_out)
                        nc.vector.tensor_tensor(y[e.s][:], x1[e.slot(3)][:], psY[:], ALU.add).then_inc(S["y"], 1)
                sweep(dve, 2 * NU, 8, 5, body, cycle=6)

            @block.tensor
            def _(pe):
                def turn(ps, tile, st):
                    for c in range(DC):
                        for n in range(HT):
                            mm = nc.tensor.transpose(ps[:, c, n * P:(n + 1) * P], tile[:, n, c * P:(c + 1) * P],
                                                     K.ident[:])
                    return mm

                def bias(to, row):
                    nc.tensor.matmul(to, K.ones3[:], K.b_parts[:, row, :], start=True, stop=False)

                def not_first(st):
                    return not (st.static and st.j == 0)

                def body(st):
                    if st.valid():
                        st.wait(pe, S["xn"], HT)
                        if not_first(st):
                            pe.wait_ge(S["Tc"], st.j)
                        turn(psT, xn[st.s], st).then_inc(S["T"], 1)
                    e = st.back(4)
                    if e.valid():
                        e.wait(pe, S["xm"], HT)
                        if not_first(e):
                            pe.wait_ge(S["Mc"], e.j)
                        turn(psM, xm[e.s], e).then_inc(S["M"], 1)
                    b = st.back(2)
                    if b.valid():
                        b.wait(pe, S["qn"])
                        if not_first(b):
                            pe.wait_ge(S["Nc"], b.j)
                        turn(psN, qn[b.s], b).then_inc(S["N"], 1)
                        b.wait(pe, S["o"], HT)
                        if not_first(b):
                            pe.wait_ge(S["Oc"], b.j)
                        for n in range(HT):
                            mm = nc.tensor.transpose(psO[:, n * P:(n + 1) * P], o[b.s][:, n, :], K.ident[:])
                        mm.then_inc(S["O"], 1)
                    if st.valid():
                        st.wait(pe, S["Tc"])
                        st.wait_free(pe, S["qn"])
                        for n in range(HT):
                            bias(psQ[st.s][:, n, :], 0)
                            for c in range(DC):
                                mm = nc.tensor.matmul(psQ[st.s][:, n, :], xnT[st.s][:, c, n * P:(n + 1) * P],
                                                      K.mixq[:, c, :], start=False, stop=(c == DC - 1))
                        mm.then_inc(S["q"], 1)
                    if b.valid():
                        b.wait(pe, S["Nc"])
                        b.wait(pe, S["Oc"])
                        if not_first(b):
                            pe.wait_ge(S["x1"], b.j)
                        for n in range(HT):
                            bias(psF[:, n, :], 1)
                            for c in range(DC):
                                nc.tensor.matmul(psF[:, n, :], qnT[b.s][:, c, n * P:(n + 1) * P], K.G[:, c, :],
                                                 start=False, stop=False)
                            mm = nc.tensor.matmul(psF[:, n, :], oT[b.s][:, n * P:(n + 1) * P], K.m2nT[:],
                                                  start=False, stop=True)
                        mm.then_inc(S["F"], 1)
                    if e.valid():
                        e.wait(pe, S["Mc"])
                        if not_first(e):
                            pe.wait_ge(S["y"], e.j)
                        for n in range(HT):
                            bias(psY[:, n, :], 2)
                            for c in range(DC):
                                mm = nc.tensor.matmul(psY[:, n, :], xmT[e.s][:, c, n * P:(n + 1) * P],
                                                      K.ffnT[:, c, :], start=False, stop=(c == DC - 1))
                        mm.then_inc(S["Y"], 1)
                sweep(pe, 2 * NU, 6, 4, body, cycle=6)

            @block.scalar
            def _(act):
                def normalise(st):
                    st.wait_dma(act, x_in)
                    st.wait(act, S["mr"])
                    st.wait_free(act, S["T"])
                    for n in range(HT):
                        nc.scalar.activation(xn[st.s][:, n, :], xt[st.slot(6)][:, n, :], ACT.Identity,
                                             scale=mr[st.s][:, 2 * n:2 * n + 1], bias=mr[st.s][:, 2 * n + 1:2 * n + 2]
                                             ).then_inc(S["xn"], 1)

                def body(st):
                    a, b, d, e = st.back(1), st.back(2), st.back(3), st.back(4)
                    if st.static and st.j == 0:
                        normalise(st)
                    if st.valid():
                        st.wait(act, S["T"])
                        st.wait_free(act, S["q"])
                        nc.scalar.copy(xnT[st.s][:], psT[:]).then_inc(S["Tc"], 1)
                    if e.valid():
                        e.wait(act, S["M"])
                        e.wait_free(act, S["Y"])
                        nc.scalar.copy(xmT[e.s][:], psM[:]).then_inc(S["Mc"], 1)
                    if b.valid():
                        b.wait(act, S["N"])
                        b.wait_free(act, S["F"])
                        nc.scalar.copy(qnT[b.s][:], psN[:]).then_inc(S["Nc"], 1)
                        b.wait(act, S["O"])
                        nc.scalar.copy(oT[b.s][:], psO[:]).then_inc(S["Oc"], 1)
                    if a.valid():
                        a.wait(act, S["q"])
                        a.wait_free(act, S["phi"])
                        nc.scalar.activation(ex[a.s][:], psQ[a.s][:], ACT.Exp, bias=K.minus_one[:]).then_inc(S["ex"], 1)
                        a.wait(act, S["gs"], HT)
                        a.wait_free(act, S["beta"])
                        nc.scalar.activation(ge[a.s][:], gs[a.s][:], ACT.Exp, scale=-1.0).then_inc(S["ge"], 1)
                    if st.ahead(1).valid():
                        normalise(st.ahead(1))
                    if d.valid():
                        d.wait(act, S["rs"])
                        d.wait(act, S["sh"])
                        d.wait_free(act, S["M"])
                        for n in range(HT):
                            nc.scalar.activation(xm[d.s][:, n, :], x1[d.slot(3)][:, n, :], ACT.Identity,
                                                 scale=rs[d.s][:, n:n + 1], bias=sh[d.s][:, n:n + 1]
                                                 ).then_inc(S["xm"], 1)
                sweep(act, 2 * NU, 6, 4, body, cycle=6)


class Kept:

    def __init__(self, nc, ctx, out):
        t = Tools(nc, ctx)
        self.out = out
        self.pool_waits, self.dve_waits, self.pe_waits, self.sp_waits = t.sems(
            "pool_waits", "dve_waits", "pe_waits", "sp_waits")

        def dram(name, shape):
            return nc.dram_tensor(name, shape, F32).ap()

        self.kv_tab, self.q_tab, self.skip_tab = dram("kv_tab", (N, 2 * C)), dram("q_tab", (N, C)), dram("skip_tab", (N, C))
        self.vj_tab, self.agg_tab = dram("vj_tab", (E, C)), dram("agg_tab", (N, C))
        self.score_tab, self.wgt_tab = dram("score_tab", (NU * H * T, P)), dram("wgt_tab", (NU * (H + 1), U))
        self.ident = t.sb("ident", [P, P])
        self.neg_half = t.sb("neg_half", [P, T])
        self.minus_one = t.sb("minus_one", [P, 1])
        self.head_mask = t.sb("head_mask", [P, P])
        self.sel_w = t.sb("sel_w", [H + 1, C])
        self.sel_m = t.sb("sel_m", [H + 1, C])
        self.not_done = t.sb("not_done", [P, 1])
        self.last_unit = t.sb("last_unit", [P, 2])
        self.mixq, self.mixk, self.mixv, self.mixo = [t.sb(n, [P, DC, D]) for n in ("mixq", "mixk", "mixv", "mixo")]
        self.b_kvqs = t.sb("b_kvqs", [P, 4 * C])
        self.b_k1, self.b_v = [t.sb(n, [P, D]) for n in ("b_k1", "b_v")]
        self.b_parts = t.sb("b_parts", [3, 3, D], BF16)
        self.ones3 = t.sb("ones3", [3, P], BF16)
        self.kvqsT = t.sb("kvqsT", [P, 4 * C])
        self.n2mT = t.sb("n2mT", [P, DC, C])
        self.m2nT = t.sb("m2nT", [P, D])
        self.ffnT = t.sb("ffnT", [P, DC, D])
        self.edgeT = t.sb("edgeT", [R, C])
        self.gate_w = t.sb("gate_w", [P, 2, C])
        self.src_cols, self.dst_cols, self.row_cols = [t.sb(n, [P, NU, T], I32) for n in ("src_cols", "dst_cols", "row_cols")]
        self.same = t.sb("same", [NU, U + 1])
        self.pen = t.sb("pen", [NU, U + 1])
        self.stat = t.sb("stat", [P, NU, T * 2])
        self.M = t.sb("M", [P, DC, D + 1])
        self.G = t.sb("G", [P, DC, D])
        self.ksum = t.sb("ksum", [P, D])

    def stat_at(self, j):
        if isinstance(j, int):
            return self.stat[:, j, :]
        return self.stat[:, bass.ds(j, 1), :].rearrange("p a b -> p (a b)")

    def stat_half(self, st):
        half = slice(st.s * T, (st.s + 1) * T)
        if st.static:
            return self.stat[:, half_unit(st), half]
        return self.stat[:, bass.ds(half_unit(st), 1), half].rearrange("p a b -> p (a b)")

    def cols_at(self, cols, j):
        if isinstance(j, int):
            return cols[:, j, :]
        return cols[:, bass.ds(j, 1), :].rearrange("p a b -> p (a b)")


STAGES = [setup, project, attend, softmax, readout, aggregate, combine]


def build(nc, A, out):
    with ExitStack() as ctx:
        K = Kept(nc, ctx, out)
        for stage in STAGES:
            stage(nc, A, K)


def kernel(**inputs):
    import numpy as _np
    import concourse.bacc as _bacc
    from concourse import mybir as _mybir
    from concourse.bass_utils import run_bass_kernel_spmd as _run

    nc = _bacc.Bacc("TRN2", target_bir_lowering=False, num_devices=1)
    arrays, args = {}, {}
    for name, a in inputs.items():
        a = _np.ascontiguousarray(a)
        arrays[f"in_{name}_dram"] = a
        args[name] = nc.dram_tensor(f"in_{name}_dram", a.shape, _mybir.dt.from_np(a.dtype), kind="ExternalInput").ap()
    out = nc.dram_tensor("out_0_dram", (N, D), F32, kind="ExternalOutput").ap()
    build(nc, args, out)
    r = _run(nc, [arrays], core_ids=[0])
    return r.results[0]["out_0_dram"]
```

```python
from contextlib import ExitStack

import concourse.bass as bass
from concourse import mybir

F32 = mybir.dt.float32
F32R = mybir.dt.float32r
BF16 = mybir.dt.bfloat16
I32 = mybir.dt.int32
ALU = mybir.AluOpType
ACT = mybir.ActivationFunctionType
AX_X = mybir.AxisListType.X

P = 128
N, D = 50000, 256
E, R = 50000, 64
C, H = 128, 4
HC = C // H
MH = 8
MC = D // MH
DC = D // P
T = 4
U = T * P
NU = -(-N // U)
LAST = N - U
DUP = (NU - 1) * U - LAST
EPS = 1e-5
BIG = 1e30
SCALE = float(HC) ** -0.5
WR = 3 * H + 1
POS_ROWS = 125
EARLY = 3
NOWHERE = 1 << 20
assert N % POS_ROWS == 0
assert N == E and C == P and NU <= P and DUP % T == 0


class Step:

    def __init__(self, i, k, total, cycle=2, apart=None):
        self.i, self.k, self.total, self.cycle, self.apart = i, k, total, cycle, apart
        self.j = cycle * i + k
        self.s = k % 2
        self.static = isinstance(i, int)

    def slot(self, n):
        return self.k % n

    def back(self, n):
        k = (self.k - n) % self.cycle
        return Step(self.i + (self.k - n - k) // self.cycle, k, self.total, self.cycle, self.apart)

    def ahead(self, n):
        return self.back(-n)

    def wait_count(self, eng, semaphore, value):
        wait = eng.wait_ge(semaphore, value)
        if self.apart is not None:
            wait.then_inc(self.apart, 1)

    def valid(self):
        return not self.static or 0 <= self.j < self.total

    def last(self):
        return self.static and self.j == self.total - 1

    def wait(self, eng, semaphore, per_step=1):
        self.wait_count(eng, semaphore, (self.j + 1) * per_step)

    def wait_free(self, eng, semaphore, per_step=1, slots=2):
        if not self.static or self.j >= slots:
            self.wait_count(eng, semaphore, (self.j - slots + 1) * per_step)

    def wait_dma(self, eng, slot_semaphores, dmas=1):
        n = len(slot_semaphores)
        uses = self.i * (self.cycle // n) + self.k // n + 1
        self.wait_count(eng, slot_semaphores[self.slot(n)], uses * (16 * dmas))

    def wait_dma_free(self, eng, slot_semaphores, dmas=1):
        n = len(slot_semaphores)
        if not self.static or self.j >= n:
            uses = self.i * (self.cycle // n) + self.k // n
            self.wait_count(eng, slot_semaphores[self.slot(n)], uses * (16 * dmas))


def sweep(eng, total, lead, lag, body, cycle=2, apart=None, reach=1):
    head = -(-lead // cycle) * cycle
    end = (total - 1 - reach) // cycle * cycle
    for j in range(head):
        body(Step(j // cycle, j % cycle, total, cycle, apart))
    with eng.Fori(head // cycle, end // cycle) as i:
        for k in range(cycle):
            body(Step(i, k, total, cycle, apart))
    for j in range(end, total + lag):
        body(Step(j // cycle, j % cycle, total, cycle, apart))


def unit_rows(dram, st):
    if st.last():
        return dram[LAST:LAST + U, :]
    if st.static:
        return dram[st.j * U:(st.j + 1) * U, :]
    return dram[bass.ds(st.j * U, U), :]


def half_unit(st):
    return st.i * (st.cycle // 2) + st.k // 2


def unit_of(st):
    return Step(st.i, st.k // 2, st.total // 2, st.cycle // 2, st.apart)


def half_rows(dram, st):
    u = half_unit(st)
    if st.static:
        first = LAST if u == NU - 1 else u * U
        rows = dram[first:first + U, :]
    else:
        rows = dram[bass.ds(u * U, U), :]
    return rows.rearrange("(p h t) d -> h p t d", h=2, t=2)[st.s]


class Split:

    def __init__(self, t, name, shape):
        self.high, self.low = t.sb(name + "_high", shape, F32R), t.sb(name + "_low", shape, F32R)

    def fill(self, nc, dve, frm, semaphore, done):
        nc.vector.tensor_copy(self.high[:], frm).then_inc(semaphore, 1)
        dve.wait_ge(semaphore, done + 1)
        nc.vector.tensor_tensor(self.low[:], frm, self.high[:], ALU.subtract).then_inc(semaphore, 1)


def split_matmul(nc, out, lhs, rhs, cols, row, start, stop):
    nc.tensor.matmul(out, lhs.low[cols], rhs.high[row], start=start, stop=False)
    nc.tensor.matmul(out, lhs.high[cols], rhs.low[row], start=False, stop=False)
    return nc.tensor.matmul(out, lhs.high[cols], rhs.high[row], start=False, stop=stop)


class Tools:

    def __init__(self, nc, ctx):
        self.nc, self.ctx = nc, ctx
        self.numbers = []

    def sb(self, name, shape, dt=F32):
        return self.ctx.enter_context(self.nc.sbuf_tensor(name, shape, dt))

    def psum(self, name, shape, dt=F32):
        return self.ctx.enter_context(self.nc.psum_tensor(name, shape, dt))

    def sem(self, name):
        semaphore = self.ctx.enter_context(self.nc.semaphore(name))
        self.numbers.append(semaphore.num)
        return semaphore

    def clear(self):
        numbers = sorted(self.numbers)
        firsts = [n for n in numbers if n - 1 not in numbers]
        lasts = [n for n in numbers if n + 1 not in numbers]
        with self.nc.Block() as block:
            @block.gpsimd
            def _(pool):
                for first, last in zip(firsts, lasts):
                    pool.sem_clear(range(first, last + 1))

    def sems(self, *names):
        return [self.sem(n) for n in names]

    def slots(self, name, n=2):
        return [self.sem(f"{name}{s}") for s in range(n)]


def scatter_positions(nc, K, pos, tiles, semaphore):
    for n in tiles:
        nc.gpsimd.indirect_dma_start(
            out=K.pos_tab[:, :], out_offset=bass.IndirectOffsetOnAxis(ap=pos[:, n:n + 1], axis=0),
            in_=pos[:, T + n:T + n + 1], in_offset=None, bounds_check=N - 1, oob_is_err=False,
            ).then_inc(semaphore, 16)


def setup(nc, A, K):
    with ExitStack() as ctx:
        t = Tools(nc, ctx)
        n2m_nat = t.sb("n2m_nat", [P, D])
        kvqs_nat = t.sb("kvqs_nat", [P, 4, P])
        we_nat = t.sb("we_nat", [P, R])
        wedge_nat = t.sb("wedge_nat", [R, R])
        m2n_nat = t.sb("m2n_nat", [P, DC, P])
        ffn_nat = t.sb("ffn_nat", [P, DC, D])
        weT = t.sb("weT", [R, C])
        mixq, mixk = t.sb("mixq_nat", [P, DC, D]), t.sb("mixk_nat", [P, DC, D])
        b_k = t.sb("b_k", [P, D])
        b_rows = t.sb("b_rows", [3, 3, D])
        b_rest = t.sb("b_rest", [3, 2, 3, D])
        b_part = t.sb("b_part", [3, 3, 3, D], BF16)
        b_sum = t.sb("b_sum", [3, 2, 3, D], BF16)
        wbeta = t.sb("wbeta", [P, 3, C])
        src_i = t.sb("src_i", [NU, U], I32)
        dst_i = t.sb("dst_i", [NU, U], I32)
        prev_i = t.sb("prev_i", [NU, 1], I32)
        next_i = t.sb("next_i", [NU, 1], I32)
        src_f = t.sb("src_f", [NU, U])
        dst_f = t.sb("dst_f", [NU, U + 2])
        row_f = t.sb("row_f", [NU, U])
        keep = t.sb("keep", [NU, U])
        no_edge = t.sb("no_edge", [POS_ROWS, N // POS_ROWS], I32)
        zero_row = t.sb("zero_row", [1, C])
        sel_w = t.sb("sel_w_f", [WR, C])
        sel_m = t.sb("sel_m_f", [WR, C])
        psA = t.psum("setup_psA", [P, 512])
        psB = t.psum("setup_psB", [P, 512])
        psC = t.psum("setup_psC", [P, 512])
        psD = t.psum("setup_psD", [P, 512])
        psE = t.psum("setup_psE", [P, 512])
        psF = t.psum("setup_psF", [P, 512])
        psG = t.psum("setup_psG", [P, 512])
        psH = t.psum("setup_psH", [P, 512])
        weights_in, index_in, edges_filled, const_set, const_done = t.sems(
            "weights_in", "index_in", "edges_filled", "const_set", "const_done")
        weights_turned, weT_ready, edgeT_ready, cols_turned, rows_turned = t.sems(
            "weights_turned", "weT_ready", "edgeT_ready", "cols_turned", "rows_turned")
        vec, dst_ready, rows_ready, parts = t.sems("setup_vec", "dst_ready", "rows_ready", "bias_parts")
        sel_set, split, fills_set, edge_set, fills_out, n2m_copied = t.sems(
            "sel_set", "weights_split", "fills_set", "edge_set", "fills_out", "n2m_copied")

        loads = [
            (n2m_nat[:], A["L0_gnn_W_n2m"]),
            (we_nat[:], A["L0_gnn_We"]),
            (wedge_nat[:], A["L0_gnn_W_edge"]),
            (m2n_nat[:], A["L0_gnn_W_m2n"].rearrange("(c p) m -> p c m", c=DC)),
            (ffn_nat[:], A["L0_ffn_weight"].rearrange("(c p) i -> p c i", c=DC)),
            (mixq[:], A["L0_mix_wq"].rearrange("(c p) o -> p c o", c=DC)),
            (mixk[:], A["L0_mix_wk"].rearrange("(c p) o -> p c o", c=DC)),
            (K.mixv[:], A["L0_mix_wv"].rearrange("(c p) o -> p c o", c=DC)),
            (K.mixo[:], A["L0_mix_wo"].rearrange("(c p) o -> p c o", c=DC)),
            (wbeta[:].rearrange("p a c -> p (a c)"), A["L0_gnn_Wbeta"].to_broadcast([P, 3 * C])),
        ]
        for n, w in enumerate(("Wk", "Wv", "Wq", "Wskip")):
            loads.append((kvqs_nat[:, n, :], A["L0_gnn_" + w]))
        for n, b in enumerate(("bk", "bv", "bq", "bskip")):
            loads.append((K.b_kvqs[:, n * C:(n + 1) * C], row_of(A["L0_gnn_" + b]).to_broadcast([P, C])))
        for tile, b in ((b_k, "L0_mix_bk"), (K.b_v, "L0_mix_bv")):
            loads.append((tile[:], row_of(A[b]).to_broadcast([P, D])))
        for n, b in enumerate(("L0_mix_bq", "L0_mix_bo", "L0_ffn_bias")):
            loads.append((b_rows[:, n, :], row_of(A[b]).to_broadcast([3, D])))

        def units(v):
            return v[0:(NU - 1) * U].rearrange("(u e) -> u e", e=U)

        src, dst = A["src"], A["dst"]
        index_loads = [
            (src_i[0:NU - 1, :], units(src)), (src_i[NU - 1:NU, :], row_of(src[LAST:N])),
            (dst_i[0:NU - 1, :], units(dst)), (dst_i[NU - 1:NU, :], row_of(dst[LAST:N])),
            (prev_i[1:NU - 1, :], dst[U - 1:(NU - 2) * U].rearrange("(u e) -> u e", e=1)[::U]),
            (prev_i[NU - 1:NU, :], row_of(dst[LAST - 1:LAST])),
            (next_i[0:NU - 1, :], dst[U:(NU - 1) * U + 1].rearrange("(u e) -> u e", e=1)[::U]),
        ]

        with nc.Block() as block:
            @block.sync
            def _(sp):
                sp.wait_ge(edges_filled, 2)
                for to, frm in index_loads:
                    sp.dma_start(to, frm, allow_slow_non_contiguous=True).then_inc(index_in, 16)
                for to, frm in loads:
                    sp.dma_start(to, frm).then_inc(weights_in, 16)
                sp.wait_ge(fills_set, 2)
                sp.dma_start(K.pos_tab.rearrange("(p a) c -> p (a c)", p=POS_ROWS), no_edge[:]).then_inc(fills_out, 16)
                sp.dma_start(K.run_tab[E:E + 1, :], zero_row[:]).then_inc(fills_out, 16)
                sp.wait_ge(fills_out, 32)

            @block.gpsimd
            def _(pool):
                nc.gpsimd.memset(prev_i[:], -1).then_inc(edges_filled, 1)
                nc.gpsimd.memset(next_i[:], -1).then_inc(edges_filled, 1)
                nc.gpsimd.memset(K.ident[:], 1.0).then_inc(const_set, 1)
                nc.gpsimd.memset(K.head_mask[:], 1.0).then_inc(const_set, 1)
                nc.gpsimd.memset(sel_w[:], 0.0).then_inc(const_set, 1)
                nc.gpsimd.memset(sel_m[:], 1.0).then_inc(const_set, 1)
                nc.gpsimd.memset(K.not_done[:], 1.0).then_inc(const_set, 1)
                nc.gpsimd.memset(K.last_unit[:], 1.0).then_inc(const_set, 1)
                nc.gpsimd.memset(K.neg_half[:], -0.5).then_inc(const_set, 1)
                nc.gpsimd.memset(K.minus_one[:], -1.0).then_inc(const_set, 1)
                nc.gpsimd.memset(K.ones3[:], 1.0)
                pool.wait_ge(const_set, 8)
                nc.gpsimd.affine_select(out=K.ident[:], in_=K.ident[:], compare_op=ALU.is_equal, fill=0.0,
                                        base=0, pattern=[[-1, P]], channel_multiplier=1).then_inc(const_done, 1)
                mask = K.head_mask[:].rearrange("p (g e) -> p g e", e=MC)
                nc.gpsimd.affine_select(out=mask, in_=mask, compare_op=ALU.is_ge, fill=0.0, base=0,
                                        pattern=[[-MC, P // MC], [0, MC]],
                                        channel_multiplier=1).then_inc(const_set, 1)
                pool.wait_ge(const_set, 9)
                nc.gpsimd.affine_select(out=mask, in_=mask, compare_op=ALU.is_ge, fill=0.0, base=MC - 1,
                                        pattern=[[MC, P // MC], [0, MC]],
                                        channel_multiplier=-1).then_inc(const_done, 1)
                sel = sel_w[:].rearrange("h (g c) -> h g c", c=HC)
                for part in range(3):
                    nc.gpsimd.affine_select(out=sel, in_=sel, compare_op=ALU.not_equal, fill=1.0, base=-part * H,
                                            pattern=[[-1, H], [0, HC]], channel_multiplier=1).then_inc(sel_set, 1)
                    pool.wait_ge(sel_set, part + 1)
                nc.gpsimd.affine_select(out=sel_m[:], in_=sel_m[:], compare_op=ALU.is_equal, fill=0.0,
                                        base=-3 * H, pattern=[[0, C]], channel_multiplier=1).then_inc(sel_set, 1)
                nc.gpsimd.memset(no_edge[:], E).then_inc(fills_set, 1)
                nc.gpsimd.memset(zero_row[:], 0.0).then_inc(fills_set, 1)
                nc.gpsimd.iota(K.pos_cols[:, :, T:2 * T], [[U, NU], [P, T]], base=0, channel_multiplier=1
                               ).then_inc(edge_set, 1)
                pool.wait_ge(edge_set, 1)
                nc.gpsimd.iota(K.pos_cols[:, NU - 1, T:2 * T], [[P, T]], base=LAST, channel_multiplier=1)
                nc.gpsimd.affine_select(out=K.not_done[:], in_=K.not_done[:], compare_op=ALU.is_ge, fill=0.0,
                                        base=-(DUP // T), pattern=[[0, 1]],
                                        channel_multiplier=1).then_inc(const_done, 1)
                for col, op in ((0, ALU.is_equal), (1, ALU.not_equal)):
                    nc.gpsimd.affine_select(out=K.last_unit[:, col:col + 1], in_=K.last_unit[:, col:col + 1],
                                            compare_op=op, fill=0.0, base=-(NU - 1), pattern=[[0, 1]],
                                            channel_multiplier=1).then_inc(const_done, 1)

            @block.vector
            def _(dve):
                dve.wait_ge(index_in, 16 * len(index_loads))
                nc.vector.tensor_copy(src_f[:], src_i[:])
                nc.vector.tensor_copy(dst_f[:, 1:U + 1], dst_i[:])
                nc.vector.tensor_copy(dst_f[:, 0:1], prev_i[:])
                nc.vector.tensor_copy(dst_f[:, U + 1:U + 2], next_i[:]).then_inc(dst_ready, 1)
                dve.wait_ge(dst_ready, 1)
                nc.vector.tensor_tensor(K.same[:], dst_f[:, 1:U + 2], dst_f[:, 0:U + 1],
                                        ALU.is_equal).then_inc(vec, 1)
                dve.wait_ge(vec, 1)
                nc.vector.tensor_scalar(K.pen[:], K.same[:], -1.0, BIG, ALU.add, ALU.mult).then_inc(vec, 1)
                nc.vector.tensor_scalar(keep[:], K.same[:, 1:U + 1], float(NOWHERE), None,
                                        ALU.mult).then_inc(vec, 1)
                dve.wait_ge(vec, 3)
                nc.vector.tensor_tensor(row_f[:], keep[:], dst_f[:, 1:U + 1], ALU.add).then_inc(rows_ready, 1)
                dve.wait_ge(cols_turned, 3)
                for cols, ps in ((K.src_cols[:], psE), (K.dst_cols[:], psF), (K.pos_cols[:, :, 0:T], psG)):
                    nc.vector.tensor_copy(cols.rearrange("p u t -> p t u"),
                                          ps[:, 0:T * NU].rearrange("p (t u) -> p t u", t=T))
                dve.wait_ge(weights_in, 16 * len(loads))
                dve.wait_ge(const_done, 1)
                nc.vector.tensor_scalar(K.b_k1[:], b_k[:], 1.0, None, ALU.add)
                dve.wait_ge(sel_set, 4)
                nc.vector.tensor_copy(K.sel_w[:], sel_w[:])
                nc.vector.tensor_copy(K.sel_m[:], sel_m[:])
                nc.vector.tensor_scalar(b_rows[:, 0, :], b_rows[:, 0, :], 1.0, None, ALU.add).then_inc(parts, 1)
                dve.wait_ge(parts, 1)
                rest = b_rows[:]
                for r in range(3):
                    nc.vector.tensor_copy(b_part[:, r], rest).then_inc(parts, 1)
                    dve.wait_ge(parts, 2 * r + 2)
                    if r < 2:
                        nc.vector.tensor_tensor(b_rest[:, r], rest, b_part[:, r], ALU.subtract).then_inc(parts, 1)
                        dve.wait_ge(parts, 2 * r + 3)
                        rest = b_rest[:, r]
                nc.vector.tensor_scalar(b_sum[:, 0], b_part[:, 0], K.ident[0:3, 0:1], None, ALU.mult).then_inc(parts, 1)
                for r in range(1, 3):
                    to = b_sum[:, 1] if r == 1 else K.b_parts[:]
                    dve.wait_ge(parts, 6 + r)
                    nc.vector.scalar_tensor_tensor(out=to, in0=b_part[:, r], scalar=K.ident[0:3, r:r + 1],
                                                   in1=b_sum[:, r - 1], op0=ALU.mult, op1=ALU.add).then_inc(parts, 1)
                K.mixq.fill(nc, dve, mixq[:], split, 0)
                K.mixk.fill(nc, dve, mixk[:], split, 2)
                dve.wait_ge(weights_turned, 4)
                K.kvqsT.fill(nc, dve, psA[:], split, 4)
                K.ffnT.fill(nc, dve, psC[:].rearrange("p (c o) -> p c o", c=DC), split, 6)
                dve.wait_ge(n2m_copied, 1)
                K.m2nT.fill(nc, dve, psB[:, D:2 * D], split, 8)
                nc.vector.tensor_tensor(K.gate_w[:, 0, :], wbeta[:, 0, :], wbeta[:, 2, :], ALU.add)
                nc.vector.tensor_tensor(K.gate_w[:, 1, :], wbeta[:, 1, :], wbeta[:, 2, :], ALU.subtract)

            @block.tensor
            def _(pe):
                pe.wait_ge(const_done, 1)
                pe.wait_ge(rows_ready, 1)
                for f, ps in ((src_f[:], psE), (dst_f[:, 1:U + 1], psF), (row_f[:], psG)):
                    for n in range(T):
                        mm = nc.tensor.transpose(ps[:, n * NU:(n + 1) * NU], f[:, n * P:(n + 1) * P],
                                                 K.ident[0:NU, 0:NU])
                    mm.then_inc(cols_turned, 1)
                pe.wait_ge(weights_in, 16 * len(loads))
                nc.tensor.transpose(psD[0:R, 0:C], we_nat[:], K.ident[:]).then_inc(weights_turned, 1)
                for n in range(4):
                    mm = nc.tensor.transpose(psA[:, n * P:(n + 1) * P], kvqs_nat[:, n, :], K.ident[:])
                mm.then_inc(weights_turned, 1)
                for c in range(DC):
                    nc.tensor.transpose(psB[:, c * P:(c + 1) * P], n2m_nat[:, c * P:(c + 1) * P], K.ident[:])
                for c in range(DC):
                    mm = nc.tensor.transpose(psB[:, (DC + c) * P:(DC + c + 1) * P], m2n_nat[:, c, :], K.ident[:])
                mm.then_inc(weights_turned, 1)
                for i in range(DC):
                    for o in range(DC):
                        mm = nc.tensor.transpose(psC[:, i * D + o * P:i * D + (o + 1) * P],
                                                 ffn_nat[:, o, i * P:(i + 1) * P], K.ident[:])
                mm.then_inc(weights_turned, 1)
                pe.wait_ge(weT_ready, 1)
                nc.tensor.matmul(psH[0:R, 0:C], wedge_nat[:], weT[:], start=True, stop=True).then_inc(edgeT_ready, 1)

            @block.scalar
            def _(act):
                act.wait_ge(weights_turned, 1)
                nc.scalar.copy(weT[:], psD[0:R, 0:C]).then_inc(weT_ready, 1)
                act.wait_ge(weights_turned, 4)
                nc.scalar.copy(K.n2mT[:].rearrange("p c m -> p (c m)"), psB[:, 0:D]).then_inc(n2m_copied, 1)
                act.wait_ge(edgeT_ready, 1)
                nc.scalar.copy(K.edgeT[:], psH[0:R, 0:C])
        t.clear()


def row_of(v):
    return v.rearrange("(a n) -> a n", a=1)


def project(nc, A, K):
    with ExitStack() as ctx:
        t = Tools(nc, ctx)
        xt = [t.sb(f"pj_x{s}", [P, T, D]) for s in range(4)]
        xn = [t.sb(f"pj_xn{s}", [P, T, D]) for s in range(2)]
        bn = [t.sb(f"pj_bn{s}", [P, T, 6]) for s in range(2)]
        mv = [t.sb(f"pj_mv{s}", [P, T, 2]) for s in range(2)]
        ve = [t.sb(f"pj_ve{s}", [P, T]) for s in range(2)]
        mr = [t.sb(f"pj_mr{s}", [P, T, 2]) for s in range(2)]
        xnT = [t.sb(f"pj_xnT{s}", [P, DC, U]) for s in range(2)]
        mT = [Split(t, f"pj_mT{s}", [P, U]) for s in range(2)]
        pr = [t.sb(f"pj_pr{s}", [P, T, 4 * C]) for s in range(2)]
        pos = [t.sb(f"pj_pos{s}", [P, 2 * T], I32) for s in range(4)]
        psT = [t.psum(f"pj_psT{c}", [P, U]) for c in range(DC)]
        psM = [t.psum(f"pj_psM{s}", [P, U]) for s in range(2)]
        psP = [t.psum(f"pj_psP{n}", [P, 4 * C]) for n in range(T)]
        x_in, tabs_out = t.slots("pj_x_in", 4), t.slots("pj_tabs_out")
        pos_out, pos_done = K.project_pos_out, t.sem("pj_pos_done")
        bn_done, mv_done, ve_done, pow_done, mr_done, xn_done, stat_done = t.sems(
            "pj_bn_done", "pj_mv_done", "pj_ve_done", "pj_pow_done", "pj_mr_done", "pj_xn_done", "pj_stat_done")
        T_done, T_copied, m_done, m_high, m_low, p_done, p_added = t.sems(
            "pj_T_done", "pj_T_copied", "pj_m_done", "pj_m_high", "pj_m_low", "pj_p_done", "pj_p_added")

        def tiles(dram, st):
            return unit_rows(dram, st).rearrange("(p t) d -> p t d", t=T)

        with nc.Block() as block:
            @block.sync
            def _(sp):
                def load(st):
                    st.wait_free(sp, xn_done, T, slots=4)
                    sp.dma_start(xt[st.slot(4)][:], tiles(A["x"], st)).then_inc(x_in[st.slot(4)], 16)

                def body(st):
                    if st.static and st.j == 0:
                        load(st)
                        load(st.ahead(1))
                    if st.ahead(2).valid():
                        load(st.ahead(2))
                    done = st.back(5)
                    if done.valid():
                        done.wait(sp, p_added, T)
                        if done.last():
                            done.back(1).wait_dma(sp, tabs_out, 3)
                        for tab, lo, hi in ((K.kv_tab, 0, 2 * C), (K.q_tab, 2 * C, 3 * C), (K.skip_tab, 3 * C, 4 * C)):
                            sp.dma_start(tiles(tab, done), pr[done.s][:, :, lo:hi]).then_inc(tabs_out[done.s], 16)
                sweep(sp, NU, 6, 5, body, cycle=4, reach=2)
                for s in range(2):
                    sp.wait_ge(tabs_out[s], 16 * 3 * (NU // 2))

            @block.vector
            def _(dve):
                def body(st):
                    if st.valid():
                        st.wait_dma_free(dve, pos_out, EARLY)
                        nc.vector.tensor_copy(pos[st.slot(4)][:], K.cols_at(K.pos_cols, st.j)).then_inc(pos_done, 1)
                        st.wait_dma(dve, x_in)
                        st.wait_free(dve, mv_done, T)
                        for n in range(T):
                            nc.vector.bn_stats(bn[st.s][:, n, :], xt[st.slot(4)][:, n, :]).then_inc(bn_done, 1)
                        st.wait_free(dve, mr_done)
                        for n in range(T):
                            dve.wait_ge(bn_done, st.j * T + n + 1).then_inc(K.dve_waits, 1)
                            nc.vector.bn_aggr(mv[st.s][:, n, :], bn[st.s][:, n, :]).then_inc(mv_done, 1)
                    mid = st.back(3)
                    if mid.valid():
                        mid.wait(dve, m_high)
                        mid.wait_free(dve, p_done, T)
                        nc.vector.tensor_tensor(mT[mid.s].low[:], psM[mid.s][:], mT[mid.s].high[:], ALU.subtract
                                                ).then_inc(m_low, 1)
                    done = st.back(4)
                    if done.valid():
                        done.wait_dma_free(dve, tabs_out, 3)
                        for n in range(T):
                            dve.wait_ge(p_done, done.j * T + n + 1)
                            nc.vector.tensor_tensor(pr[done.s][:, n, :], psP[n][:], K.b_kvqs[:],
                                                    ALU.add).then_inc(p_added, 1)
                    if st.valid():
                        st.wait(dve, pow_done)
                        st.wait_free(dve, stat_done)
                        st.wait_free(dve, xn_done, T)
                        nc.vector.scalar_tensor_tensor(out=mr[st.s][:, :, 1], in0=mv[st.s][:, :, 0], scalar=-1.0,
                                                       in1=mr[st.s][:, :, 0], op0=ALU.mult, op1=ALU.mult
                                                       ).then_inc(mr_done, 1)
                sweep(dve, NU, 6, 4, body, cycle=4)

            @block.gpsimd
            def _(pool):
                def body(st):
                    if st.valid():
                        st.wait(pool, mv_done, T)
                        nc.gpsimd.tensor_scalar(ve[st.s][:], mv[st.s][:, :, 1], EPS, None, ALU.add).then_inc(ve_done, 1)
                        st.wait_free(pool, mr_done)
                        st.wait_free(pool, stat_done)
                        st.wait_free(pool, xn_done, T)
                        st.wait(pool, ve_done)
                        nc.gpsimd.tensor_tensor(mr[st.s][:, :, 0], ve[st.s][:], K.neg_half[:], ALU.pow
                                                ).then_inc(pow_done, 1)
                    kept = st.back(1)
                    if kept.valid():
                        kept.wait(pool, mr_done)
                        nc.gpsimd.tensor_copy(K.stat_at(kept.j), mr[kept.s][:].rearrange("p t a -> p (t a)")
                                              ).then_inc(stat_done, 1)
                    if st.valid():
                        st.wait(pool, pos_done)
                        if st.last():
                            st.back(1).wait_dma(pool, pos_out, EARLY)
                        scatter_positions(nc, K, pos[st.slot(4)], range(EARLY), pos_out[st.slot(4)])
                sweep(pool, NU, 2, 1, body, cycle=4, apart=K.pool_waits)
                for s in range(4):
                    pool.wait_ge(pos_out[s], 16 * EARLY * len(range(s, NU, 4)))

            @block.tensor
            def _(pe):
                def body(st):
                    if st.valid():
                        st.wait(pe, xn_done, T)
                        if not (st.static and st.j == 0):
                            pe.wait_ge(T_copied, st.j * DC)
                        for c in range(DC):
                            for n in range(T):
                                mm = nc.tensor.transpose(psT[c][:, n * P:(n + 1) * P],
                                                         xn[st.s][:, n, c * P:(c + 1) * P], K.ident[:])
                        mm.then_inc(T_done, 1)
                    mid = st.back(1)
                    if mid.valid():
                        mid.wait(pe, T_copied, DC)
                        mid.wait_free(pe, m_low)
                        for c in range(DC):
                            mm = nc.tensor.matmul(psM[mid.s][:], K.n2mT[:, c, :], xnT[mid.s][:, c, :],
                                                  start=(c == 0), stop=(c == DC - 1))
                        mm.then_inc(m_done, 1)
                    late = st.back(2)
                    if late.valid():
                        late.wait(pe, m_low)
                        for n in range(T):
                            if not (late.static and late.j == 0):
                                pe.wait_ge(p_added, (late.j - 1) * T + n + 1)
                            split_matmul(nc, psP[n][:], mT[late.s], K.kvqsT,
                                         (slice(None), slice(n * P, (n + 1) * P)), slice(None),
                                         start=True, stop=True).then_inc(p_done, 1)
                sweep(pe, NU, 4, 2, body, cycle=4)

            @block.scalar
            def _(act):
                def normalise(st, lo, hi):
                    if lo == 0:
                        st.wait(act, mr_done)
                        st.wait_dma(act, x_in)
                        st.wait_free(act, T_done)
                    for n in range(lo, hi):
                        nc.scalar.activation(xn[st.s][:, n, :], xt[st.slot(4)][:, n, :], ACT.Identity,
                                             scale=mr[st.s][:, n, 0:1], bias=mr[st.s][:, n, 1:2]
                                             ).then_inc(xn_done, 1)

                def body(st):
                    if st.static and st.j == 0:
                        normalise(st, 0, T)
                    if st.valid():
                        st.wait(act, T_done)
                        st.wait_free(act, m_done)
                        for c in range(DC):
                            nc.scalar.copy(xnT[st.s][:, c, :], psT[c][:]).then_inc(T_copied, 1)
                    if st.ahead(1).valid():
                        normalise(st.ahead(1), 0, T // 2)
                    mid = st.back(1)
                    if mid.valid():
                        mid.wait(act, m_done)
                        mid.wait_free(act, p_done, T)
                        mid.wait_free(act, m_low)
                        nc.scalar.copy(mT[mid.s].high[:], psM[mid.s][:]).then_inc(m_high, 1)
                    if st.ahead(1).valid():
                        normalise(st.ahead(1), T // 2, T)
                sweep(act, NU, 4, 1, body, cycle=4)
        t.clear()


def attend(nc, A, K):
    with ExitStack() as ctx:
        t = Tools(nc, ctx)
        xt = [t.sb(f"at_x{s}", [P, T, D]) for s in range(3)]
        xn = [t.sb(f"at_xn{s}", [P, T, D + 1]) for s in range(6)]
        mr = [t.sb(f"at_mr{s}", [P, T, 2]) for s in range(2)]
        xnT = [Split(t, f"at_xnT{s}", [P, DC, U]) for s in range(2)]
        z1 = [t.sb(f"at_z1{s}", [P, T, D]) for s in range(2)]
        ex = [t.sb(f"at_ex{s}", [P, T, D]) for s in range(2)]
        phi = [t.sb(f"at_phi{s}", [P, T, D]) for s in range(2)]
        ea = [t.sb(f"at_ea{s}", [P, T, R]) for s in range(3)]
        eaT = [t.sb(f"at_eaT{s}", [R, U]) for s in range(2)]
        kv = [t.sb(f"at_kv{s}", [P, T, 2 * C]) for s in range(6)]
        qd = [t.sb(f"at_qd{s}", [P, T, C]) for s in range(6)]
        vj = [t.sb(f"at_vj{s}", [P, T, C]) for s in range(2)]
        prod = t.sb("at_prod", [P, T, C])
        sc = [t.sb(f"at_sc{s}", [P, H, T]) for s in range(2)]
        scT = [t.sb(f"at_scT{s}", [H * T, P]) for s in range(2)]
        idx = [t.sb(f"at_idx{s}", [P, 2, T], I32) for s in range(6)]
        psT = [t.psum(f"at_psT{c}", [P, U]) for c in range(DC)]
        psK = t.psum("at_psK", [P, 2, D])
        psE = t.psum("at_psE", [P, T, C])
        psX = t.psum("at_psX", [P, U])
        psS = t.psum("at_psS", [P, P])
        acc = [t.psum(f"at_acc{c}", [P, D + 1]) for c in range(DC)]
        x_in, ea_in = t.slots("at_x_in", 3), t.slots("at_ea_in", 3)
        kv_in, qd_in = K.kv_in, K.qd_in
        vj_out, sc_out = t.slots("at_vj_out"), t.slots("at_sc_out")
        ones_set, mr_done, xn_done, T_done, T_high, T_low, k_done, z_done, ex_done, phi_done, masked, acc_step = t.sems(
            "at_ones_set", "at_mr_done", "at_xn_done", "at_T_done", "at_T_high", "at_T_low", "at_k_done", "at_z_done",
            "at_ex_done", "at_phi_done", "at_masked", "at_acc_step")
        idx_done, eaT_done, eaT_copied, e_done, vj_done, kj_done, prod_done, sc_done, scT_done, scT_copied = t.sems(
            "at_idx_done", "at_eaT_done", "at_eaT_copied", "at_e_done", "at_vj_done", "at_kj_done",
            "at_prod_done", "at_sc_done", "at_scT_done", "at_scT_copied")

        def edge_tiles(dram, st):
            return unit_rows(dram, st).rearrange("(t p) d -> p t d", p=P)

        with nc.Block() as block:
            @block.sync
            def _(sp):
                def load(st):
                    st.wait_free(sp, eaT_done, slots=3)
                    sp.dma_start(ea[st.slot(3)][:], edge_tiles(A["edge_attr_64"], st)).then_inc(ea_in[st.slot(3)], 16)
                    st.wait_free(sp, xn_done, T, slots=3)
                    sp.dma_start(xt[st.slot(3)][:], unit_rows(A["x"], st).rearrange("(p t) d -> p t d", t=T)
                                 ).then_inc(x_in[st.slot(3)], 16)

                def body(st):
                    if st.static and st.j == 0:
                        load(st)
                        load(st.ahead(1))
                    if st.ahead(2).valid():
                        load(st.ahead(2))
                    mid = st.back(2)
                    if mid.valid():
                        mid.wait(sp, vj_done)
                        if mid.last():
                            mid.back(1).wait_dma(sp, vj_out)
                        sp.dma_start(edge_tiles(K.vj_tab, mid), vj[mid.s][:]).then_inc(vj_out[mid.s], 16)
                    late = st.back(3)
                    if late.valid():
                        late.wait(sp, scT_copied)
                        rows = H * T
                        to = (K.score_tab[late.j * rows:(late.j + 1) * rows, :] if late.static else
                              K.score_tab[bass.ds(late.j * rows, rows), :])
                        sp.dma_start(to, scT[late.s][:]).then_inc(sc_out[late.s], 16)
                sweep(sp, NU, 6, 3, body, cycle=6, reach=2)
                for s in range(2):
                    sp.wait_ge(vj_out[s], 16 * (NU // 2))
                    sp.wait_ge(sc_out[s], 16 * (NU // 2))

            @block.gpsimd
            def _(pool):
                for s in range(6):
                    nc.gpsimd.memset(xn[s][:, :, D:D + 1], 1.0).then_inc(ones_set, 1)

                def gather(st):
                    st.wait(pool, idx_done)
                    st.wait_free(pool, kj_done, slots=6)
                    for n in range(T):
                        nc.gpsimd.indirect_dma_start(
                            out=kv[st.slot(6)][:, n, :], out_offset=None, in_=K.kv_tab[:, :],
                            in_offset=bass.IndirectOffsetOnAxis(ap=idx[st.slot(6)][:, 0, n:n + 1], axis=0),
                            ).then_inc(kv_in[st.slot(6)], 16)
                    st.wait_free(pool, prod_done, slots=6)
                    for n in range(T):
                        nc.gpsimd.indirect_dma_start(
                            out=qd[st.slot(6)][:, n, :], out_offset=None, in_=K.q_tab[:, :],
                            in_offset=bass.IndirectOffsetOnAxis(ap=idx[st.slot(6)][:, 1, n:n + 1], axis=0),
                            ).then_inc(qd_in[st.slot(6)], 16)

                def body(st):
                    if st.valid():
                        gather(st)
                sweep(pool, NU, 2, 0, body, cycle=6, apart=K.pool_waits)

            @block.vector
            def _(dve):
                def index(st):
                    st.wait_dma_free(dve, kv_in, T)
                    st.wait_dma_free(dve, qd_in, T)
                    nc.vector.tensor_copy(idx[st.slot(6)][:, 0, :], K.cols_at(K.src_cols, st.j))
                    nc.vector.tensor_copy(idx[st.slot(6)][:, 1, :], K.cols_at(K.dst_cols, st.j)).then_inc(idx_done, 1)

                def normalise(st):
                    st.wait_free(dve, xn_done, T)
                    nc.vector.tensor_copy(mr[st.s][:].rearrange("p t a -> p (t a)"), K.stat_at(st.j)
                                          ).then_inc(mr_done, 1)
                    st.wait(dve, mr_done)
                    st.wait_dma(dve, x_in)
                    st.wait_free(dve, T_done, slots=6)
                    st.wait_free(dve, acc_step, slots=6)
                    for n in range(T):
                        nc.vector.tensor_scalar(xn[st.slot(6)][:, n, 0:D], xt[st.slot(3)][:, n, :],
                                                mr[st.s][:, n, 0:1], mr[st.s][:, n, 1:2], ALU.mult, ALU.add
                                                ).then_inc(xn_done, 1)

                def add_bias(st, g):
                    dve.wait_ge(k_done, st.j * 2 + g + 1)
                    nc.vector.tensor_tensor(
                        z1[st.s][:, 2 * g:2 * g + 2, :], psK[:],
                        K.b_k1[:].rearrange("p (a d) -> p a d", a=1).to_broadcast([P, 2, D]),
                        ALU.add).then_inc(z_done, 1)

                def body(st):
                    if st.static and st.j == 0:
                        index(st)
                        index(st.ahead(1))
                        normalise(st)
                    if st.ahead(2).valid():
                        index(st.ahead(2))
                    if st.ahead(1).valid():
                        normalise(st.ahead(1))
                    if st.valid():
                        st.wait_free(dve, k_done, 2)
                        for c in range(DC):
                            dve.wait_ge(T_high, st.j * DC + c + 1)
                            nc.vector.tensor_tensor(xnT[st.s].low[:, c, :], psT[c][:], xnT[st.s].high[:, c, :],
                                                    ALU.subtract).then_inc(T_low, 1)
                    mid = st.back(1)
                    if mid.valid():
                        mid.wait_free(dve, ex_done, 2)
                        mid.wait_free(dve, phi_done, 2)
                        mid.wait(dve, e_done)
                        mid.wait_dma(dve, kv_in, T)
                        mid.wait_dma_free(dve, vj_out)
                        nc.vector.tensor_tensor(vj[mid.s][:], kv[mid.slot(6)][:, :, C:2 * C], psE[:], ALU.add
                                                ).then_inc(vj_done, 1)
                        add_bias(mid, 0)
                        mid.wait(dve, vj_done)
                        nc.vector.tensor_tensor(psE[:], kv[mid.slot(6)][:, :, 0:C], psE[:], ALU.add).then_inc(kj_done, 1)
                    late = st.back(2)
                    if late.valid():
                        late.wait_free(dve, acc_step)
                        for g in range(2):
                            dve.wait_ge(ex_done, late.j * 2 + g + 1)
                            nc.vector.scalar_tensor_tensor(
                                out=phi[late.s][:, 2 * g:2 * g + 2, :], in0=ex[late.s][:, 2 * g:2 * g + 2, :],
                                scalar=1.0, in1=z1[late.s][:, 2 * g:2 * g + 2, :], op0=ALU.min, op1=ALU.max
                                ).then_inc(phi_done, 1)
                        if late.last():
                            late.wait(dve, phi_done, 2)
                            nc.vector.tensor_scalar(phi[late.s][:], phi[late.s][:], K.not_done[:, 0:1], None,
                                                    ALU.mult).then_inc(masked, 1)
                    if mid.valid():
                        add_bias(mid, 1)
                        mid.wait(dve, kj_done)
                        mid.wait_dma(dve, qd_in, T)
                        if not (mid.static and mid.j == 0):
                            dve.wait_ge(sc_done, mid.j)
                        nc.vector.tensor_tensor(prod[:], qd[mid.slot(6)][:], psE[:], ALU.mult).then_inc(prod_done, 1)
                        mid.wait(dve, prod_done)
                        mid.wait_free(dve, scT_done)
                        nc.vector.tensor_reduce(sc[mid.s][:].rearrange("p h t -> p t h"),
                                                prod[:].rearrange("p t (h c) -> p t h c", h=H), AX_X, ALU.add
                                                ).then_inc(sc_done, 1)
                sweep(dve, NU, 4, 2, body, cycle=6)

            @block.tensor
            def _(pe):
                pe.wait_ge(ones_set, 6)

                def body(st):
                    if st.valid():
                        st.wait_dma(pe, ea_in)
                        if not (st.static and st.j == 0):
                            pe.wait_ge(eaT_copied, st.j).then_inc(K.pe_waits, 1)
                        for n in range(T):
                            mm = nc.tensor.transpose(psX[0:R, n * P:(n + 1) * P], ea[st.slot(3)][:, n, :], K.ident[:])
                        mm.then_inc(eaT_done, 1)
                        st.wait(pe, xn_done, T)
                        if not (st.static and st.j == 0):
                            pe.wait_ge(T_low, st.j * DC)
                        for c in range(DC):
                            for n in range(T):
                                mm = nc.tensor.transpose(psT[c][:, n * P:(n + 1) * P],
                                                         xn[st.slot(6)][:, n, c * P:(c + 1) * P], K.ident[:])
                        mm.then_inc(T_done, 1)
                    mid, late = st.back(1), st.back(3)
                    if mid.valid():
                        mid.wait(pe, eaT_copied)
                        if not (mid.static and mid.j == 0):
                            pe.wait_ge(prod_done, mid.j)
                        for n in range(T):
                            mm = nc.tensor.matmul(psE[:, n, :], eaT[mid.s][:, n * P:(n + 1) * P], K.edgeT[:],
                                                  start=True, stop=True)
                        mm.then_inc(e_done, 1)
                    for g in range(2):
                        if mid.valid():
                            if g == 0:
                                mid.wait(pe, T_low, DC)
                            if not (mid.static and mid.j == 0 and g == 0):
                                pe.wait_ge(z_done, mid.j * 2 + g)
                            for n in range(2):
                                for c in range(DC):
                                    rows = (slice(None), c, slice((2 * g + n) * P, (2 * g + n + 1) * P))
                                    mm = split_matmul(nc, psK[:, n, :], xnT[mid.s], K.mixk, rows, (slice(None), c),
                                                      start=(c == 0), stop=(c == DC - 1))
                            mm.then_inc(k_done, 1)
                        if late.valid():
                            if g == 0:
                                late.wait(pe, phi_done, 2)
                                if late.last():
                                    pe.wait_ge(masked, 1)
                            for n in range(2 * g, 2 * g + 2):
                                for c in range(DC):
                                    first = late.static and late.j == 0 and n == 0
                                    mm = nc.tensor.matmul(acc[c][:], phi[late.s][:, n, c * P:(c + 1) * P],
                                                          xn[late.slot(6)][:, n, :], start=first,
                                                          stop=late.last() and n == T - 1, skip_group_check=True)
                            if g == 1:
                                mm.then_inc(acc_step, 1)
                    score = st.back(2)
                    if score.valid():
                        score.wait(pe, sc_done)
                        if not (score.static and score.j == 0):
                            pe.wait_ge(scT_copied, score.j)
                        nc.tensor.transpose(psS[0:H * T, :], sc[score.s][:].rearrange("p h t -> p (h t)"),
                                            K.ident[:]).then_inc(scT_done, 1)
                sweep(pe, NU, 4, 3, body, cycle=6)

            @block.scalar
            def _(act):
                def body(st):
                    if st.valid():
                        st.wait(act, eaT_done)
                        st.wait_free(act, e_done)
                        nc.scalar.copy(eaT[st.s][:], psX[0:R, :]).then_inc(eaT_copied, 1)
                        st.wait(act, T_done)
                        st.wait_free(act, k_done, 2)
                        st.wait_free(act, T_low, DC)
                        for c in range(DC):
                            nc.scalar.copy(xnT[st.s].high[:, c, :], psT[c][:]).then_inc(T_high, 1)
                    mid = st.back(1)
                    if mid.valid():
                        mid.wait_free(act, phi_done, 2)
                        for g in range(2):
                            act.wait_ge(z_done, mid.j * 2 + g + 1)
                            nc.scalar.activation(ex[mid.s][:, 2 * g:2 * g + 2, :], z1[mid.s][:, 2 * g:2 * g + 2, :],
                                                 ACT.Exp, bias=K.minus_one[:]).then_inc(ex_done, 1)
                    score = st.back(2)
                    if score.valid():
                        score.wait(act, scT_done)
                        score.wait_dma_free(act, sc_out)
                        nc.scalar.copy(scT[score.s][:], psS[0:H * T, :]).then_inc(scT_copied, 1)
                sweep(act, NU, 4, 2, body, cycle=6)
                act.wait_ge(acc_step, NU)
                for c in range(DC):
                    nc.scalar.copy(K.M[:, c, :], acc[c][:])
        t.clear()


def softmax(nc, A, K):
    with ExitStack() as ctx:
        t = Tools(nc, ctx)
        score = t.sb("sm_score", [NU, H, U])
        fwd = t.sb("sm_fwd", [NU, H, U])
        whole = t.sb("sm_whole", [NU, H, U])
        prob = t.sb("sm_prob", [NU, H, U])
        wgt = t.sb("sm_wgt", [NU, WR, U], BF16)
        hand = t.sb("sm_hand", [NU, 2, H])
        behind = t.sb("sm_behind", [NU, H])
        chain = t.sb("sm_chain", [H, 2, NU])
        carry = t.sb("sm_carry", [H, NU + 2])
        start = t.sb("sm_start", [NU, H])
        psX = t.psum("sm_psX", [P, P])
        psY = t.psum("sm_psY", [P, P])
        psZ = t.psum("sm_psZ", [P, P])
        score_in, wgt_out, vec, hand_ready, turned, carry_ready, turned_back, shifted, prob_ready, wgt_ready = t.sems(
            "sm_score_in", "sm_wgt_out", "sm_vec", "sm_hand_ready", "sm_turned", "sm_carry_ready",
            "sm_turned_back", "sm_shifted", "sm_prob_ready", "sm_wgt_ready")
        BEFORE = U - DUP
        scans = [("on", ALU.add, ALU.max, -BIG), ("back", ALU.add, ALU.max, -BIG),
                 ("on", ALU.mult, ALU.add, 0.0), ("back", ALU.add, ALU.max, -BIG)]

        with nc.Block() as block:
            @block.sync
            def _(sp):
                sp.dma_start(score[:].rearrange("u h e -> u (h e)"),
                             K.score_tab.rearrange("(u r) e -> u (r e)", r=H * T)).then_inc(score_in, 16)
                sp.wait_ge(wgt_ready, 1)
                sp.dma_start(K.wgt_tab.rearrange("(u r) e -> u (r e)", r=WR),
                             wgt[:].rearrange("u h e -> u (h e)")).then_inc(wgt_out, 16)
                sp.wait_ge(wgt_out, 16)

            @block.vector
            def _(dve):
                count = [0]

                def chained(ins):
                    ins.then_inc(vec, 1)
                    count[0] += 1
                    dve.wait_ge(vec, count[0])

                def scan_units(n, way, op0, op1, empty, frm, to):
                    gates = K.pen if op0 == ALU.add else K.same
                    along = slice(None) if way == "on" else slice(None, None, -1)
                    gate = gates[:, 0:U] if way == "on" else gates[:, 1:U + 1]
                    end = U - 1 if way == "on" else 0
                    for h in range(H):
                        ins = nc.vector.tensor_tensor_scan(to[:, h, along], gate[:, along], frm[:, h, along],
                                                           empty, op0, op1)
                    chained(ins)
                    chained(nc.vector.tensor_copy(hand[:, 0, :], to[:, :, end]))
                    chained(nc.vector.tensor_reduce(hand[:, 1, 0:1], gate, AX_X, ALU.min))
                    if way == "on":
                        u = NU - 2
                        chained(nc.vector.tensor_copy(hand[u:u + 1, 0, :], to[u:u + 1, :, BEFORE - 1]))
                        chained(nc.vector.tensor_reduce(hand[u:u + 1, 1, 0:1], gate[u:u + 1, 0:BEFORE], AX_X, ALU.min))
                    else:
                        chained(nc.vector.tensor_scalar(behind[:], to[:, :, DUP], K.last_unit[0:NU, 0:1], None,
                                                        ALU.mult))
                        chained(nc.vector.scalar_tensor_tensor(
                            out=hand[:, 0, :], in0=hand[:, 0, :], scalar=K.last_unit[0:NU, 1:2],
                            in1=behind[:], op0=ALU.mult, op1=ALU.add))
                    nc.vector.tensor_copy(hand[:, 1, 1:H], hand[:, 1, 0:1].to_broadcast([NU, H - 1])
                                          ).then_inc(hand_ready, 1)
                    dve.wait_ge(turned, n + 1)
                    nc.vector.memset(carry[:], empty)
                    nc.vector.tensor_copy(chain[:, 0, :], psX[0:H, 0:NU])
                    chained(nc.vector.tensor_copy(chain[:, 1, :], psY[0:H, 0:NU]))
                    nc.vector.tensor_tensor_scan(carry[:, 1:NU + 1][:, along], chain[:, 1, along],
                                                 chain[:, 0, along], empty, op0, op1).then_inc(carry_ready, 1)
                    dve.wait_ge(turned_back, n + 1)
                    chained(nc.vector.tensor_copy(start[:], psZ[0:NU, 0:H]))
                    for h in range(H):
                        ins = nc.vector.tensor_tensor_scan(to[:, h, along], gate[:, along], frm[:, h, along],
                                                           start[:, h:h + 1], op0, op1)
                    chained(ins)

                dve.wait_ge(score_in, 16)
                scan_units(0, *scans[0], score, fwd)
                scan_units(1, *scans[1], fwd, whole)
                nc.vector.tensor_tensor(score[:], score[:], whole[:], ALU.subtract).then_inc(shifted, 1)
                dve.wait_ge(prob_ready, 1)
                scan_units(2, *scans[2], prob, fwd)
                scan_units(3, *scans[3], fwd, whole)
                chained(nc.vector.tensor_scalar(whole[:], whole[:], 1e-16, None, ALU.add))
                chained(nc.vector.reciprocal(whole[:], whole[:]))
                chained(nc.vector.tensor_tensor(score[:], prob[:], whole[:], ALU.mult))
                chained(nc.vector.tensor_copy(wgt[:, 0:H, :], score[:]))
                chained(nc.vector.tensor_tensor(fwd[:], score[:], wgt[:, 0:H, :], ALU.subtract))
                chained(nc.vector.tensor_copy(wgt[:, H:2 * H, :], fwd[:]))
                nc.vector.tensor_tensor(wgt[:, 2 * H:3 * H, :], fwd[:], wgt[:, H:2 * H, :], ALU.subtract)
                nc.vector.tensor_copy(wgt[:, 3 * H, :], K.same[:, 0:U]).then_inc(wgt_ready, 1)

            @block.scalar
            def _(act):
                act.wait_ge(shifted, 1)
                nc.scalar.activation(prob[:].rearrange("u h e -> u (h e)"), score[:].rearrange("u h e -> u (h e)"),
                                     ACT.Exp, scale=SCALE).then_inc(prob_ready, 1)

            @block.tensor
            def _(pe):
                for n, (way, *_) in enumerate(scans):
                    pe.wait_ge(hand_ready, n + 1)
                    nc.tensor.transpose(psX[0:H, 0:NU], hand[:, 0, :], K.ident[0:NU, 0:NU])
                    nc.tensor.transpose(psY[0:H, 0:NU], hand[:, 1, :], K.ident[0:NU, 0:NU]).then_inc(turned, 1)
                    pe.wait_ge(carry_ready, n + 1)
                    frm = carry[:, 0:NU] if way == "on" else carry[:, 2:NU + 2]
                    nc.tensor.transpose(psZ[0:NU, 0:H], frm, K.ident[0:H, 0:H]).then_inc(turned_back, 1)
        t.clear()


def readout(nc, A, K):
    with ExitStack() as ctx:
        t = Tools(nc, ctx)
        MT = t.sb("ro_MT", [P, DC, D])
        kvm = t.sb("ro_kvm", [P, DC, P])
        kvT = t.sb("ro_kvT", [P, DC, P])
        ks = t.sb("ro_ks", [P, DC, P])
        psT = [t.psum(f"ro_psT{c}", [P, D]) for c in range(DC)]
        psV = t.psum("ro_psV", [P, DC, P])
        psKT = t.psum("ro_psKT", [P, DC, P])
        psS = t.psum("ro_psS", [P, DC, P])
        psG = t.psum("ro_psG", [P, DC, D])
        m_turned, m_copied, kv_done, ks_ready, vec, kvm_ready, kv_turned, kv_copied, g_done, ks_turned = t.sems(
            "ro_m_turned", "ro_m_copied", "ro_kv_done", "ro_ks_ready", "ro_vec", "ro_kvm_ready", "ro_kv_turned",
            "ro_kv_copied", "ro_g_done", "ro_ks_turned")
        with nc.Block() as block:
            @block.tensor
            def _(pe):
                for x in range(DC):
                    for d in range(DC):
                        mm = nc.tensor.transpose(psT[x][:, d * P:(d + 1) * P], K.M[:, d, x * P:(x + 1) * P], K.ident[:])
                mm.then_inc(m_turned, 1)
                pe.wait_ge(m_copied, DC)
                for d in range(DC):
                    for x in range(DC):
                        mm = nc.tensor.matmul(psV[:, d, :], MT[:, x, d * P:(d + 1) * P],
                                              K.mixv[:, x, d * P:(d + 1) * P], start=(x == 0), stop=(x == DC - 1))
                mm.then_inc(kv_done, 1)
                pe.wait_ge(ks_ready, 1)
                for d in range(DC):
                    mm = nc.tensor.transpose(psS[:, d, :], ks[:, d, :], K.ident[:])
                mm.then_inc(ks_turned, 1)
                pe.wait_ge(kvm_ready, 1)
                for d in range(DC):
                    mm = nc.tensor.transpose(psKT[:, d, :], kvm[:, d, :], K.ident[:])
                mm.then_inc(kv_turned, 1)
                pe.wait_ge(kv_copied, 1)
                for d in range(DC):
                    mm = nc.tensor.matmul(psG[:, d, :], kvT[:, d, :], K.mixo[:, d, :], start=True, stop=True)
                mm.then_inc(g_done, 1)

            @block.scalar
            def _(act):
                act.wait_ge(m_turned, 1)
                for x in range(DC):
                    nc.scalar.copy(MT[:, x, :], psT[x][:]).then_inc(m_copied, 1)
                act.wait_ge(kv_turned, 1)
                nc.scalar.copy(kvT[:], psKT[:]).then_inc(kv_copied, 1)

            @block.vector
            def _(dve):
                for d in range(DC):
                    ins = nc.vector.tensor_copy(ks[:, d, :], K.M[:, d, D:D + 1].to_broadcast([P, P]))
                ins.then_inc(ks_ready, 1)
                dve.wait_ge(kv_done, 1)
                for d in range(DC):
                    ins = nc.vector.scalar_tensor_tensor(out=kvm[:, d, :], in0=K.b_v[:, d * P:(d + 1) * P],
                                                         scalar=K.M[:, d, D:D + 1], in1=psV[:, d, :],
                                                         op0=ALU.mult, op1=ALU.add)
                ins.then_inc(vec, 1)
                dve.wait_ge(vec, 1)
                for d in range(DC):
                    ins = nc.vector.tensor_tensor(kvm[:, d, :], kvm[:, d, :], K.head_mask[:], ALU.mult)
                ins.then_inc(kvm_ready, 1)
                dve.wait_ge(ks_turned, 1)
                nc.vector.tensor_copy(K.ksum[:], psS[:].rearrange("p c d -> p (c d)"))
                dve.wait_ge(g_done, 1)
                K.G.fill(nc, dve, psG[:], vec, 1)
        t.clear()


def aggregate(nc, A, K):
    with ExitStack() as ctx:
        t = Tools(nc, ctx)
        vj = [t.sb(f"ag_vj{s}", [P, T, C]) for s in range(4)]
        wg = [t.sb(f"ag_wg{s}", [WR, U], BF16) for s in range(4)]
        vT = [t.sb(f"ag_vT{s}", [P, U]) for s in range(2)]
        msg = [t.sb(f"ag_msg{s}", [P, U]) for s in range(2)]
        run = [t.sb(f"ag_run{s}", [P, U]) for s in range(4)]
        rows = [t.sb(f"ag_rows{s}", [P, T, C]) for s in range(4)]
        pos = [t.sb(f"ag_pos{s}", [P, 2 * T], I32) for s in range(4)]
        psV = [t.psum(f"ag_psV{s}", [P, U]) for s in range(2)]
        psW = [t.psum(f"ag_psW{s}", [P, U]) for s in range(2)]
        psG = [t.psum(f"ag_psG{s}", [P, U]) for s in range(2)]
        psR = [t.psum(f"ag_psR{s}", [P, T, C]) for s in range(2)]
        vj_in, wg_in, rows_out = t.slots("ag_vj_in", 4), t.slots("ag_wg_in", 4), t.slots("ag_rows_out", 4)
        v_turned, v_copied, w_spread, msg_done, run_done, run_turned, rows_done, pos_done = t.sems(
            "ag_v_turned", "ag_v_copied", "ag_w_spread", "ag_msg_done", "ag_run_done", "ag_run_turned",
            "ag_rows_done", "ag_pos_done")
        pos_out = K.aggregate_pos_out

        with nc.Block() as block:
            @block.sync
            def _(sp):
                def load(st):
                    st.wait_free(sp, v_turned, slots=4)
                    sp.dma_start(vj[st.slot(4)][:], unit_rows(K.vj_tab, st).rearrange("(t p) d -> p t d", p=P)
                                 ).then_inc(vj_in[st.slot(4)], 16)
                    st.wait_free(sp, w_spread, slots=4)
                    frm = (K.wgt_tab[st.j * WR:(st.j + 1) * WR, :] if st.static else
                           K.wgt_tab[bass.ds(st.j * WR, WR), :])
                    sp.dma_start(wg[st.slot(4)][:], frm).then_inc(wg_in[st.slot(4)], 16)

                def body(st):
                    if st.static and st.j == 0:
                        load(st)
                        load(st.ahead(1))
                    if st.ahead(2).valid():
                        load(st.ahead(2))
                    done = st.back(4)
                    if done.valid():
                        done.wait(sp, rows_done)
                        if done.last():
                            done.back(1).wait_dma(sp, rows_out)
                        sp.dma_start(unit_rows(K.run_tab, done).rearrange("(t p) d -> p t d", p=P),
                                     rows[done.slot(4)][:]).then_inc(rows_out[done.slot(4)], 16)
                sweep(sp, NU, 4, 4, body, cycle=4, reach=2)
                for s in range(4):
                    sp.wait_ge(rows_out[s], 16 * len(range(s, NU, 4)))

            @block.tensor
            def _(pe):
                def body(st):
                    if st.valid():
                        st.wait_dma(pe, vj_in)
                        st.wait_free(pe, v_copied)
                        for n in range(T):
                            mm = nc.tensor.transpose(psV[st.s][:, n * P:(n + 1) * P], vj[st.slot(4)][:, n, :], K.ident[:])
                        mm.then_inc(v_turned, 1)
                    late = st.back(3)
                    if late.valid():
                        late.wait(pe, run_done)
                        late.wait_free(pe, rows_done)
                        for n in range(T):
                            mm = nc.tensor.transpose(psR[late.s][:, n, :], run[late.slot(4)][:, n * P:(n + 1) * P], K.ident[:])
                        mm.then_inc(run_turned, 1)
                    if st.valid():
                        st.wait_dma(pe, wg_in)
                        st.wait_free(pe, run_done)
                        nc.tensor.matmul(psW[st.s][:], K.sel_w[:], wg[st.slot(4)][:], start=True, stop=True)
                        nc.tensor.matmul(psG[st.s][:], K.sel_m[:], wg[st.slot(4)][:], start=True, stop=True
                                         ).then_inc(w_spread, 1)
                sweep(pe, NU, 4, 3, body, cycle=4)

            @block.scalar
            def _(act):
                def body(st):
                    if st.valid():
                        st.wait(act, v_turned)
                        st.wait_free(act, msg_done)
                        nc.scalar.copy(vT[st.s][:], psV[st.s][:]).then_inc(v_copied, 1)
                    late = st.back(3)
                    if late.valid():
                        late.wait(act, run_turned)
                        late.wait_dma_free(act, rows_out)
                        nc.scalar.copy(rows[late.slot(4)][:], psR[late.s][:]).then_inc(rows_done, 1)
                sweep(act, NU, 4, 3, body, cycle=4)

            @block.vector
            def _(dve):
                def position(st):
                    st.wait_dma_free(dve, pos_out, T - EARLY)
                    nc.vector.tensor_copy(pos[st.slot(4)][:], K.cols_at(K.pos_cols, st.j)).then_inc(pos_done, 1)

                def body(st):
                    if st.static and st.j == 0:
                        position(st)
                        position(st.ahead(1))
                    if st.ahead(2).valid():
                        position(st.ahead(2))
                    mid = st.back(1)
                    if mid.valid():
                        mid.wait(dve, msg_done)
                        mid.wait_free(dve, run_turned, slots=4)
                        if mid.static and mid.j == 0:
                            first = 0.0
                        else:
                            dve.wait_ge(run_done, mid.j)
                            col = U - DUP if mid.last() else U
                            first = run[mid.back(1).slot(4)][:, col - 1:col]
                        nc.vector.tensor_tensor_scan(run[mid.slot(4)][:], psG[mid.s][:], msg[mid.s][:], first,
                                                     ALU.mult, ALU.add).then_inc(run_done, 1)
                    if st.valid():
                        st.wait(dve, v_copied)
                        st.wait(dve, w_spread)
                        st.wait_free(dve, run_done)
                        nc.vector.tensor_tensor(msg[st.s][:], vT[st.s][:], psW[st.s][:], ALU.mult).then_inc(msg_done, 1)
                sweep(dve, NU, 4, 1, body, cycle=4)

            @block.gpsimd
            def _(pool):
                def body(st):
                    st.wait(pool, pos_done)
                    if st.last():
                        st.back(1).wait_dma(pool, pos_out, T - EARLY)
                    scatter_positions(nc, K, pos[st.slot(4)], range(EARLY, T), pos_out[st.slot(4)])
                sweep(pool, NU, 2, 0, body, cycle=4, apart=K.pool_waits)
                for s in range(4):
                    pool.wait_ge(pos_out[s], 16 * (T - EARLY) * len(range(s, NU, 4)))
        t.clear()


def combine(nc, A, K):
    HT = 2
    with ExitStack() as ctx:
        t = Tools(nc, ctx)

        def two(name, shape, dt=F32):
            return [t.sb(f"cb_{name}{s}", shape, dt) for s in range(2)]

        def two_split(name, shape):
            return [Split(t, f"cb_{name}{s}", shape) for s in range(2)]

        xt = [t.sb(f"cb_x{s}", [P, HT, D]) for s in range(8)]
        ax = [t.sb(f"cb_ax{s}", [P, HT, 2, C]) for s in range(8)]
        mr, xn = two("mr", [P, HT * 2]), two("xn", [P, HT, D])
        xnT, qnT, xmT = [two_split(n, [P, DC, HT * P]) for n in ("xnT", "qnT", "xmT")]
        qnF = two("qnF", [P, DC, HT * P])
        ex, pk, qn = two("ex", [P, HT, D]), two("pk", [P, HT, D]), two("qn", [P, HT, D])
        nrm, rn = two("nrm", [P, HT, MH]), two("rn", [P, HT, MH])
        gp, gs, ge, beta = two("gp", [P, HT, 2 * C]), two("gs", [P, HT]), two("ge", [P, HT]), two("beta", [P, HT])
        dif, o = two("dif", [P, HT, C]), two("o", [P, HT, C])
        oT, oF = two_split("oT", [P, HT * P]), two("oF", [P, HT * P])
        x1 = [t.sb(f"cb_x1{s}", [P, HT, D]) for s in range(4)]
        bn, mv, ve, sh = two("bn", [P, HT, 6]), two("mv", [P, HT, 2]), two("ve", [P, HT]), two("sh", [P, HT])
        nm = two("nm", [P, HT])
        rs, xm, y = two("rs", [P, HT]), two("xm", [P, HT, D]), two("y", [P, HT, D])
        psT = t.psum("cb_psT", [P, DC, HT * P])
        psQ = [t.psum(f"cb_psQ{s}", [P, HT, D]) for s in range(2)]
        psN = t.psum("cb_psN", [P, DC, HT * P])
        psO = t.psum("cb_psO", [P, HT * P])
        psF = t.psum("cb_psF", [P, HT, D])
        psM = t.psum("cb_psM", [P, DC, HT * P])
        psY = t.psum("cb_psY", [P, HT, D])
        last_edge = [t.sb(f"cb_last_edge{s}", [P, T], I32) for s in range(4)]
        x_in, skip_in, agg_in = t.slots("cb_x_in", 8), t.slots("cb_skip_in", 8), K.agg_in
        edge_in, y_out = t.slots("cb_edge_in", 4), t.slots("cb_y_out")
        names = ("mr xn T Th Tl q ex phi pk nrm nre rn qn N Nh Nl gs ge gb beta dif db o O Oh Ol F "
                 "x1 bn mv ve nm rs sh xm M Mh Ml Y y").split()
        S = {n: t.sem("cb_" + n) for n in names}

        with nc.Block() as block:
            @block.sync
            def _(sp):
                def load(st):
                    slot = st.slot(8)
                    st.wait_free(sp, S["x1"], slots=8)
                    sp.dma_start(xt[slot][:], half_rows(A["x"], st)).then_inc(x_in[slot], 16)
                    st.wait_free(sp, S["gs"], HT, slots=8)
                    st.wait_free(sp, S["o"], slots=8)
                    sp.dma_start(ax[slot][:, :, 1, :], half_rows(K.skip_tab, st)).then_inc(skip_in[slot], 16)
                    if st.s == 0:
                        for half in (0, 1):
                            st.ahead(half).wait_dma_free(sp, agg_in, HT)
                        sp.dma_start(last_edge[slot // 2][:], unit_rows(K.pos_tab, unit_of(st)).rearrange(
                            "(p t) c -> p (t c)", t=T)).then_inc(edge_in[slot // 2], 16)

                def body(st):
                    if st.static and st.j == 0:
                        load(st)
                        load(st.ahead(1))
                    if st.ahead(2).valid():
                        load(st.ahead(2))
                    done = st.back(8)
                    if done.valid():
                        done.wait(sp, S["y"])
                        if done.static and half_unit(done) == NU - 1:
                            done.back(1).wait_dma(sp, y_out)
                            done.back(2).wait_dma(sp, y_out)
                        sp.dma_start(half_rows(K.out, done), y[done.s][:]).then_inc(y_out[done.s], 16)
                sweep(sp, 2 * NU, 16, 8, body, cycle=8, apart=K.sp_waits)
                for s in range(2):
                    sp.wait_ge(y_out[s], 16 * NU)

            @block.gpsimd
            def _(pool):
                def gather(st):
                    unit_of(st).wait_dma(pool, edge_in)
                    for n in range(HT):
                        col = st.s * HT + n
                        nc.gpsimd.indirect_dma_start(
                            out=ax[st.slot(8)][:, n, 0, :], out_offset=None, in_=K.run_tab[:, :],
                            in_offset=bass.IndirectOffsetOnAxis(ap=last_edge[st.slot(8) // 2][:, col:col + 1], axis=0),
                            ).then_inc(agg_in[st.slot(8)], 16)

                def body(st):
                    a, b, d = st.back(2), st.back(3), st.back(5)
                    if st.static and st.j == 0:
                        gather(st)
                    if st.ahead(1).valid():
                        st.ahead(1).wait_free(pool, S["gs"], HT, slots=8)
                        gather(st.ahead(1))
                    if d.valid():
                        d.wait(pool, S["mv"], HT)
                        nc.gpsimd.tensor_scalar(ve[d.s][:], mv[d.s][:, :, 1], EPS, None, ALU.add).then_inc(S["ve"], 1)
                        nc.gpsimd.tensor_scalar(nm[d.s][:], mv[d.s][:, :, 0], -1.0, None, ALU.mult).then_inc(S["nm"], 1)
                        d.wait(pool, S["ve"])
                        d.wait_free(pool, S["xm"], HT)
                        nc.gpsimd.tensor_tensor(rs[d.s][:], ve[d.s][:], K.neg_half[:, 0:HT], ALU.pow
                                                ).then_inc(S["rs"], 1)
                        d.wait(pool, S["nm"])
                        d.wait(pool, S["rs"])
                        nc.gpsimd.tensor_tensor(sh[d.s][:], nm[d.s][:], rs[d.s][:], ALU.mult).then_inc(S["sh"], 1)
                    if b.valid():
                        b.wait(pool, S["Nh"])
                        b.wait_free(pool, S["F"])
                        nc.gpsimd.tensor_tensor(qnT[b.s].low[:], qnF[b.s][:], qnT[b.s].high[:], ALU.subtract
                                                ).then_inc(S["Nl"], 1)
                        b.wait(pool, S["Oh"])
                        nc.gpsimd.tensor_tensor(oT[b.s].low[:], oF[b.s][:], oT[b.s].high[:], ALU.subtract
                                                ).then_inc(S["Ol"], 1)
                    dif_of = st.back(1)
                    if dif_of.valid():
                        dif_of.wait_dma(pool, skip_in)
                        dif_of.wait_dma(pool, agg_in, HT)
                        dif_of.wait_free(pool, S["o"])
                        nc.gpsimd.tensor_tensor(dif[dif_of.s][:], ax[dif_of.slot(8)][:, :, 1, :],
                                                ax[dif_of.slot(8)][:, :, 0, :], ALU.subtract).then_inc(S["dif"], 1)
                    if a.valid():
                        a.wait(pool, S["db"], HT)
                        a.wait_free(pool, S["O"])
                        nc.gpsimd.tensor_tensor(o[a.s][:], dif[a.s][:], ax[a.slot(8)][:, :, 0, :], ALU.add
                                                ).then_inc(S["o"], 1)
                sweep(pool, 2 * NU, 8, 5, body, cycle=8, apart=K.pool_waits)

            @block.vector
            def _(dve):
                def rowwise(tile, shape):
                    return tile.rearrange("p (a d) -> p a d", a=1).to_broadcast(shape)

                def gate(st, n):
                    if n == 0:
                        st.wait_dma(dve, skip_in)
                        st.wait_dma(dve, agg_in, HT)
                        st.wait_free(dve, S["ge"])
                    nc.vector.tensor_tensor_reduce(
                        out=gp[st.s][:, n, :], in0=ax[st.slot(8)][:, n, :, :].rearrange("p a c -> p (a c)"),
                        in1=K.gate_w[:].rearrange("p a c -> p (a c)"), scale=1.0, scalar=0.0,
                        op0=ALU.mult, op1=ALU.add, accum_out=gs[st.s][:, n:n + 1]).then_inc(S["gs"], 1)

                def body(st):
                    a = st.back(2)
                    d = st.back(5)
                    m = st.back(6)
                    e = st.back(8)
                    if d.valid():
                        d.wait(dve, S["F"])
                        d.wait_free(dve, S["y"], slots=4)
                        d.wait_free(dve, S["xm"], HT, slots=4)
                        nc.vector.tensor_tensor(x1[d.slot(4)][:], xt[d.slot(8)][:], psF[:], ALU.add).then_inc(S["x1"], 1)
                    if e.valid():
                        e.wait(dve, S["Y"])
                        e.wait_dma_free(dve, y_out)
                        nc.vector.tensor_tensor(y[e.s][:], x1[e.slot(4)][:], psY[:], ALU.add).then_inc(S["y"], 1)
                    if a.valid():
                        a.wait(dve, S["ex"])
                        nc.vector.scalar_tensor_tensor(out=psQ[a.s][:], in0=ex[a.s][:], scalar=1.0, in1=psQ[a.s][:],
                                                       op0=ALU.min, op1=ALU.max).then_inc(S["phi"], 1)
                    if st.valid():
                        st.wait(dve, S["Th"])
                        st.wait_free(dve, S["q"])
                        nc.vector.tensor_tensor(xnT[st.s].low[:], psT[:], xnT[st.s].high[:], ALU.subtract
                                                ).then_inc(S["Tl"], 1)
                    if d.valid():
                        d.wait(dve, S["x1"])
                        for n in range(HT):
                            nc.vector.bn_stats(bn[d.s][:, n, :], x1[d.slot(4)][:, n, :]).then_inc(S["bn"], 1)
                    if a.valid():
                        a.wait(dve, S["phi"])
                        nc.vector.tensor_tensor(pk[a.s][:], psQ[a.s][:], rowwise(K.ksum[:], [P, HT, D]), ALU.mult
                                                ).then_inc(S["pk"], 1)
                    if d.valid():
                        d.wait_free(dve, S["ve"])
                        d.wait_free(dve, S["nm"])
                        dve.wait_ge(S["bn"], (d.j + 1) * HT).then_inc(K.dve_waits, 1)
                        for n in range(HT):
                            nc.vector.bn_aggr(mv[d.s][:, n, :], bn[d.s][:, n, :]).then_inc(S["mv"], 1)
                    if a.valid():
                        a.wait(dve, S["pk"])
                        nc.vector.tensor_reduce(nrm[a.s][:], pk[a.s][:].rearrange("p t (h d) -> p t h d", h=MH),
                                                AX_X, ALU.add).then_inc(S["nrm"], 1)
                        a.wait(dve, S["ge"])
                        nc.vector.tensor_scalar(ge[a.s][:], ge[a.s][:], 1.0, None, ALU.add).then_inc(S["gb"], 1)
                    if st.valid():
                        gate(st, 0)
                    if a.valid():
                        a.wait(dve, S["nrm"])
                        nc.vector.tensor_scalar(nrm[a.s][:], nrm[a.s][:], 1e-6, None, ALU.add).then_inc(S["nre"], 1)
                        a.wait(dve, S["gb"])
                        a.wait_free(dve, S["db"], HT)
                        nc.vector.reciprocal(beta[a.s][:], ge[a.s][:]).then_inc(S["beta"], 1)
                    if st.valid():
                        gate(st, 1)
                    if a.valid():
                        a.wait(dve, S["nre"])
                        nc.vector.reciprocal(rn[a.s][:], nrm[a.s][:]).then_inc(S["rn"], 1)
                    if m.valid():
                        m.wait(dve, S["Mh"])
                        m.wait_free(dve, S["Y"])
                        nc.vector.tensor_tensor(xmT[m.s].low[:], psM[:], xmT[m.s].high[:], ALU.subtract
                                                ).then_inc(S["Ml"], 1)
                    if a.valid():
                        a.wait(dve, S["rn"])
                        a.wait_free(dve, S["N"])
                        nc.vector.tensor_tensor(qn[a.s][:].rearrange("p t (h d) -> p t h d", h=MH),
                                                psQ[a.s][:].rearrange("p t (h d) -> p t h d", h=MH),
                                                rn[a.s][:].rearrange("p t (h a) -> p t h a", a=1)
                                                .to_broadcast([P, HT, MH, MC]), ALU.mult).then_inc(S["qn"], 1)
                sweep(dve, 2 * NU, 8, 8, body, cycle=8)

            @block.tensor
            def _(pe):
                def turn(ps, tile, st):
                    for c in range(DC):
                        for n in range(HT):
                            mm = nc.tensor.transpose(ps[:, c, n * P:(n + 1) * P], tile[:, n, c * P:(c + 1) * P],
                                                     K.ident[:])
                    return mm

                def bias(to, row):
                    nc.tensor.matmul(to, K.ones3[:], K.b_parts[:, row, :], start=True, stop=False)

                def not_first(st):
                    return not (st.static and st.j == 0)

                def body(st):
                    q, b, f, m, e = st.back(1), st.back(3), st.back(4), st.back(6), st.back(7)
                    if st.valid():
                        st.wait(pe, S["xn"], HT)
                        if not_first(st):
                            pe.wait_ge(S["Tl"], st.j)
                        turn(psT, xn[st.s], st).then_inc(S["T"], 1)
                    if q.valid():
                        q.wait(pe, S["Tl"])
                        q.wait_free(pe, S["qn"])
                        for n in range(HT):
                            bias(psQ[q.s][:, n, :], 0)
                            for c in range(DC):
                                mm = split_matmul(nc, psQ[q.s][:, n, :], xnT[q.s], K.mixq,
                                                  (slice(None), c, slice(n * P, (n + 1) * P)), (slice(None), c),
                                                  start=False, stop=(c == DC - 1))
                        mm.then_inc(S["q"], 1)
                    if m.valid():
                        m.wait(pe, S["xm"], HT)
                        if not_first(m):
                            pe.wait_ge(S["Ml"], m.j)
                        turn(psM, xm[m.s], m).then_inc(S["M"], 1)
                    if b.valid():
                        b.wait(pe, S["qn"])
                        if not_first(b):
                            pe.wait_ge(S["Nh"], b.j)
                        turn(psN, qn[b.s], b).then_inc(S["N"], 1)
                        b.wait(pe, S["o"])
                        if not_first(b):
                            pe.wait_ge(S["Oh"], b.j)
                        for n in range(HT):
                            mm = nc.tensor.transpose(psO[:, n * P:(n + 1) * P], o[b.s][:, n, :], K.ident[:])
                        mm.then_inc(S["O"], 1)
                    if f.valid():
                        f.wait(pe, S["Nl"])
                        f.wait(pe, S["Ol"])
                        if not_first(f):
                            pe.wait_ge(S["x1"], f.j)
                        for n in range(HT):
                            bias(psF[:, n, :], 1)
                            for c in range(DC):
                                split_matmul(nc, psF[:, n, :], qnT[f.s], K.G,
                                             (slice(None), c, slice(n * P, (n + 1) * P)), (slice(None), c),
                                             start=False, stop=False)
                            mm = split_matmul(nc, psF[:, n, :], oT[f.s], K.m2nT,
                                              (slice(None), slice(n * P, (n + 1) * P)), slice(None),
                                              start=False, stop=True)
                        mm.then_inc(S["F"], 1)
                    if e.valid():
                        e.wait(pe, S["Ml"])
                        if not_first(e):
                            pe.wait_ge(S["y"], e.j)
                        for n in range(HT):
                            bias(psY[:, n, :], 2)
                            for c in range(DC):
                                mm = split_matmul(nc, psY[:, n, :], xmT[e.s], K.ffnT,
                                                  (slice(None), c, slice(n * P, (n + 1) * P)), (slice(None), c),
                                                  start=False, stop=(c == DC - 1))
                        mm.then_inc(S["Y"], 1)
                sweep(pe, 2 * NU, 8, 7, body, cycle=8)

            @block.scalar
            def _(act):
                def normalise(st):
                    st.wait_free(act, S["xn"], HT)
                    nc.scalar.copy(mr[st.s][:], K.stat_half(st)).then_inc(S["mr"], 1)
                    st.wait_dma(act, x_in)
                    st.wait(act, S["mr"])
                    st.wait_free(act, S["T"])
                    for n in range(HT):
                        nc.scalar.activation(xn[st.s][:, n, :], xt[st.slot(8)][:, n, :], ACT.Identity,
                                             scale=mr[st.s][:, 2 * n:2 * n + 1], bias=mr[st.s][:, 2 * n + 1:2 * n + 2]
                                             ).then_inc(S["xn"], 1)

                def body(st):
                    a, b, d, m = st.back(1), st.back(3), st.back(5), st.back(6)
                    if st.static and st.j == 0:
                        normalise(st)
                    if st.valid():
                        st.wait(act, S["T"])
                        st.wait_free(act, S["q"])
                        st.wait_free(act, S["Tl"])
                        nc.scalar.copy(xnT[st.s].high[:], psT[:]).then_inc(S["Th"], 1)
                    if a.valid():
                        a.wait(act, S["q"])
                        a.wait_free(act, S["phi"])
                        nc.scalar.activation(ex[a.s][:], psQ[a.s][:], ACT.Exp, bias=K.minus_one[:]).then_inc(S["ex"], 1)
                        a.wait(act, S["gs"], HT)
                        a.wait_free(act, S["beta"])
                        nc.scalar.activation(ge[a.s][:], gs[a.s][:], ACT.Exp, scale=-1.0).then_inc(S["ge"], 1)
                    if m.valid():
                        m.wait(act, S["M"])
                        m.wait_free(act, S["Y"])
                        m.wait_free(act, S["Ml"])
                        nc.scalar.copy(xmT[m.s].high[:], psM[:]).then_inc(S["Mh"], 1)
                    if b.valid():
                        b.wait(act, S["N"])
                        b.wait_free(act, S["F"])
                        b.wait_free(act, S["Nl"])
                        nc.scalar.copy(qnF[b.s][:], psN[:])
                        nc.scalar.copy(qnT[b.s].high[:], psN[:]).then_inc(S["Nh"], 1)
                        b.wait(act, S["O"])
                        b.wait_free(act, S["Ol"])
                        nc.scalar.copy(oF[b.s][:], psO[:])
                        nc.scalar.copy(oT[b.s].high[:], psO[:]).then_inc(S["Oh"], 1)
                    if st.ahead(1).valid():
                        normalise(st.ahead(1))
                    if d.valid():
                        d.wait(act, S["rs"])
                        d.wait(act, S["sh"])
                        d.wait_free(act, S["M"])
                        for n in range(HT):
                            nc.scalar.activation(xm[d.s][:, n, :], x1[d.slot(4)][:, n, :], ACT.Identity,
                                                 scale=rs[d.s][:, n:n + 1], bias=sh[d.s][:, n:n + 1]
                                                 ).then_inc(S["xm"], 1)
                    c = st.back(2)
                    if c.valid():
                        c.wait(act, S["beta"])
                        c.wait(act, S["dif"])
                        for n in range(HT):
                            nc.scalar.activation(dif[c.s][:, n, :], dif[c.s][:, n, :], ACT.Copy,
                                                 scale=beta[c.s][:, n:n + 1]).then_inc(S["db"], 1)
                sweep(act, 2 * NU, 8, 6, body, cycle=8)


class Kept:

    def __init__(self, nc, ctx, out):
        t = Tools(nc, ctx)
        self.out = out
        self.pool_waits, self.dve_waits, self.pe_waits, self.sp_waits = t.sems(
            "pool_waits", "dve_waits", "pe_waits", "sp_waits")

        self.project_pos_out, self.aggregate_pos_out = t.slots("pj_pos_out", 4), t.slots("ag_pos_out", 4)
        self.kv_in, self.qd_in, self.agg_in = t.slots("at_kv_in", 6), t.slots("at_qd_in", 6), t.slots("cb_agg_in", 8)

        def dram(name, shape, dt=F32):
            return nc.dram_tensor(name, shape, dt).ap()

        self.kv_tab, self.q_tab, self.skip_tab = dram("kv_tab", (N, 2 * C)), dram("q_tab", (N, C)), dram("skip_tab", (N, C))
        self.vj_tab = dram("vj_tab", (E, C))
        self.run_tab = dram("run_tab", (E + 1, C))
        self.pos_tab = dram("pos_tab", (N, 1), I32)
        self.score_tab, self.wgt_tab = dram("score_tab", (NU * H * T, P)), dram("wgt_tab", (NU * WR, U), BF16)
        self.ident = t.sb("ident", [P, P])
        self.neg_half = t.sb("neg_half", [P, T])
        self.minus_one = t.sb("minus_one", [P, 1])
        self.head_mask = t.sb("head_mask", [P, P])
        self.sel_w = t.sb("sel_w", [WR, C], BF16)
        self.sel_m = t.sb("sel_m", [WR, C], BF16)
        self.not_done = t.sb("not_done", [P, 1])
        self.last_unit = t.sb("last_unit", [P, 2])
        self.mixv, self.mixo = [t.sb(n, [P, DC, D]) for n in ("mixv", "mixo")]
        self.mixq, self.mixk = Split(t, "mixq", [P, DC, D]), Split(t, "mixk", [P, DC, D])
        self.b_kvqs = t.sb("b_kvqs", [P, 4 * C])
        self.b_k1, self.b_v = [t.sb(n, [P, D]) for n in ("b_k1", "b_v")]
        self.b_parts = t.sb("b_parts", [3, 3, D], BF16)
        self.ones3 = t.sb("ones3", [3, P], BF16)
        self.kvqsT = Split(t, "kvqsT", [P, 4 * C])
        self.n2mT = t.sb("n2mT", [P, DC, C])
        self.m2nT = Split(t, "m2nT", [P, D])
        self.ffnT = Split(t, "ffnT", [P, DC, D])
        self.edgeT = t.sb("edgeT", [R, C])
        self.gate_w = t.sb("gate_w", [P, 2, C])
        self.src_cols, self.dst_cols = [t.sb(n, [P, NU, T], I32) for n in ("src_cols", "dst_cols")]
        self.pos_cols = t.sb("pos_cols", [P, NU, 2 * T], I32)
        self.same = t.sb("same", [NU, U + 1])
        self.pen = t.sb("pen", [NU, U + 1])
        self.stat = t.sb("stat", [P, NU, T * 2])
        self.M = t.sb("M", [P, DC, D + 1])
        self.G = Split(t, "G", [P, DC, D])
        self.ksum = t.sb("ksum", [P, D])

    def stat_at(self, j):
        if isinstance(j, int):
            return self.stat[:, j, :]
        return self.stat[:, bass.ds(j, 1), :].rearrange("p a b -> p (a b)")

    def stat_half(self, st):
        half = slice(st.s * T, (st.s + 1) * T)
        if st.static:
            return self.stat[:, half_unit(st), half]
        return self.stat[:, bass.ds(half_unit(st), 1), half].rearrange("p a b -> p (a b)")

    def cols_at(self, cols, j):
        if isinstance(j, int):
            return cols[:, j, :]
        return cols[:, bass.ds(j, 1), :].rearrange("p a b -> p (a b)")


STAGES = [setup, project, attend, softmax, readout, aggregate, combine]


def build(nc, A, out):
    with ExitStack() as ctx:
        K = Kept(nc, ctx, out)
        for stage in STAGES:
            stage(nc, A, K)


def kernel(**inputs):
    import numpy as _np
    import concourse.bacc as _bacc
    from concourse import mybir as _mybir
    from concourse.bass_utils import run_bass_kernel_spmd as _run

    nc = _bacc.Bacc("TRN2", target_bir_lowering=False, num_devices=1)
    arrays, args = {}, {}
    for name, a in inputs.items():
        a = _np.ascontiguousarray(a)
        arrays[f"in_{name}_dram"] = a
        args[name] = nc.dram_tensor(f"in_{name}_dram", a.shape, _mybir.dt.from_np(a.dtype), kind="ExternalInput").ap()
    out = nc.dram_tensor("out_0_dram", (N, D), F32, kind="ExternalOutput").ap()
    build(nc, args, out)
    r = _run(nc, [arrays], core_ids=[0])
    return r.results[0]["out_0_dram"]
```
